# Optimizing a Trainium2 kernel written in Bass

```python
import numpy as np
import jax
import jax.numpy as jnp

def _softmax(x, axis=-1):
    return jax.nn.softmax(x, axis=axis)

def _gelu(x):
    return jax.nn.gelu(x, approximate=True)

def _silu(x):
    return jax.nn.silu(x)

def _sigmoid(x):
    return jax.nn.sigmoid(x)

def _layernorm(x, axis=-1, eps=1e-05):
    m = jnp.mean(x, axis=axis, keepdims=True)
    v = jnp.var(x, axis=axis, keepdims=True)
    return (x - m) / jnp.sqrt(v + eps)

def _scatter_add(tgt, idx, src, axis=0):
    return tgt.at[idx].add(src)

def _segment_sum(src, seg, n):
    return jax.ops.segment_sum(src, seg, n)
kernel_name = 'mk_flamingo_gated_d1_seqx_r4_ee75bf'

def setup_inputs(seed: int=0):
    np.random.seed(seed)
    _w = jnp.asarray

    def _rec_inputs():
        import jax
        import jax.numpy as jnp
        _rk = jax.random.key(seed)
        x = -0.0002928 + 1 * jax.random.normal(jax.random.fold_in(_rk, 1), (4, 1024, 256), jnp.float32)
        _lenS = 1024 - jax.random.randint(jax.random.fold_in(_rk, 7), (4,), 0, max(1, 1024 // 4) + 1, jnp.int32)
        _lenS2 = 154 - jax.random.randint(jax.random.fold_in(_rk, 8), (4,), 0, max(1, 154 // 4) + 1, jnp.int32)
        _ctx_1024P = jax.random.normal(jax.random.fold_in(_rk, 11), (4, 16, 256), jnp.float32)
        _ctx_1024c = jax.random.dirichlet(jax.random.fold_in(_rk, 511), 0.3 * jnp.ones((16,), jnp.float32), (4, 154))
        _ctx_1024t = jnp.einsum('bsk,bkd->bsd', _ctx_1024c, _ctx_1024P)
        _ctx_1024t = _ctx_1024t * jax.lax.rsqrt(jnp.mean(jnp.square(_ctx_1024t)) + 1e-12) * 0.953939
        ctx_1024 = -1.39393e-06 + 0.999914 * (_ctx_1024t + 0.3 * jax.random.normal(jax.random.fold_in(_rk, 611), (4, 154, 256), jnp.float32))
        _g = jax.random.normal(jax.random.fold_in(_rk, 9001), (2, 1), jnp.float32)
        _g = jnp.sign(_g) * jnp.maximum(jnp.abs(_g), 1.0) + (_g == 0) * 1.0
        g_xattn = _g[0]
        g_ffn = _g[1]
        return (x, ctx_1024, g_xattn, g_ffn)
    x, ctx_1024, g_xattn, g_ffn = _rec_inputs()

    def _L0_xattn_setup():
        import jax, jax.numpy as jnp
        import numpy as np
        EMBED = 256
        HEADS = 16
        HEAD_DIM = EMBED // HEADS
        key = jax.random.key(seed)
        ks = jax.random.split(key, 10)
        B, SQ, SK = (2, 512, 512)
        s = 0.02
        return {'decoder_hidden_state': jax.random.normal(ks[0], (B, SQ, EMBED), jnp.float32), 'encoder_hidden_state': jax.random.normal(ks[1], (B, SK, EMBED), jnp.float32), 'wq': jax.random.normal(ks[2], (HEADS, EMBED, HEAD_DIM), jnp.float32) * s, 'bq': jax.random.normal(ks[3], (HEADS, HEAD_DIM), jnp.float32) * s, 'wk': jax.random.normal(ks[4], (HEADS, EMBED, HEAD_DIM), jnp.float32) * s, 'bk': jax.random.normal(ks[5], (HEADS, HEAD_DIM), jnp.float32) * s, 'wv': jax.random.normal(ks[6], (HEADS, EMBED, HEAD_DIM), jnp.float32) * s, 'bv': jax.random.normal(ks[7], (HEADS, HEAD_DIM), jnp.float32) * s, 'wo': jax.random.normal(ks[8], (EMBED, EMBED), jnp.float32) * s, 'bo': jax.random.normal(ks[9], (EMBED,), jnp.float32) * s}
    _L0_xattn_all = _L0_xattn_setup()
    _L0_xattn_in = {k: v for k, v in _L0_xattn_all.items() if k in ('wq', 'bq', 'wk', 'bk', 'wv', 'bv', 'wo', 'bo')}
    del _L0_xattn_all

    def _L0_ffn_setup():
        import jax, jax.numpy as jnp
        import numpy as np
        B, S, D = (4, 1024, 256)
        H = 1024
        RH = 256
        E = 16
        K = 2
        NS = 1

        def _swiglu(x, w1, w2, w3):
            return jax.nn.silu(x @ w1) * (x @ w2) @ w3
        key = jax.random.key(seed)
        ks = jax.random.split(key, 9)
        s = 0.02
        return {'x': jax.random.normal(ks[0], (B, S, D), dtype=jnp.float32), 'router_w': jax.random.normal(ks[1], (D, E), dtype=jnp.float32) * s, 'expert_bias': jnp.zeros((E,), dtype=jnp.float32), 'shared_w1': jax.random.normal(ks[2], (NS, D, H), dtype=jnp.float32) * s, 'shared_w2': jax.random.normal(ks[3], (NS, D, H), dtype=jnp.float32) * s, 'shared_w3': jax.random.normal(ks[4], (NS, H, D), dtype=jnp.float32) * s, 'routed_w1': jax.random.normal(ks[5], (E, D, RH), dtype=jnp.float32) * s, 'routed_w2': jax.random.normal(ks[6], (E, D, RH), dtype=jnp.float32) * s, 'routed_w3': jax.random.normal(ks[7], (E, RH, D), dtype=jnp.float32) * s}
    _L0_ffn_all = _L0_ffn_setup()
    _L0_ffn_in = {k: v for k, v in _L0_ffn_all.items() if k in ('router_w', 'expert_bias', 'shared_w1', 'shared_w2', 'shared_w3', 'routed_w1', 'routed_w2', 'routed_w3')}
    del _L0_ffn_all
    return {'x': x, 'ctx_1024': ctx_1024, 'g_xattn': g_xattn, 'g_ffn': g_ffn, 'L0_xattn_wq': _L0_xattn_in['wq'], 'L0_xattn_bq': _L0_xattn_in['bq'], 'L0_xattn_wk': _L0_xattn_in['wk'], 'L0_xattn_bk': _L0_xattn_in['bk'], 'L0_xattn_wv': _L0_xattn_in['wv'], 'L0_xattn_bv': _L0_xattn_in['bv'], 'L0_xattn_wo': _L0_xattn_in['wo'], 'L0_xattn_bo': _L0_xattn_in['bo'], 'L0_ffn_router_w': _L0_ffn_in['router_w'], 'L0_ffn_expert_bias': _L0_ffn_in['expert_bias'], 'L0_ffn_shared_w1': _L0_ffn_in['shared_w1'], 'L0_ffn_shared_w2': _L0_ffn_in['shared_w2'], 'L0_ffn_shared_w3': _L0_ffn_in['shared_w3'], 'L0_ffn_routed_w1': _L0_ffn_in['routed_w1'], 'L0_ffn_routed_w2': _L0_ffn_in['routed_w2'], 'L0_ffn_routed_w3': _L0_ffn_in['routed_w3']}

def reference(x, ctx_1024, g_xattn, g_ffn, L0_xattn_wq, L0_xattn_bq, L0_xattn_wk, L0_xattn_bk, L0_xattn_wv, L0_xattn_bv, L0_xattn_wo, L0_xattn_bo, L0_ffn_router_w, L0_ffn_expert_bias, L0_ffn_shared_w1, L0_ffn_shared_w2, L0_ffn_shared_w3, L0_ffn_routed_w1, L0_ffn_routed_w2, L0_ffn_routed_w3):
    import jax
    import jax.numpy as jnp

    def _L0_xattn_ref(decoder_hidden_state, encoder_hidden_state, wq, bq, wk, bk, wv, bv, wo, bo):
        import jax, jax.numpy as jnp
        import numpy as np
        EMBED = 256
        HEADS = 16
        HEAD_DIM = EMBED // HEADS
        q = jnp.einsum('bqe,hed->bhqd', decoder_hidden_state, wq) + bq[None, :, None, :]
        k = jnp.einsum('bke,hed->bhkd', encoder_hidden_state, wk) + bk[None, :, None, :]
        v = jnp.einsum('bke,hed->bhkd', encoder_hidden_state, wv) + bv[None, :, None, :]
        scale = 1.0 / jnp.sqrt(jnp.asarray(HEAD_DIM, q.dtype))
        scores = jnp.einsum('bhqd,bhkd->bhqk', q, k) * scale
        attn = jax.nn.softmax(scores, axis=-1)
        ctx = jnp.einsum('bhqk,bhkd->bhqd', attn, v)
        B, H, SQ, D = ctx.shape
        ctx = jnp.transpose(ctx, (0, 2, 1, 3)).reshape(B, SQ, H * D)
        return ctx @ wo + bo

    def _L0_ffn_ref(x, router_w, expert_bias, shared_w1, shared_w2, shared_w3, routed_w1, routed_w2, routed_w3):
        import jax, jax.numpy as jnp
        import numpy as np
        B, S, D = (4, 1024, 256)
        H = 1024
        RH = 256
        E = 16
        K = 2
        NS = 1

        def _swiglu(x, w1, w2, w3):
            return jax.nn.silu(x @ w1) * (x @ w2) @ w3
        shared_out = jnp.sum(jax.vmap(lambda w1, w2, w3: _swiglu(x, w1, w2, w3))(shared_w1, shared_w2, shared_w3), axis=0)
        scores = jax.nn.sigmoid(x @ router_w)
        sel_scores = scores + expert_bias
        _, top_idx = jax.lax.top_k(sel_scores, K)
        top_scores = jnp.take_along_axis(scores, top_idx, axis=-1)
        gates = jnp.sum(jax.nn.one_hot(top_idx, E, dtype=scores.dtype) * top_scores[..., None], axis=-2)
        xf = x.reshape(-1, D)
        gf = gates.reshape(-1, E).T

        def body(acc, ws):
            w1, w2, w3, g = ws
            return (acc + _swiglu(xf, w1, w2, w3) * g[:, None], None)
        routed_out, _ = jax.lax.scan(body, jnp.zeros_like(xf), (routed_w1, routed_w2, routed_w3, gf))
        return shared_out + routed_out.reshape(x.shape)
    x = x + jnp.tanh(g_xattn[0]) * _L0_xattn_ref(_layernorm(x, axis=-1), ctx_1024, L0_xattn_wq, L0_xattn_bq, L0_xattn_wk, L0_xattn_bk, L0_xattn_wv, L0_xattn_bv, L0_xattn_wo, L0_xattn_bo)
    x = x + jnp.tanh(g_ffn[0]) * _L0_ffn_ref(_layernorm(x, axis=-1), L0_ffn_router_w, L0_ffn_expert_bias, L0_ffn_shared_w1, L0_ffn_shared_w2, L0_ffn_shared_w3, L0_ffn_routed_w1, L0_ffn_routed_w2, L0_ffn_routed_w3)
    return x

_drawn_inputs = setup_inputs


def setup_inputs(seed=0):
    import zlib

    import numpy as np

    out = dict(_drawn_inputs(seed))
    spreads = {'L0_ffn_expert_bias': (0.0, 0.547)}
    factors = {'L0_xattn_wq': 8.0,
     'L0_xattn_bq': 8.0,
     'L0_xattn_wk': 8.0,
     'L0_xattn_bk': 64.0,
     'L0_xattn_bv': 8.0,
     'L0_xattn_bo': 3.587,
     'L0_ffn_router_w': 5.965,
     'L0_ffn_routed_w1': 4.492,
     'L0_ffn_routed_w2': 4.45,
     'L0_ffn_routed_w3': 4.443,
     'L0_ffn_shared_w1': 3.625,
     'L0_ffn_shared_w2': 3.588,
     'L0_ffn_shared_w3': 3.593}
    for name, (base, spread) in spreads.items():
        noise = np.random.default_rng([zlib.crc32(name.encode()), seed]).standard_normal(out[name].shape)
        drawn = base * np.exp(spread * noise) if base else spread * noise
        out[name] = jnp.asarray(drawn.astype(out[name].dtype))
    for name, factor in factors.items():
        out[name] = (out[name] * factor).astype(out[name].dtype)
    return out
```

```python
from contextlib import ExitStack

import concourse.bass as bass
from concourse import mybir

F32 = mybir.dt.float32
F32R = mybir.dt.float32r
I32 = mybir.dt.int32
U32 = mybir.dt.uint32
ALU = mybir.AluOpType
ACT = mybir.ActivationFunctionType
AX = mybir.AxisListType.X

P = 128
QUAD = 32
CHUNK_TILES = 4
CH = CHUNK_TILES * P
EPS = 1e-5


def step_events(front, back):
    order = []
    if back:
        order += [("ST", u) for u in range(10)] + [("PV", 0)]
        order += [("ST", u) for u in range(10, 15)] + [("OT", 0), ("PV", 1)]
        order += [("ST", u) for u in range(15, 20)] + [("OT", 1), ("PV", 2), ("OT", 2), ("PV", 3), ("OT", 3)]
    elif front:
        order = [("SA", u) for u in range(32)]
    events, sa = [], 0
    for kind, u in order:
        events.append((kind, u))
        if front and kind == "ST" and u >= 4:
            events += [("SA", sa), ("SA", sa + 1)]
            sa += 2
    units = [e for e in events if e[0] in ("ST", "SA")]
    return events, {e: n % 4 for n, e in enumerate(units)}


def bank_holders(q, front, back):
    def count(step, e):
        return (20 * step if e[0] == "ST" else 32 * (step + 1)) + e[1] + 1

    units = [e for e in step_events(front, back)[0] if e[0] in ("ST", "SA")]
    if not back:
        before = [("K", 7), ("K", 8), ("V", 7), ("V", 8)]
    else:
        first = isinstance(q, int) and q == 0
        last4 = [e for e in step_events(True, not first)[0] if e[0] in ("ST", "SA")][-4:]
        before = [(e[0], count(q - 1, e)) for e in last4]
    held = before + [(e[0], count(q, e)) for e in units]
    return {e: held[n] for n, e in enumerate(units)}


def flamingo_block(nc, x, ctx_in, g_xattn, g_ffn, wq, bq, wk, bk, wv, bv, wo, bo,
                   router_w, expert_bias, sw1, sw2, sw3, rw1, rw2, rw3, out):
    B, SQ, D = x.shape
    SK = ctx_in.shape[1]
    H, _, HD = wq.shape
    KC = D // P
    PAIRS = H // 2
    HALF_PAIRS = PAIRS // 2
    KP = 160
    REM = SK - P
    T = B * SQ
    NT, NCH = T // P, T // CH
    GROUPS = H // 4
    ROWS = 3 * QUAD
    SCALE = float(HD) ** -0.5
    E, _, RH = rw1.shape
    SH = sw1.shape[2]
    HT = SH // P
    assert SQ == 2 * CH and D == 2 * P and P < SK <= P + QUAD and HD == 16 and H == 16

    x_t = x.rearrange("b (n p) d -> p (b n) d", p=P)
    out_t = out.rearrange("b (n p) d -> p (b n) d", p=P)

    keep = ExitStack()

    def sbuf(name, shape, dt=F32, stack=keep):
        return stack.enter_context(nc.sbuf_tensor(name, shape, dt))

    def sem(name):
        return keep.enter_context(nc.semaphore(name))

    TOPK = 2
    TILES = (TOPK * T - E) // P + E
    TILES += TILES % 2
    slots_x = nc.dram_tensor("slots_x", [TILES * P, D], F32, kind="Internal").ap()

    def after(eng, semaphore, value):
        if not isinstance(value, int) or value > 0:
            eng.wait_ge(semaphore, value)

    def chunk_tiles(q):
        return bass.ds(q * CHUNK_TILES, CHUNK_TILES)

    dve_holds, pool_holds = sem("dve_holds"), sem("pool_holds")

    x_sb = sbuf("x_sb", [P, NT, D])
    xn2_rows = nc.dram_tensor("xn2_rows", [P, NT, D], F32, kind="Internal").ap()
    xn2T_cols = nc.dram_tensor("xn2T_cols", [P, KC, T], F32, kind="Internal").ap()
    logits = sbuf("logits", [P, NT, E])
    ident = sbuf("ident", [P, P])
    gates = sbuf("gates", [P, 2])
    tg = sbuf("tg", [P, 2])

    with ExitStack() as st:
        def sb(name, shape, dt=F32):
            return sbuf(name, shape, dt, st)

        def ps(name):
            return st.enter_context(nc.psum_tensor(name, [P, CH], F32))

        wq_sb, wk_sb, wv_sb = (sb(n, [P, KC, H, HD]) for n in ("wq_sb", "wk_sb", "wv_sb"))
        wo_sb = sb("wo_sb", [P, KC, D])
        rw_sb = sb("rw_sb", [P, KC, E])
        bq_sb, bk_sb = sb("bq_sb", [P, 2]), sb("bk_sb", [P, 2])
        bv_sb, bo_sb = sb("bv_sb", [P, D]), sb("bo_sb", [P, D])
        ctx_sb = sb("ctx_sb", [P, 2, D])
        ctxT = sb("ctxT", [P, KC, B, SK])
        kf = sb("kf", [P, 2, B, KP])
        kh, kl = sb("kh", [P, 2, B, KP], F32R), sb("kl", [P, 2, B, KP], F32R)
        v_all = sb("v_all", [P, 2, B, D])
        k_max = sb("k_max", [ROWS, PAIRS, 2, KP], F32R)
        k_st = sb("k_st", [ROWS + 2, PAIRS, 3, P], F32R)
        ones_rows = sb("ones_rows", [2, 2, 3, P])
        v_main = sb("v_main", [P, H, QUAD])
        v_rem = sb("v_rem", [P, GROUPS, P])
        stats, mv = sb("stats", [P, 4, 6]), sb("mv", [P, 4, 2])
        ve, rstd = sb("ve", [P, 4]), sb("rstd", [P, 4])
        minus_half = sb("minus_half", [P, 4])
        stats2, mv2 = sb("stats2", [P, 4, 6]), sb("mv2", [P, 4, 2])
        ve2, rstd2 = sb("ve2", [P, 4]), sb("rstd2", [P, 4])
        xn = sb("xn", [P, 4, D])
        xnT = sb("xnT", [P, KC, CH])
        qf = sb("qf", [P, 2, CH])
        qh, ql = sb("qh", [P, 2, CH], F32R), sb("ql", [P, 2, CH], F32R)
        q_st = [sb(f"q_st{i}", [ROWS + 2, PAIRS, CH], F32R) for i in range(2)]
        mx = sb("mx", [P, 4, 2, PAIRS])
        mT = sb("mT", [H, CH], F32R)
        probs = sb("probs", [P, 2, 5, CH])
        oT = sb("oT", [P, CH])
        rden = sb("rden", [P, 4, 4])
        ctxn = sb("ctxn", [P, 4, D])
        ctxnT = sb("ctxnT", [P, KC, CH])
        att = sb("att", [P, 4, D])
        xn2c = sb("xn2c", [P, 4, D])
        xn2T = sb("xn2T", [P, KC, CH])

        zeros = sb("zeros", [P, D])

        T0, T1, M, PV = ps("T0"), ps("T1"), ps("M"), ps("PV")
        S = [ps(f"S{i}") for i in range(4)]

        consts_done = sem("consts_done")
        weights_loaded = sem("weights_loaded")
        ones_loaded = sem("ones_loaded")
        slots_cleared = sem("slots_cleared")
        gates_loaded, tg_ready = sem("gates_loaded"), sem("tg_ready")
        ctx_loaded = sem("ctx_loaded")
        ctxT_done, ctxT_ready = sem("ctxT_done"), sem("ctxT_ready")
        kT_done, kf_ready = sem("kT_done"), sem("kf_ready")
        kh_ready, kl_ready = sem("kh_ready"), sem("kl_ready")
        kmax_loaded, kst_loaded = sem("kmax_loaded"), sem("kst_loaded")
        v_done, v_kept, v_loaded = sem("v_done"), sem("v_kept"), sem("v_loaded")
        x_loaded, x_rest_loaded = sem("x_loaded"), sem("x_rest_loaded")
        ln_step, rstd_ready, xn_ready = sem("ln_step"), sem("rstd_ready"), sem("xn_ready")
        xn_transposed, xnT_ready = sem("xn_transposed"), sem("xnT_ready")
        q_done, qf_ready = sem("q_done"), sem("qf_ready")
        qh_ready, ql_ready = sem("qh_ready"), sem("ql_ready")
        q_loaded = [sem(f"q_loaded{i}") for i in range(2)]
        m_loaded = [sem(f"m_loaded{i}") for i in range(2)]
        sa_done, sa_read, st_done = sem("sa_done"), sem("sa_read"), sem("st_done")
        mT_done, mT_ready = sem("mT_done"), sem("mT_ready")
        probs_ready, pv_done = sem("probs_ready"), sem("pv_done")
        oT_ready, o_done = sem("oT_ready"), sem("o_done")
        rden_ready, ctxn_ready = sem("rden_ready"), sem("ctxn_ready")
        ctxn_transposed, ctxnT_ready = sem("ctxn_transposed"), sem("ctxnT_ready")
        wo_done, att_ready, x1_ready = sem("wo_done"), sem("att_ready"), sem("x1_ready")
        ln2_step, rstd2_ready, xn2_ready = sem("ln2_step"), sem("rstd2_ready"), sem("xn2_ready")
        xn2_stored, xn2T_stored = sem("xn2_stored"), sem("xn2T_stored")
        xn2_transposed, xn2T_ready = sem("xn2_transposed"), sem("xn2T_ready")
        lg_done = sem("lg_done")
        logits_ready = sem("logits_ready")
        kf_padded = sem("kf_padded")

        N_KDMA = 16 * 3 * 2 * HALF_PAIRS
        N_QDMA = 16 * 3 * HALF_PAIRS
        N_VDMA = 16 * 5
        N_WEIGHTS = 16 * (3 * KC + 2 + 2 + 2)

        CONSTS = 18

        def run_steps(eng, step):
            step(eng, -1, -1, 1, True, False, False)
            step(eng, 0, 0, 0, True, True, False)
            with eng.Fori(0, B - 1) as b:
                step(eng, b * 2 + 1, b, 1, True, True, True)
                step(eng, b * 2 + 2, b + 1, 0, True, True, True)
            step(eng, NCH - 1, B - 1, 1, False, True, True)
            step(eng, NCH, B, 0, False, False, True)

        def raw(ap):
            return ap.bitcast(F32)

        with nc.Block() as block:
            @block.sync
            def _(sp):
                sp.dma_start(x_sb[:, 0:2 * CHUNK_TILES, :], x_t[:, 0:2 * CHUNK_TILES, :]).then_inc(x_loaded, 16)

                def load_ctx(b):
                    if b:
                        sp.wait_ge(ctxT_done, b)
                        sp.wait_ge(ctx_loaded, 32 * b)
                    sp.dma_start(ctx_sb[:, 0, :], ctx_in[b, 0:P, :]).then_inc(ctx_loaded, 16)
                    sp.dma_start(ctx_sb[0:REM, 1, :], ctx_in[b, P:SK, :]).then_inc(ctx_loaded, 16)

                load_ctx(0)
                for w_sb, w in ((wk_sb, wk), (wv_sb, wv), (wq_sb, wq)):
                    for kc in range(KC):
                        sp.dma_start(w_sb[:, kc], w[:, kc * P:(kc + 1) * P, :].rearrange("h p d -> p h d")
                                     ).then_inc(weights_loaded, 16)
                for b_sb, b_in in ((bq_sb, bq), (bk_sb, bk)):
                    sp.dma_start(b_sb[:], b_in.rearrange("(c h) d -> (h d) c", c=2), allow_slow_non_contiguous=True).then_inc(weights_loaded, 16)
                sp.dma_start(bv_sb[:], bv.rearrange("h d -> (h d)").partition_broadcast(P)).then_inc(weights_loaded, 16)
                sp.dma_start(bo_sb[:], bo.partition_broadcast(P)).then_inc(weights_loaded, 16)
                sp.dma_start(wo_sb[:], wo.rearrange("(c p) n -> p c n", p=P)).then_inc(weights_loaded, 16)
                sp.dma_start(rw_sb[:], router_w.rearrange("(c p) n -> p c n", p=P)).then_inc(weights_loaded, 16)
                sp.dma_start(gates[:, 0:1], g_xattn.partition_broadcast(P)).then_inc(gates_loaded, 16)
                sp.dma_start(gates[:, 1:2], g_ffn.partition_broadcast(P)).then_inc(gates_loaded, 16)
                for b in range(1, B):
                    load_ctx(b)
                for b in range(1, B):
                    sp.dma_start(x_sb[:, 2 * b * CHUNK_TILES:2 * (b + 1) * CHUNK_TILES, :],
                                 x_t[:, 2 * b * CHUNK_TILES:2 * (b + 1) * CHUNK_TILES, :]).then_inc(x_rest_loaded, 16)
                sp.wait_ge(consts_done, CONSTS)
                for p in range(PAIRS):
                        sp.dma_start(raw(k_st[ROWS:ROWS + 2, p, :, :]), ones_rows[:, p % 2, :, :]).then_inc(ones_loaded, 16)

                sp.dma_start(slots_x.rearrange("(t p) d -> p t d", p=P), zeros[:].rearrange(
                    "p (o d) -> p o d", o=1).to_broadcast([P, TILES, D])).then_inc(slots_cleared, 16)

                def place_keys(dst, loaded, keys, slot, b):
                    for part, src in enumerate((kh, kl, kh)):
                        for j in range(HALF_PAIRS):
                            for i in range(2):
                                rows = slice(QUAD * j + HD * i, QUAD * j + HD * (i + 1))
                                at, cols = slot(i, j)
                                sp.dma_start(
                                    raw(dst[QUAD * part + HD * i:QUAD * part + HD * (i + 1), j::HALF_PAIRS, at, cols]),
                                    raw(src[rows, :, bass.ds(b, 1), keys]).rearrange("p c o k -> p c (o k)")
                                ).then_inc(loaded, 16)

                def step(sp, q, b, k, front, back, prev):
                    n, bn = q + 1, b + 1 if k else b
                    if front and k:
                        if back:
                            sp.wait_ge(sa_done, 32 * n)
                        else:
                            sp.wait_ge(kh_ready, 1)
                            sp.wait_ge(kl_ready, 1)
                        place_keys(k_max, kmax_loaded, slice(0, KP), lambda i, j: (i, slice(0, KP)), bn)
                    if front:
                        after(sp, st_done, 20 * q)
                        sp.wait_ge(qh_ready, 2 * n + 2)
                        sp.wait_ge(ql_ready, 2 * n + 2)
                        for part, src in enumerate((qh, qh, ql)):
                            for j in range(HALF_PAIRS):
                                sp.dma_start(raw(q_st[1 - k][QUAD * part:QUAD * (part + 1), j::HALF_PAIRS, :]),
                                             raw(src[QUAD * j:QUAD * (j + 1), :, :])).then_inc(q_loaded[1 - k], 16)
                    if front and k:
                        if back:
                            sp.wait_ge(st_done, 20 * n)
                        place_keys(k_st, kst_loaded, slice(0, P), lambda i, j: (i, slice(0, P)), bn)
                        place_keys(k_st, kst_loaded, slice(P, KP), lambda i, j: (
                            2, slice(QUAD * (2 * (j % 2) + i), QUAD * (2 * (j % 2) + i + 1))), bn)
                        if back:
                            sp.wait_ge(pv_done, 4 * n)
                        else:
                            sp.wait_ge(v_kept, 2 * B)
                        sp.dma_start(v_main[:, :, 0:HD], v_all[:, 0, bass.ds(bn, 1), :].rearrange(
                            "p o (h d) -> p (o h) d", d=HD)).then_inc(v_loaded, 16)
                        for j in range(4):
                            sp.dma_start(v_rem[QUAD * j:QUAD * j + REM, :, QUAD * j:QUAD * j + HD],
                                         v_all[0:REM, 1, bass.ds(bn, 1), :].rearrange(
                                             "p o (g j d) -> p (o g) j d", j=4, d=HD)[:, :, j, :]
                                         ).then_inc(v_loaded, 16)
                    if prev:
                        sp.wait_ge(xn2_ready, q)
                        sp.dma_start(xn2_rows[:, chunk_tiles(q - 1), :], xn2c[:]).then_inc(xn2_stored, 16)
                    if front:
                        sp.wait_ge(mT_ready, n + 1)
                        for i in range(2):
                            sp.dma_start(raw(q_st[1 - k][ROWS + i:ROWS + i + 1, :, :]),
                                         raw(mT[PAIRS * i:PAIRS * (i + 1), :])).then_inc(m_loaded[1 - k], 16)

                    if prev:
                        sp.wait_ge(xn2T_ready, 2 * q)
                        sp.dma_start(xn2T_cols[:, :, bass.ds((q - 1) * CH, CH)], xn2T[:]).then_inc(xn2T_stored, 16)

                run_steps(sp, step)
                sp.wait_ge(xn2_stored, 16 * NCH)
                sp.wait_ge(xn2T_stored, 16 * NCH)
                sp.wait_ge(slots_cleared, 16)

            @block.gpsimd
            def _(pool):
                g = nc.gpsimd
                count = [0]

                def const(ins):
                    ins.then_inc(consts_done, 1)
                    count[0] += 1
                    pool.wait_ge(consts_done, count[0])

                def select(ap, pattern, base, mult):
                    const(g.affine_select(out=ap, in_=ap, compare_op=ALU.not_equal, fill=1.0, base=base,
                                          pattern=pattern, channel_multiplier=mult))

                const(g.memset(zeros[:], 0.0))
                const(g.memset(ident[:], 0.0))
                const(g.memset(ones_rows[:], 0.0))
                const(g.memset(minus_half[:], -0.5))
                const(g.memset(v_main[:], 0.0))
                const(g.memset(v_rem[:], 0.0))
                const(g.memset(k_max[:].bitcast(F32), 0.0))
                const(g.memset(k_st[:].bitcast(F32), 0.0))
                select(ident[:], [[-1, P]], 0, 1)
                for parity in range(2):
                    select(ones_rows[:, parity, 0:2, :], [[-1, 2], [0, P]], 0, 1)
                    select(ones_rows[:, parity, 2, 2 * QUAD * parity:2 * QUAD * (parity + 1)].rearrange(
                        "r (i c) -> r i c", i=2), [[-1, 2], [0, QUAD]], 0, 1)
                const(g.memset(v_main[:, :, HD:HD + 1], 1.0))
                for j in range(4):
                    const(g.memset(v_rem[QUAD * j:QUAD * j + REM, :, QUAD * j + HD:QUAD * j + HD + 1], 1.0))
                assert count[0] == CONSTS
                pool.wait_ge(kf_ready, 2 * B)
                g.tensor_copy(kf[:, :, :, SK:KP], kf[:, :, :, SK - 1:SK].to_broadcast([P, 2, B, KP - SK])
                              ).then_inc(kf_padded, 1)
                pool.wait_ge(kf_padded, 1)
                g.tensor_copy(kh[:], kf[:]).then_inc(kh_ready, 1)
                pool.wait_ge(kh_ready, 1)
                g.tensor_tensor(kl[:], kf[:], kh[:].bitcast(F32), ALU.subtract).then_inc(kl_ready, 1)

                def step(pool, q, b, k, front, back, prev):
                    n, bn = q + 1, b + 1 if k else b
                    if front:
                        pool.wait_ge(ln_step, 3 * n + 3)
                        if back:
                            pool.wait_ge(xn_ready, n)
                        g.tensor_tensor(rstd[:], ve[:], minus_half[:], ALU.pow).then_inc(rstd_ready, 1)
                    if prev:
                        pool.wait_ge(ln2_step, 3 * q)
                        g.tensor_tensor(rstd2[:], ve2[:], minus_half[:], ALU.pow).then_inc(rstd2_ready, 1)
                    if front:
                        if back:
                            pool.wait_ge(q_loaded[k], N_QDMA * (b + 1))
                        for c in range(2):
                            pool.wait_ge(qf_ready, 2 * n + c + 1)
                            pool.sem_inc(pool_holds, 1)
                            g.tensor_copy(qh[:, c, :], qf[:, c, :]).then_inc(qh_ready, 1)
                            pool.wait_ge(qh_ready, 2 * n + c + 1)
                            g.tensor_tensor(ql[:, c, :], qf[:, c, :], qh[:, c, :].bitcast(F32),
                                            ALU.subtract).then_inc(ql_ready, 1)

                run_steps(pool, step)

            @block.scalar
            def _(act):
                s = nc.scalar
                act.wait_ge(gates_loaded, 32)
                s.activation(tg[:], gates[:], ACT.Tanh).then_inc(tg_ready, 1)
                act.wait_ge(weights_loaded, N_WEIGHTS)
                for b in range(B):
                    act.wait_ge(ctxT_done, b + 1)
                    s.copy(ctxT[:, :, b, :], T0[:, 0:2 * SK].rearrange("p (c k) -> p c k", c=2)
                           ).then_inc(ctxT_ready, 1)
                for b in range(B):
                    for c in range(2):
                        act.wait_ge(kT_done, 2 * b + c + 1)
                        s.activation(kf[:, c, b, 0:SK], S[c][:, 0:SK], ACT.Identity, bias=bk_sb[:, c:c + 1]
                                     ).then_inc(kf_ready, 1)

                def step(act, q, b, k, front, back, prev):
                    n, bn = q + 1, b + 1 if k else b
                    if front:
                        for c, T_c in enumerate((T0, T1)):
                            act.wait_ge(xn_transposed, 2 * n + c + 1)
                            after(act, q_done, 2 * n)
                            s.copy(xnT[:, c, :], T_c[:]).then_inc(xnT_ready, 1)
                        for c in range(2):
                            act.wait_ge(q_done, 2 * n + c + 1)
                            if back:
                                act.wait_ge(ql_ready, 2 * n)
                            s.activation(qf[:, c, :], M[:], ACT.Identity, bias=bq_sb[:, c:c + 1]
                                         ).then_inc(qf_ready, 1)
                    events, banks = step_events(front, back)
                    for kind, u in events:
                        if kind == "ST":
                            g, i = u // 5, u % 5
                            act.wait_ge(st_done, 20 * q + u + 1)
                            after(act, pv_done, 4 * q + g - 1)
                            s.activation(probs[:, g % 2, i, :], S[banks[kind, u]][:], ACT.Exp,
                                         scale=SCALE).then_inc(probs_ready, 1)
                        if kind == "PV" and u > 0:
                            copy_out(act, q, u - 1)
                            if u == 3:
                                copy_out(act, q, 3)
                    if prev:
                        for c, T_c in enumerate((T0, T1)):
                            act.wait_ge(xn2_transposed, 2 * q - 1 + c)
                            after(act, lg_done, q - 1)
                            after(act, xn2T_stored, 16 * (q - 1))
                            s.copy(xn2T[:, c, :], T_c[:]).then_inc(xn2T_ready, 1)
                    if back:
                        for c, T_c in enumerate((T0, T1)):
                            act.wait_ge(ctxn_transposed, 2 * q + c + 1)
                            after(act, wo_done, 2 * q)
                            s.copy(ctxnT[:, c, :], T_c[:]).then_inc(ctxnT_ready, 1)

                def copy_out(act, q, g):
                    act.wait_ge(pv_done, 4 * q + g + 1)
                    after(act, o_done, 4 * q + g)
                    s.copy(oT[:], PV[:]).then_inc(oT_ready, 1)

                run_steps(act, step)

            @block.vector
            def _(dve):
                v = nc.vector
                for b in range(B):
                    for r, rows in ((0, P), (1, REM)):
                        dve.wait_ge(v_done, 2 * b + r + 1)
                        if b == 0 and r == 0:
                            dve.wait_ge(weights_loaded, N_WEIGHTS)
                        v.tensor_tensor(v_all[0:rows, r, b, :], S[2 + r][0:rows, 0:D], bv_sb[0:rows, :], ALU.add
                                        ).then_inc(v_kept, 1)

                def statistics(q, st_, mv_, ve_, step_sem, ve_read):
                    for t in range(CHUNK_TILES):
                        last = v.bn_stats(st_[:, t, :], x_sb[:, bass.ds(q * CHUNK_TILES + t, 1), :].rearrange(
                            "p o d -> p (o d)"))
                    last.then_inc(step_sem, 1)
                    dve.wait_ge(step_sem, 3 * q + 1)
                    dve.sem_inc(dve_holds, 1)
                    for t in range(CHUNK_TILES):
                        last = v.bn_aggr(mv_[:, t, :], st_[:, t, :])
                    last.then_inc(step_sem, 1)
                    dve.wait_ge(step_sem, 3 * q + 2)
                    after(dve, ve_read, q)
                    v.tensor_scalar(ve_[:], mv_[:, :, 1], EPS, None, ALU.add).then_inc(step_sem, 1)

                def normalise(q, mv_, rstd_, out_, done):
                    for t in range(CHUNK_TILES):
                        last = v.tensor_scalar(out_[:, t, :], x_sb[:, bass.ds(q * CHUNK_TILES + t, 1), :].rearrange(
                            "p o d -> p (o d)"), mv_[:, t, 0:1], rstd_[:, t:t + 1], ALU.subtract, ALU.mult)
                    last.then_inc(done, 1)

                def step(dve, q, b, k, front, back, prev):
                    n = q + 1
                    if front:
                        if isinstance(n, int) and n < 2:
                            dve.wait_ge(x_loaded, 16)
                        else:
                            dve.wait_ge(x_rest_loaded, 16 * (B - 1))
                        statistics(n, stats, mv, ve, ln_step, rstd_ready)
                    if prev:
                        if isinstance(q, int) and q == 1 or not isinstance(q, int):
                            dve.wait_ge(tg_ready, 1)
                        for c, bank in enumerate((M, PV)):
                            dve.wait_ge(wo_done, 2 * q - 1 + c)
                            v.tensor_tensor(att[:, 2 * c:2 * c + 2, :], bank[:].rearrange("p (t d) -> p t d", t=2),
                                            bo_sb[:].rearrange("p (o d) -> p o d", o=1).to_broadcast([P, 2, D]),
                                            ALU.add).then_inc(att_ready, 1)
                        dve.wait_ge(att_ready, 2 * q)
                        v.scalar_tensor_tensor(x_sb[:, chunk_tiles(q - 1), :], att[:], tg[:, 0:1],
                                               x_sb[:, chunk_tiles(q - 1), :], ALU.mult, ALU.add
                                               ).then_inc(x1_ready, 1)
                    if front:
                        dve.wait_ge(rstd_ready, n + 1)
                        after(dve, xn_transposed, 2 * n)
                        normalise(n, mv, rstd, xn, xn_ready)
                    if prev:
                        dve.wait_ge(x1_ready, q)
                        dve.sem_inc(dve_holds, 1)
                        statistics(q - 1, stats2, mv2, ve2, ln2_step, rstd2_ready)
                        dve.wait_ge(rstd2_ready, q)
                        after(dve, xn2_transposed, 2 * (q - 1))
                        after(dve, xn2_stored, 16 * (q - 1))
                        normalise(q - 1, mv2, rstd2, xn2c, xn2_ready)
                    events, banks = step_events(front, back)
                    for kind, u in events:
                        if kind == "SA":
                            t, p = u // PAIRS, u % PAIRS
                            dve.wait_ge(sa_done, 32 * n + u + 1)
                            if u == 0:
                                after(dve, mT_done, n)
                            v.reduce_max(mx[:, t, :, p], S[banks[kind, u]][:, 0:2 * KP].rearrange(
                                "p (i k) -> p i k", i=2), AX).then_inc(sa_read, 1)
                        if kind == "OT":
                            turned = T1[:].rearrange("p (t j r) -> p t j r", t=4, j=4)
                            dve.wait_ge(o_done, 4 * q + u + 1)
                            v.reciprocal(rden[:], turned[:, :, :, HD]).then_inc(rden_ready, 1)
                            dve.wait_ge(rden_ready, 4 * q + u + 1)
                            if u == 0:
                                after(dve, ctxn_transposed, 2 * q)
                            v.tensor_tensor(
                                ctxn[:, :, 4 * HD * u:4 * HD * (u + 1)].rearrange("p t (j d) -> p t j d", j=4),
                                turned[:, :, :, 0:HD],
                                rden[:].rearrange("p t (j o) -> p t j o", o=1).to_broadcast([P, 4, 4, HD]),
                                ALU.mult).then_inc(ctxn_ready, 1)
                    if front:
                        dve.wait_ge(mT_done, n + 1)
                        if back:
                            dve.wait_ge(m_loaded[k], 32 * (b + 1))
                        v.tensor_scalar(mT[:], T0[0:H, :], -1.0, None, ALU.mult).then_inc(mT_ready, 1)
                    if prev:
                        dve.wait_ge(lg_done, q)
                        v.tensor_copy(logits[:, chunk_tiles(q - 1), :],
                                      M[:, 0:4 * E].rearrange("p (t e) -> p t e", t=4)).then_inc(logits_ready, 1)

                run_steps(dve, step)

            @block.tensor
            def _(pe):
                mm, turn = nc.tensor.matmul, nc.tensor.transpose
                pe.wait_ge(consts_done, CONSTS)
                for b in range(B):
                    pe.wait_ge(ctx_loaded, 32 * (b + 1))
                    after(pe, ctxT_ready, b)
                    for c in range(KC):
                        turn(T0[:, c * SK:c * SK + P], ctx_sb[:, 0, c * P:(c + 1) * P], ident[:])
                        last = turn(T0[:, c * SK + P:(c + 1) * SK], ctx_sb[0:REM, 1, c * P:(c + 1) * P],
                                    ident[0:REM, 0:REM])
                    last.then_inc(ctxT_done, 1)
                pe.wait_ge(weights_loaded, N_WEIGHTS)
                for b in range(B):
                    pe.wait_ge(ctxT_ready, b + 1)
                    for c in range(2):
                        after(pe, kf_ready, 2 * b + c - 1)
                        for kc in range(KC):
                            last = mm(S[c][:, 0:SK], wk_sb[:, kc, 8 * c:8 * c + 8, :].rearrange("p h d -> p (h d)"),
                                      ctxT[:, kc, b, :], start=kc == 0, stop=kc == KC - 1)
                        last.then_inc(kT_done, 1)
                    for r, keys in ((0, slice(0, P)), (1, slice(P, SK))):
                        after(pe, v_kept, 2 * b + r - 1)
                        for kc in range(KC):
                            last = mm(S[2 + r][0:keys.stop - keys.start, 0:D], ctxT[:, kc, b, keys],
                                      wv_sb[:, kc].rearrange("p h d -> p (h d)"), start=kc == 0, stop=kc == KC - 1)
                        last.then_inc(v_done, 1)

                def step(pe, q, b, k, front, back, prev):
                    n, bn = q + 1, b + 1 if k else b
                    if front:
                        pe.wait_ge(xn_ready, n + 1)
                        for c, T_c in enumerate((T0, T1)):
                            if prev:
                                pe.wait_ge(ctxnT_ready, 2 * q - 1 + c)
                            elif back:
                                pe.wait_ge(mT_ready, 1)
                                pe.wait_ge(xnT_ready, 2)
                            else:
                                pe.wait_ge(ctxT_ready, B)
                            for t in range(CHUNK_TILES):
                                last = turn(T_c[:, t * P:(t + 1) * P], xn[:, t, c * P:(c + 1) * P], ident[:])
                            last.then_inc(xn_transposed, 1)
                        pe.wait_ge(xnT_ready, 2 * n + 2)
                        for c in range(2):
                            if c == 0 and prev:
                                pe.wait_ge(att_ready, 2 * q - 1)
                            if c == 1:
                                pe.wait_ge(qf_ready, 2 * n + 1)
                            for kc in range(KC):
                                last = mm(M[:], wq_sb[:, kc, 8 * c:8 * c + 8, :].rearrange("p h d -> p (h d)"),
                                          xnT[:, kc, :], start=kc == 0, stop=kc == KC - 1)
                            last.then_inc(q_done, 1)
                    events, banks = step_events(front, back)
                    held = bank_holders(q, front, back)
                    for kind, u in events:
                        if kind in ("ST", "SA"):
                            was, value = held[kind, u]
                            pe.wait_ge({"ST": probs_ready, "SA": sa_read, "K": kf_ready, "V": v_kept}[was], value)
                            bank = S[banks[kind, u]]
                        if kind == "SA":
                            t, p = u // PAIRS, u % PAIRS
                            if u == 0:
                                pe.wait_ge(q_loaded[1 - k], N_QDMA * (bn + 1))
                                pe.wait_ge(kmax_loaded, N_KDMA * (bn + 1))
                            mm(bank[:, 0:2 * KP], q_st[1 - k][0:ROWS, p, t * P:(t + 1) * P],
                               k_max[:, p, :, :].rearrange("r i k -> r (i k)"), start=True, stop=True
                               ).then_inc(sa_done, 1)
                        if kind == "ST":
                            g, i = u // 5, u % 5
                            if u == 0:
                                pe.wait_ge(m_loaded[k], 32 * (b + 1))
                                pe.wait_ge(kst_loaded, 2 * N_KDMA * (b + 1))
                                pe.wait_ge(ones_loaded, 16 * PAIRS)
                            if i < 4:
                                p = 2 * g + i // 2
                                last = mm(bank[:], k_st[:, p, i % 2, :], q_st[k][:, p, :],
                                          start=True, stop=True)
                            else:
                                for p in (2 * g, 2 * g + 1):
                                    last = mm(bank[:], k_st[:, p, 2, :], q_st[k][:, p, :],
                                              start=p == 2 * g, stop=p == 2 * g + 1)
                            last.then_inc(st_done, 1)
                        if kind == "PV":
                            pe.wait_ge(probs_ready, 20 * q + 5 * u + 5)
                            if u == 0:
                                pe.wait_ge(v_loaded, N_VDMA * (b + 1))
                                after(pe, att_ready, 2 * q)
                            else:
                                pe.wait_ge(oT_ready, 4 * q + u)
                            for j in range(4):
                                mm(PV[QUAD * j:QUAD * (j + 1), :], v_main[:, 4 * u + j, :], probs[:, u % 2, j, :],
                                   start=True, stop=False)
                            mm(PV[:], v_rem[:, u, :], probs[:, u % 2, 4, :], start=False, stop=True
                               ).then_inc(pv_done, 1)
                        if kind == "OT":
                            pe.wait_ge(oT_ready, 4 * q + u + 1)
                            if u > 0:
                                pe.wait_ge(ctxn_ready, 4 * q + u)
                            elif front:
                                pe.wait_ge(xnT_ready, 2 * n + 2)
                            else:
                                pe.wait_ge(ctxnT_ready, 2 * q)
                            for t in range(CHUNK_TILES):
                                last = turn(T1[:, t * P:(t + 1) * P], oT[:, t * P:(t + 1) * P], ident[:])
                            last.then_inc(o_done, 1)
                    if front:
                        pe.wait_ge(sa_read, 32 * (n + 1))
                        pe.wait_ge(xnT_ready, 2 * n + 1)
                        for t in range(CHUNK_TILES):
                            last = turn(T0[0:H, t * P:(t + 1) * P], mx[:, t].rearrange("p i c -> p (i c)"), ident[:])
                        last.then_inc(mT_done, 1)
                    if prev:
                        pe.wait_ge(xn2_ready, q)
                        for c, T_c in enumerate((T0, T1)):
                            if c == 0 and front:
                                pe.wait_ge(mT_ready, n + 1)
                            elif c == 1 and back:
                                pe.wait_ge(ctxn_ready, 4 * q + 4)
                            else:
                                pe.wait_ge(ctxnT_ready, 2 * q - 1 + c)
                            for t in range(CHUNK_TILES):
                                last = turn(T_c[:, t * P:(t + 1) * P], xn2c[:, t, c * P:(c + 1) * P], ident[:])
                            last.then_inc(xn2_transposed, 1)
                        pe.wait_ge(xn2T_ready, 2 * q)
                        if front:
                            pe.wait_ge(qf_ready, 2 * n + 2)
                        else:
                            pe.wait_ge(att_ready, 2 * q - 1)
                        for t in range(CHUNK_TILES):
                            for kc in range(KC):
                                last = mm(M[:, t * E:(t + 1) * E], xn2T[:, kc, t * P:(t + 1) * P], rw_sb[:, kc, :],
                                          start=kc == 0, stop=kc == KC - 1)
                        last.then_inc(lg_done, 1)
                    if back:
                        pe.wait_ge(ctxn_ready, 4 * q + 4)
                        for c, T_c in enumerate((T0, T1)):
                            if prev:
                                pe.wait_ge(xn2T_ready, 2 * q - 1 + c)
                            elif c == 0:
                                pe.wait_ge(mT_ready, n + 1)
                            for t in range(CHUNK_TILES):
                                last = turn(T_c[:, t * P:(t + 1) * P], ctxn[:, t, c * P:(c + 1) * P], ident[:])
                            last.then_inc(ctxn_transposed, 1)
                        pe.wait_ge(ctxnT_ready, 2 * q + 2)
                        for c, bank in enumerate((M, PV)):
                            if c == 0 and prev:
                                pe.wait_ge(logits_ready, q)
                            elif c == 0:
                                pe.wait_ge(qf_ready, 2 * n + 2)
                            if c == 1:
                                pe.wait_ge(oT_ready, 4 * q + 4)
                            for t in (2 * c, 2 * c + 1):
                                for kc in range(KC):
                                    last = mm(bank[:, (t % 2) * D:(t % 2 + 1) * D], ctxnT[:, kc, t * P:(t + 1) * P],
                                              wo_sb[:, kc, :], start=kc == 0, stop=kc == KC - 1)
                            last.then_inc(wo_done, 1)

                run_steps(pe, step)

    with ExitStack() as st:
        def sb(name, shape, dt=F32):
            return sbuf(name, shape, dt, st)

        def ps(name):
            return st.enter_context(nc.psum_tensor(name, [P, CH], F32))

        MAX_TILES = T // P
        NR = RH // P

        x_rows = slots_x
        y_rows = nc.dram_tensor("y_rows", [TILES * P, D], F32, kind="Internal").ap()

        w12 = sb("w12", [P, E, KC, 2 * RH])
        w3 = sb("w3", [P, E, NR, D])
        s12 = sb("s12", [P, KC, 2, SH])
        s3 = sb("s3", [P, HT, D])
        xT = [sb(f"xT{i}", [P, KC, CH]) for i in range(2)]
        silu_s = [sb(f"silu_s{i}", [P, CH]) for i in range(2)]
        act_s = [sb(f"act_s{i}", [P, CH]) for i in range(2)]

        bias_sb = sb("bias_sb", [P, E])
        iota_e = sb("iota_e", [P, E])
        iota_p = sb("iota_p", [P, MAX_TILES])
        iota_t = sb("iota_t", [1, TILES])
        before = sb("before", [P, P])
        ones = sb("ones", [P, P])
        score = sb("score", [P, NT, E])
        N = NT * E
        scratch = sb("scratch", [P, max(TILES * E + 4 * N, 12 * D)])
        tile_cmp = scratch[0:1, 0:TILES * E].rearrange("p (t e) -> p t e", e=E)
        sel = scratch[:, 0:N].rearrange("p (t e) -> p t e", e=E)
        at = TILES * E
        total, upto = (scratch[:, at + i * N:at + (i + 1) * N].rearrange("p (e t) -> p e t", e=E) for i in range(2))
        zero_row = scratch[:, at + 2 * N:at + 3 * N]
        tmp = scratch[:, at + 3 * N:at + 4 * N].rearrange("p (t e) -> p t e", e=E)
        xs, sil, hid, ys = ([scratch[:, (2 * n + i) * D:(2 * n + i + 1) * D] for i in range(2)] for n in range(4))
        xsT, hidT = ([scratch[:, (2 * n + i) * D:(2 * n + i + 1) * D].rearrange("p (c k) -> p c k", c=2)
                      for i in range(2)] for n in (4, 5))
        best, best_at = sb("best", [P, NT, 8]), sb("best_at", [P, NT, 8], U32)
        best_f = sb("best_f", [P, NT, TOPK])
        hot = [sb(f"hot{i}", [P, NT, E]) for i in range(TOPK)]
        hots = sb("hots", [P, NT, E])
        gate = sb("gate", [P, NT, TOPK])
        count_e, pad_e, end_e = sb("count_e", [P, E]), sb("pad_e", [P, E]), sb("end_e", [P, E])
        shift_e = sb("shift_e", [P, E])
        slot_f = sb("slot_f", [P, NT, TOPK])
        slot = sb("slot", [P, NT, TOPK], I32)
        tile_f, tile_e = sb("tile_f", [1, TILES]), sb("tile_e", [1, TILES], I32)

        idx = [sb(f"idx{i}", [P, CHUNK_TILES, TOPK], I32) for i in range(2)]
        rows = [sb(f"rows{i}", [P, CHUNK_TILES, D]) for i in range(2)]

        bank = [ps(f"bank{i}") for i in range(8)]

        w_loaded = sem("w_loaded")
        we_loaded = sem("we_loaded")
        bias_loaded = sem("bias_loaded")
        iotas_done = sem("iotas_done")
        xT_loaded = [sem(f"xT_loaded{i}") for i in range(2)]
        tanh_ready = sem("tanh_ready")
        route = sem("route")
        ranks_done = sem("ranks_done")
        slots_ready = sem("slots_ready")
        tiles_ready = sem("tiles_ready")
        h_done, silu_ready, act_ready = sem("h_done"), sem("silu_ready"), sem("act_ready")
        act_used, y_added = sem("act_used"), sem("y_added")
        rows_loaded = [sem(f"rows_loaded{i}") for i in range(2)]
        idx_ready = sem("idx_ready")
        rows_placed = [sem(f"rows_placed{i}") for i in range(2)]
        xs_loaded = [sem(f"xs_loaded{i}") for i in range(2)]
        xs_turned, xsT_ready = sem("xs_turned"), sem("xsT_ready")
        up_done, sil_ready, hid_ready = sem("up_done"), sem("sil_ready"), sem("hid_ready")
        hid_turned, hidT_ready = sem("hid_turned"), sem("hidT_ready")
        down_done, ys_ready = sem("down_done"), sem("ys_ready")
        ys_stored = [sem(f"ys_stored{i}") for i in range(2)]
        got = [sem(f"got{i}") for i in range(2)]
        idx2_ready = sem("idx2_ready")
        got_used = sem("got_used")
        out_stored = sem("out_stored")

        IOTAS = 6
        N_SCATTER = 16 * CHUNK_TILES * TOPK
        gathered = [w3[:, i * CHUNK_TILES * TOPK // NR:(i + 1) * CHUNK_TILES * TOPK // NR].rearrange(
            "p e r d -> p (e r) d").rearrange("p (t k) d -> p t k d", k=TOPK) for i in range(2)]

        with nc.Block() as block:
            @block.sync
            def _(sp):
                sp.dma_start(bias_sb[:], expert_bias.partition_broadcast(P)).then_inc(bias_loaded, 16)
                for i in range(2):
                    sp.dma_start(xT[i][:], xn2T_cols[:, :, i * CH:(i + 1) * CH]).then_inc(xT_loaded[i], 16)
                sp.dma_start(s12[:, :, 0, :], sw1[0].rearrange("(c p) n -> p c n", p=P)).then_inc(w_loaded, 16)
                sp.dma_start(s12[:, :, 1, :], sw2[0].rearrange("(c p) n -> p c n", p=P)).then_inc(w_loaded, 16)
                sp.dma_start(s3[:], sw3[0].rearrange("(c p) n -> p c n", p=P)).then_inc(w_loaded, 16)
                for i in range(2):
                    sp.dma_start(rows[i][:], xn2_rows[:, i * CHUNK_TILES:(i + 1) * CHUNK_TILES, :]
                                 ).then_inc(rows_loaded[i], 16)
                for kc in range(KC):
                    sp.dma_start(w12[:, :, kc, 0:RH], rw1[:, kc * P:(kc + 1) * P, :].rearrange("e p n -> p e n")
                                 ).then_inc(we_loaded, 16)
                    sp.dma_start(w12[:, :, kc, RH:2 * RH], rw2[:, kc * P:(kc + 1) * P, :].rearrange("e p n -> p e n")
                                 ).then_inc(we_loaded, 16)
                    sp.dma_start(w3[:, :, kc, :], rw3[:, kc * P:(kc + 1) * P, :].rearrange("e p n -> p e n")
                                 ).then_inc(we_loaded, 16)
                with sp.Fori(1, NCH // 2) as j:
                    for i in range(2):
                        sp.wait_ge(h_done, HT * (j * 2 + i - 1))
                        sp.dma_start(xT[i][:], xn2T_cols[:, :, bass.ds((j * 2 + i) * CH, CH)]
                                     ).then_inc(xT_loaded[i], 16)
                    for i in range(2):
                        sp.wait_ge(rows_placed[i], j * N_SCATTER)
                        sp.dma_start(rows[i][:], xn2_rows[:, bass.ds((j * 2 + i) * CHUNK_TILES, CHUNK_TILES), :]
                                     ).then_inc(rows_loaded[i], 16)
                for i in range(2):
                    sp.wait_ge(rows_placed[i], NCH // 2 * N_SCATTER)
                def load_tile(t, i):
                    after(sp, xs_turned, t - 1)
                    sp.dma_start(xs[i][:], x_rows[bass.ds(t * P, P), :]).then_inc(xs_loaded[i], 16)

                def store_tile(t, i):
                    sp.wait_ge(ys_ready, t + 1)
                    sp.dma_start(y_rows[bass.ds(t * P, P), :], ys[i][:]).then_inc(ys_stored[i], 16)

                for t in range(4):
                    load_tile(t, t % 2)
                with sp.Fori(0, TILES // 2 - 2) as j:
                    for i in range(2):
                        load_tile(j * 2 + 4 + i, i)
                        store_tile(j * 2 + i, i)
                for t in range(TILES - 4, TILES):
                    store_tile(t, t % 2)
                with sp.Fori(0, NCH) as c:
                    sp.wait_ge(got_used, c + 1)
                    sp.dma_start(out_t[:, chunk_tiles(c), :], x_sb[:, chunk_tiles(c), :]).then_inc(out_stored, 16)
                sp.wait_ge(out_stored, 16 * NCH)
                for i in range(2):
                    sp.wait_ge(ys_stored[i], 16 * (TILES // 2))

            @block.gpsimd
            def _(pool):
                g = nc.gpsimd
                count = [0]

                def const(ins):
                    ins.then_inc(iotas_done, 1)
                    count[0] += 1
                    pool.wait_ge(iotas_done, count[0])

                fl = dict(allow_small_or_imprecise_dtypes=True)
                const(g.iota(iota_e[:], pattern=[[1, E]], base=0, channel_multiplier=0, **fl))
                const(g.iota(iota_p[:], pattern=[[P, MAX_TILES]], base=0, channel_multiplier=0, **fl))
                const(g.iota(iota_t[:], pattern=[[1, TILES]], base=0, channel_multiplier=0, **fl))
                const(g.memset(ones[:], 1.0))
                const(g.memset(zero_row[:], 0.0))
                const(g.affine_select(out=before[:], in_=ones[:], compare_op=ALU.is_gt, fill=0.0, base=0,
                                      pattern=[[1, P]], channel_multiplier=-1))
                assert count[0] == IOTAS
                pool.wait_ge(slots_ready, 1)

                def copy_idx(i, c, done):
                    g.tensor_copy(idx[i][:], slot[:, chunk_tiles(c), :]).then_inc(done, 1)
                    pool.wait_ge(done, c + 1)

                with pool.Fori(0, NCH // 2) as j:
                    for i in range(2):
                        c = j * 2 + i
                        pool.wait_ge(rows_placed[i], j * N_SCATTER)
                        copy_idx(i, c, idx_ready)
                        pool.wait_ge(rows_loaded[i], j * 16 + 16)
                        pool.sem_inc(pool_holds, 1)
                        for t in range(CHUNK_TILES):
                            for k in range(TOPK):
                                pool.indirect_dma_start(
                                    out=x_rows, out_offset=bass.IndirectOffsetOnAxis(ap=idx[i][:, t, k:k + 1], axis=0),
                                    in_=rows[i][:, t, :], in_offset=None).then_inc(rows_placed[i], 16)
                for i in range(2):
                    pool.wait_ge(rows_placed[i], NCH // 2 * N_SCATTER)
                    pool.wait_ge(ys_stored[i], 16 * (TILES // 2))
                with pool.Fori(0, NCH // 2) as j:
                    for i in range(2):
                        c = j * 2 + i
                        pool.wait_ge(got[i], j * N_SCATTER)
                        copy_idx(i, c, idx2_ready)
                        pool.wait_ge(got_used, c - i)
                        pool.sem_inc(pool_holds, 1)
                        for t in range(CHUNK_TILES):
                            for k in range(TOPK):
                                pool.indirect_dma_start(
                                    out=gathered[i][:, t, k, :], out_offset=None, in_=y_rows,
                                    in_offset=bass.IndirectOffsetOnAxis(ap=idx[i][:, t, k:k + 1], axis=0)
                                ).then_inc(got[i], 16)

            @block.scalar
            def _(act):
                s = nc.scalar
                s.activation(score[:], logits[:], ACT.Tanh, scale=0.5).then_inc(tanh_ready, 1)
                with act.Fori(0, NCH) as c:
                    for m in range(HT):
                        act.wait_ge(h_done, c * HT + m + 1)
                        after(act, act_ready, c * HT + m - 1) if m else act.wait_ge(act_ready, c * HT)
                        s.activation(silu_s[m % 2][:], bank[m % 2][:], ACT.Silu).then_inc(silu_ready, 1)

                def turn_in(t, i):
                    act.wait_ge(xs_turned, t + 1)
                    after(act, up_done, t - 1)
                    s.copy(xsT[i][:], bank[i][:, 0:D].rearrange("p (c k) -> p c k", c=KC)).then_inc(xsT_ready, 1)

                def silu(t, i):
                    act.wait_ge(up_done, t + 1)
                    after(act, hid_ready, t - 1)
                    s.activation(sil[i][:], bank[2 + i][:, 0:RH], ACT.Silu).then_inc(sil_ready, 1)

                turn_in(0, 0)
                turn_in(1, 1)
                silu(0, 0)
                with act.Fori(0, TILES // 2 - 1) as j:
                    for i in range(2):
                        turn_in(j * 2 + 2 + i, i)
                        silu(j * 2 + 1 + i, 1 - i)
                silu(TILES - 1, 1)

            @block.vector
            def _(dve):
                v = nc.vector
                done = [0]

                def then(ins):
                    done[0] += 1
                    ins.then_inc(route, 1)
                    dve.wait_ge(route, done[0])

                def over_e(ap):
                    return ap.rearrange("p (o e) -> p o e", o=1).to_broadcast([P, NT, E])

                def over_last(ap, n):
                    return ap.rearrange("p t (k o) -> p t k o", o=1)[:, :, 0, :].to_broadcast([P, NT, n])

                dve.wait_ge(tanh_ready, 1)
                dve.wait_ge(bias_loaded, 16)
                dve.wait_ge(iotas_done, IOTAS)
                then(v.tensor_scalar(score[:], score[:], 0.5, 0.5, ALU.mult, ALU.add))
                then(v.tensor_tensor(sel[:], score[:], over_e(bias_sb[:]), ALU.add))
                for t in range(NT):
                    last = v.max(best[:, t, :], sel[:, t, :])
                then(last)
                for t in range(NT):
                    last = v.max_index(best_at[:, t, :], best[:, t, :], sel[:, t, :])
                then(last)
                then(v.tensor_copy(best_f[:], best_at[:, :, 0:TOPK]))
                for k in range(TOPK):
                    then(v.tensor_tensor(hot[k][:], over_e(iota_e[:]), over_last(best_f[:, :, k:k + 1], E), ALU.is_equal))
                    then(v.tensor_tensor(tmp[:], hot[k][:], score[:], ALU.mult))
                    then(v.reduce_sum(gate[:, :, k], tmp[:], AX))
                then(v.tensor_scalar(gate[:], gate[:], tg[:, 1:2], None, ALU.mult))
                then(v.tensor_tensor(hots[:], hot[0][:], hot[1][:], ALU.add))
                HOTS = done[0]
                assert HOTS == 13
                dve.wait_ge(ranks_done, 1)
                then(v.tensor_copy(total[:], bank[5][:].rearrange("p (t e) -> p e t", e=E)))
                then(v.tensor_tensor_scan(upto[:].rearrange("p e t -> p (e t)"), total[:].rearrange("p e t -> p (e t)"),
                                          zero_row, 0.0, ALU.add, ALU.add))
                then(v.tensor_copy(end_e[:], upto[:, :, NT - 1]))
                then(v.tensor_copy(count_e[:, 0:1], end_e[:, 0:1]))
                then(v.tensor_tensor(count_e[:, 1:E], end_e[:, 1:E], end_e[:, 0:E - 1], ALU.subtract))
                cmp = tmp[:].rearrange("p t e -> p (t e)").rearrange("p (e n) -> p e n", e=E)
                then(v.tensor_tensor(cmp, count_e[:].rearrange("p (e o) -> p e o", o=1).to_broadcast([P, E, MAX_TILES]),
                                     iota_p[:].rearrange("p (o n) -> p o n", o=1).to_broadcast([P, E, MAX_TILES]),
                                     ALU.is_gt))
                then(v.reduce_sum(pad_e[:], cmp, AX))
                then(v.tensor_tensor(shift_e[:], count_e[:], end_e[:], ALU.subtract))
                then(v.tensor_tensor_scan(end_e[:], pad_e[:], zero_row[:, 0:E], 0.0, ALU.add, ALU.add))
                then(v.tensor_tensor(tile_cmp[:], end_e[0:1, :].rearrange("p (o e) -> p o e", o=1).to_broadcast(
                    [1, TILES, E]), iota_t[:].rearrange("p (t o) -> p t o", o=1).to_broadcast([1, TILES, E]), ALU.is_le))
                then(v.reduce_sum(tile_f[:], tile_cmp[:], AX))
                v.tensor_scalar(tile_e[:], tile_f[:], float(E - 1), None, ALU.min).then_inc(tiles_ready, 1)
                then(v.tensor_tensor(pad_e[:], end_e[:], pad_e[:], ALU.subtract))
                then(v.scalar_tensor_tensor(shift_e[:], pad_e[:], float(P), shift_e[:], ALU.mult, ALU.add))
                then(v.tensor_tensor(upto[:], upto[:], total[:], ALU.subtract))
                then(v.tensor_tensor(tmp[:], bank[4][:].rearrange("p (t e) -> p t e", e=E),
                                     upto[:].rearrange("p e t -> p t e"), ALU.add))
                then(v.tensor_tensor(tmp[:], tmp[:], over_e(shift_e[:]), ALU.add))
                for k in range(TOPK):
                    then(v.tensor_tensor(hots[:], hot[k][:], tmp[:], ALU.mult))
                    then(v.reduce_sum(slot_f[:, :, k], hots[:], AX))
                v.tensor_copy(slot[:], slot_f[:]).then_inc(slots_ready, 1)
                with dve.Fori(0, NCH) as c:
                    for m in range(HT):
                        dve.wait_ge(silu_ready, c * HT + m + 1)
                        if m >= 2:
                            dve.wait_ge(act_used, c * HT + m - 1)
                        v.tensor_tensor(act_s[m % 2][:], silu_s[m % 2][:], bank[2 + m % 2][:], ALU.mult
                                        ).then_inc(act_ready, 1)
                    for t in range(CHUNK_TILES):
                        if t == 0:
                            dve.wait_ge(act_used, c * HT + HT)
                        row = x_sb[:, bass.ds(c * CHUNK_TILES + t, 1), :].rearrange("p o d -> p (o d)")
                        last = v.scalar_tensor_tensor(row, bank[4 + t][:, 0:D], tg[:, 1:2], row, ALU.mult, ALU.add)
                    last.then_inc(y_added, 1)

                def hidden(t, i):
                    dve.wait_ge(sil_ready, t + 1)
                    after(dve, hid_turned, t - 1)
                    v.tensor_tensor(hid[i][:], sil[i][:], bank[2 + i][:, RH:2 * RH], ALU.mult).then_inc(hid_ready, 1)

                def turn_hidden(t, i):
                    dve.wait_ge(hid_turned, t + 1)
                    after(dve, down_done, t - 1)
                    v.tensor_copy(hidT[i][:], bank[4 + i][:, 0:RH].rearrange("p (c k) -> p c k", c=NR)
                                  ).then_inc(hidT_ready, 1)

                def outputs(t, i):
                    dve.wait_ge(down_done, t + 1)
                    if isinstance(t, int) and t < 2:
                        pass
                    else:
                        dve.wait_ge(ys_stored[i], (t - i) * 8)
                    v.tensor_copy(ys[i][:], bank[6 + i][:, 0:D]).then_inc(ys_ready, 1)

                hidden(0, 0)
                hidden(1, 1)
                turn_hidden(0, 0)
                outputs_from = 0
                hidden(2, 0)
                turn_hidden(1, 1)
                outputs(0, 0)
                hidden(3, 1)
                turn_hidden(2, 0)
                outputs(1, 1)
                with dve.Fori(1, TILES // 2 - 1) as j:
                    for i in range(2):
                        hidden(j * 2 + 2 + i, i)
                        turn_hidden(j * 2 + 1 + i, 1 - i)
                        outputs(j * 2 + i, i)
                turn_hidden(TILES - 1, 1)
                outputs(TILES - 2, 0)
                outputs(TILES - 1, 1)

                with dve.Fori(0, NCH // 2) as j:
                    for i in range(2):
                        dve.wait_ge(got[i], j * N_SCATTER + N_SCATTER)
                        c = j * 2 + i
                        for k in range(TOPK):
                            for t in range(CHUNK_TILES):
                                row = x_sb[:, bass.ds(c * CHUNK_TILES + t, 1), :].rearrange("p o d -> p (o d)")
                                last = v.scalar_tensor_tensor(
                                    row, gathered[i][:, t, k, :],
                                    gate[:, bass.ds(c * CHUNK_TILES + t, 1), k], row, ALU.mult, ALU.add)
                            if k == 0:
                                last.then_inc(y_added, 1)
                                dve.wait_ge(y_added, NCH + c + 1)
                        last.then_inc(got_used, 1)

            @block.tensor
            def _(pe):
                mm, turn = nc.tensor.matmul, nc.tensor.transpose
                pe.wait_ge(route, 13)
                pe.wait_ge(iotas_done, IOTAS)
                mm(bank[4][:], before[:], hots[:].rearrange("p t e -> p (t e)"), start=True, stop=True)
                mm(bank[5][:], ones[:], hots[:].rearrange("p t e -> p (t e)"), start=True, stop=True
                   ).then_inc(ranks_done, 1)

                pe.wait_ge(w_loaded, 48)
                pe.wait_ge(slots_ready, 1)
                with pe.Fori(0, NCH // 2) as j:
                    for i in range(2):
                        c = j * 2 + i
                        pe.wait_ge(xT_loaded[i], j * 16 + 16)

                        def down(m):
                            pe.wait_ge(act_ready, c * HT + m + 1)
                            if m == 0:
                                pe.wait_ge(y_added, c)
                            for t in range(CHUNK_TILES):
                                last = mm(bank[4 + t][:, 0:D], act_s[m % 2][:, t * P:(t + 1) * P], s3[:, m, :],
                                          start=m == 0, stop=m == HT - 1)
                            last.then_inc(act_used, 1)

                        for m in range(HT):
                            if m >= 2:
                                pe.wait_ge(act_ready, c * HT + m - 1)
                            for u in range(2):
                                for kc in range(KC):
                                    last = mm(bank[2 * u + m % 2][:], s12[:, kc, u, m * P:(m + 1) * P], xT[i][:, kc, :],
                                              start=kc == 0, stop=kc == KC - 1)
                            last.then_inc(h_done, 1)
                            if m > 0:
                                down(m - 1)
                        down(HT - 1)

                pe.wait_ge(we_loaded, 16 * 3 * KC)
                pe.wait_ge(tiles_ready, 1)

                def expert(t):
                    return pe.value_load(tile_e[0:1, bass.ds(t, 1)], min_val=0, max_val=E - 1)

                def turn_in(t, i):
                    pe.wait_ge(xs_loaded[i], (t - i) * 8 + 16)
                    after(pe, xsT_ready, t - 1)
                    for kc in range(KC):
                        last = turn(bank[i][:, kc * P:(kc + 1) * P], xs[i][:, kc * P:(kc + 1) * P], ident[:])
                    last.then_inc(xs_turned, 1)

                def up(t, i, e):
                    pe.wait_ge(xsT_ready, t + 1)
                    after(pe, hid_ready, t - 1)
                    for kc in range(KC):
                        last = mm(bank[2 + i][:], xsT[i][:, kc, :],
                                  w12[:, bass.ds(e, 1), kc, :].rearrange("p o n -> p (o n)"),
                                  start=kc == 0, stop=kc == KC - 1)
                    last.then_inc(up_done, 1)

                def turn_hidden(t, i):
                    pe.wait_ge(hid_ready, t + 1)
                    after(pe, hidT_ready, t - 1)
                    for r in range(NR):
                        last = turn(bank[4 + i][:, r * P:(r + 1) * P], hid[i][:, r * P:(r + 1) * P], ident[:])
                    last.then_inc(hid_turned, 1)

                def down(t, i, e):
                    pe.wait_ge(hidT_ready, t + 1)
                    after(pe, ys_ready, t - 1)
                    for r in range(NR):
                        last = mm(bank[6 + i][:, 0:D], hidT[i][:, r, :],
                                  w3[:, bass.ds(e, 1), r, :].rearrange("p o n -> p (o n)"),
                                  start=r == 0, stop=r == NR - 1)
                    last.then_inc(down_done, 1)

                pe.wait_ge(y_added, NCH)
                turn_in(0, 0)
                turn_in(1, 1)
                up(0, 0, expert(0))
                turn_in(2, 0)
                up(1, 1, expert(1))
                turn_hidden(0, 0)

                def tile_step(t, i):
                    turn_in(t + 3, 1 - i)
                    up(t + 2, i, expert(t + 2))
                    turn_hidden(t + 1, 1 - i)
                    down(t, i, expert(t))

                tile_step(0, 0)
                tile_step(1, 1)
                with pe.Fori(1, TILES // 2 - 2) as j:
                    for i in range(2):
                        tile_step(j * 2 + i, i)
                turn_in(TILES - 1, 1)
                up(TILES - 2, 0, expert(TILES - 2))
                turn_hidden(TILES - 3, 1)
                down(TILES - 4, 0, expert(TILES - 4))
                up(TILES - 1, 1, expert(TILES - 1))
                turn_hidden(TILES - 2, 0)
                down(TILES - 3, 1, expert(TILES - 3))
                turn_hidden(TILES - 1, 1)
                down(TILES - 2, 0, expert(TILES - 2))
                down(TILES - 1, 1, expert(TILES - 1))

    keep.close()


_INS = ["x", "ctx_1024", "g_xattn", "g_ffn", "L0_xattn_wq", "L0_xattn_bq", "L0_xattn_wk", "L0_xattn_bk",
        "L0_xattn_wv", "L0_xattn_bv", "L0_xattn_wo", "L0_xattn_bo", "L0_ffn_router_w", "L0_ffn_expert_bias",
        "L0_ffn_shared_w1", "L0_ffn_shared_w2", "L0_ffn_shared_w3", "L0_ffn_routed_w1", "L0_ffn_routed_w2",
        "L0_ffn_routed_w3"]


def kernel(**inputs):
    import numpy as _np
    import concourse.bacc as _bacc
    from concourse import mybir as _mybir
    from concourse.bass_utils import run_bass_kernel_spmd as _run

    nc = _bacc.Bacc("TRN2", target_bir_lowering=False, num_devices=1)
    arrays, args = {}, []
    for name in _INS:
        a = _np.ascontiguousarray(inputs[name])
        arrays[f"in_{name}_dram"] = a
        args.append(nc.dram_tensor(f"in_{name}_dram", a.shape, _mybir.dt.from_np(a.dtype), kind="ExternalInput").ap())
    shape = inputs["x"].shape
    args.append(nc.dram_tensor("out_dram", shape, _mybir.dt.float32, kind="ExternalOutput").ap())
    flamingo_block(nc, *args)
    return _run(nc, [arrays], core_ids=[0]).results[0]["out_dram"]
```

```python
from contextlib import ExitStack

import concourse.bass as bass
from concourse import mybir

F32 = mybir.dt.float32
F32R = mybir.dt.float32r
I32 = mybir.dt.int32
U32 = mybir.dt.uint32
ALU = mybir.AluOpType
ACT = mybir.ActivationFunctionType
AX = mybir.AxisListType.X

P = 128
QUAD = 32
CHUNK_TILES = 4
CH = CHUNK_TILES * P
EPS = 1e-5


def step_events(early, front, back, prev):
    order = []
    for n in range(20):
        if back:
            order.append(("ST", n))
        if n == 0 and prev:
            order += [("C0", 0), ("C1", 0)]
        if n == 3 and prev:
            order += [("W0", 0), ("W1", 0), ("X1", 0)]
        if n == 4 and early:
            order.append(("L1", 0))
        if n == 6 and prev:
            order.append(("L2", 0))
        if front and n >= 4:
            order += [("SA", 2 * n - 8), ("SA", 2 * n - 7)]
        if back:
            order += {9: [("PV", 0)], 14: [("OT", 0), ("PV", 1)], 19: [("OT", 1), ("PV", 2)]}.get(n, [])
        if n == 10 and prev:
            order.append(("X0", 0))
        if n == 12 and prev:
            order.append(("XX", 0))
        if n == 13 and early:
            order.append(("N0", 0))
        if n == 15 and early:
            order.append(("N1", 0))
        if n == 16 and prev:
            order.append(("RT", 0))
        if n == 17 and early:
            order.append(("Q0", 0))
        if n == 19 and early:
            order.append(("Q1", 0))
    if front:
        order.append(("MT", 0))
    if back:
        order += [("OT", 2), ("PV", 3), ("OT", 3)]
    units = [e for e in order if e[0] in ("ST", "SA")]
    return order, {e: n % 4 for n, e in enumerate(units)}


def bank_holders(q, early, front, back, prev):
    def count(step, e):
        return (20 * step if e[0] == "ST" else 32 * (step + 1)) + e[1] + 1

    units = [e for e in step_events(early, front, back, prev)[0] if e[0] in ("ST", "SA")]
    if not back:
        before = [("K", 7), ("K", 8), ("V", 7), ("V", 8)]
    else:
        first = isinstance(q, int) and q == 0
        last4 = [e for e in step_events(True, True, not first, False)[0] if e[0] in ("ST", "SA")][-4:]
        before = [(e[0], count(q - 1, e)) for e in last4]
    held = before + [(e[0], count(q, e)) for e in units]
    return {e: held[n] for n, e in enumerate(units)}


def flamingo_block(nc, x, ctx_in, g_xattn, g_ffn, wq, bq, wk, bk, wv, bv, wo, bo,
                   router_w, expert_bias, sw1, sw2, sw3, rw1, rw2, rw3, out):
    B, SQ, D = x.shape
    SK = ctx_in.shape[1]
    H, _, HD = wq.shape
    KC = D // P
    PAIRS = H // 2
    HALF_PAIRS = PAIRS // 2
    KP = 160
    REM = SK - P
    T = B * SQ
    NT, NCH = T // P, T // CH
    GROUPS = H // 4
    ROWS = 3 * QUAD
    HALF = P // 2
    SCALE = float(HD) ** -0.5
    E, _, RH = rw1.shape
    SH = sw1.shape[2]
    HT = SH // P
    assert SQ == 2 * CH and D == 2 * P and P < SK <= P + QUAD and HD == 16 and H == 16

    x_t = x.rearrange("b (n p) d -> p (b n) d", p=P)
    out_t = out.rearrange("b (n p) d -> p (b n) d", p=P)

    keep = ExitStack()

    place = {}

    def sbuf(name, shape, dt=F32, stack=keep):
        tensor = stack.enter_context(nc.sbuf_tensor(name, shape, dt))
        size = 4
        for n in shape[1:]:
            size *= n
        place[name] = nc.sbuf_base - (size + 31) // 32 * 32
        return tensor

    def over(host, at, name, shape, dt=F32):
        return nc.alloc_sbuf_tensor_at(name, shape, dt, offset=place[host] + 4 * at)

    def sem(name):
        return keep.enter_context(nc.semaphore(name))

    TOPK = 2
    TILES = (TOPK * T - E) // P + E
    TILES += TILES % 2
    slots_x = nc.dram_tensor("slots_x", [TILES * P, D], F32, kind="Internal").ap()
    slot_home = nc.dram_tensor("slot_home", [TILES * P, 1], I32, kind="Internal").ap()

    def after(eng, semaphore, value):
        if not isinstance(value, int) or value > 0:
            eng.wait_ge(semaphore, value)

    def chunk_tiles(q):
        return bass.ds(q * CHUNK_TILES, CHUNK_TILES)

    dve_holds, pool_holds = sem("dve_holds"), sem("pool_holds")

    x_sb = sbuf("x_sb", [P, NT, D])
    xn2_rows = nc.dram_tensor("xn2_rows", [P, NT, D], F32, kind="Internal").ap()
    stacks = nc.dram_tensor("stacks", [PAIRS, ROWS, B, 2 * KP], F32, kind="Internal").ap()
    xn2T_cols = nc.dram_tensor("xn2T_cols", [P, KC, T], F32, kind="Internal").ap()
    hot = sbuf("hot", [P, NT, TOPK, E])
    hots = sbuf("hots", [P, NT, E])
    gate = sbuf("gate", [P, NT, TOPK])
    shared_w = sbuf("shared_w", [P, KC * 2 * SH + HT * D])
    s12 = shared_w[:, 0:KC * 2 * SH].rearrange("p (c u n) -> p c u n", c=KC, u=2)
    s3 = shared_w[:, KC * 2 * SH:].rearrange("p (m d) -> p m d", m=HT)
    shared_w_loaded = sem("shared_w_loaded")
    ident = sbuf("ident", [P, P])
    gates = sbuf("gates", [P, 2])
    tg = sbuf("tg", [P, 2])

    with ExitStack() as st:
        def sb(name, shape, dt=F32):
            return sbuf(name, shape, dt, st)

        def ps(name):
            return st.enter_context(nc.psum_tensor(name, [P, CH], F32))

        wq_sb, wk_sb, wv_sb = (sb(n, [P, KC, H, HD]) for n in ("wq_sb", "wk_sb", "wv_sb"))
        wo_sb = sb("wo_sb", [P, KC, D])
        rw_sb = sb("rw_sb", [P, KC, E])
        bq_sb, bk_sb = sb("bq_sb", [P, 2]), sb("bk_sb", [P, 2])
        bv_sb, bo_sb = sb("bv_sb", [P, D]), sb("bo_sb", [P, D])
        oT = sb("oT", [P, CH])
        ctx_sb = oT[:].rearrange("p (r d) -> p r d", r=2)
        ctxT = sb("ctxT", [P, KC, B, SK])
        probs = sb("probs", [P, 2, 5, CH])
        kf = probs[:].rearrange("p g i n -> p (g i n)")[:, 0:2 * B * KP].rearrange("p (c b k) -> p c b k", c=2, b=B)
        kh, kl = (over("shared_w", n * 4 * B * KP, f"k{n}", [P, 2, B, KP * 2], F32R) for n in range(2))
        v_all = sb("v_all", [P, 2, B, H, HD + 1])
        k_max = sb("k_max", [ROWS, PAIRS, 2 * KP], F32R)
        k_st = sb("k_st", [ROWS + 2, PAIRS, 3 * HALF + 2 * P], F32R)
        head_mask, mask_sum = sb("head_mask", [P, 2]), sb("mask_sum", [P, 8])
        ones_rows = sb("ones_rows", [2, 3 * HALF + 2 * P])
        v_main = sb("v_main", [P, H, QUAD])
        v_rem = sb("v_rem", [P, GROUPS, P])
        stats, mv = sb("stats", [P, 4, 6]), sb("mv", [P, 4, 2])
        ve, rstd = sb("ve", [P, 4]), sb("rstd", [P, 4])
        minus_half = sb("minus_half", [P, 4])
        stats2, mv2 = sb("stats2", [P, 4, 6]), sb("mv2", [P, 4, 2])
        ve2, rstd2 = sb("ve2", [P, 4]), sb("rstd2", [P, 4])
        xn = sb("xn", [P, 4, D])
        xnT = sb("xnT", [P, KC, CH])
        qh, ql = sb("qh", [P, 2, CH], F32R), sb("ql", [P, 2, CH], F32R)
        q_st = [sb(f"q_st{i}", [ROWS + 2, PAIRS, CH], F32R) for i in range(2)]
        mx = sb("mx", [P, 4, 2, PAIRS])
        mT = sb("mT", [H, CH], F32R)
        rden = sb("rden", [P, 4, 4])
        ctxn = sb("ctxn", [P, 4, D])
        ctxnT = sb("ctxnT", [P, KC, CH])
        xn2c = sb("xn2c", [P, 4, D])
        att = xn2c
        xn2T = sb("xn2T", [P, KC, CH])

        zeros = sb("zeros", [P, D])
        no_home = sb("no_home", [P, TILES], I32)
        bias_sb, iota_e = sb("bias_sb", [P, E]), sb("iota_e", [P, E])
        exp_neg, score, sel = (sb(n, [P, 4, E]) for n in ("exp_neg", "score", "sel"))
        best, best_at = sb("best", [P, 4, 8]), sb("best_at", [P, 4, 8], U32)
        best_f = sb("best_f", [P, 4, TOPK])
        gated = sb("gated", [P, 4, TOPK, E])

        T0, T1, M, PV = ps("T0"), ps("T1"), ps("M"), ps("PV")
        S = [ps(f"S{i}") for i in range(4)]

        consts_done = sem("consts_done")
        weights_loaded = sem("weights_loaded")
        ones_loaded = sem("ones_loaded")
        slots_cleared = sem("slots_cleared")
        gates_loaded, tg_ready = sem("gates_loaded"), sem("tg_ready")
        ctx_loaded = sem("ctx_loaded")
        ctxT_done, ctxT_ready = sem("ctxT_done"), sem("ctxT_ready")
        kT_done, kf_ready = sem("kT_done"), sem("kf_ready")
        kh_ready, kl_ready = sem("kh_ready"), sem("kl_ready")
        kmax_loaded, kst_loaded = sem("kmax_loaded"), sem("kst_loaded")
        v_done, v_kept, v_loaded = sem("v_done"), sem("v_kept"), sem("v_loaded")
        x_loaded, x_rest_loaded = sem("x_loaded"), sem("x_rest_loaded")
        ln_step, rstd_ready, xn_ready = sem("ln_step"), sem("rstd_ready"), sem("xn_ready")
        xn_transposed, xnT_ready = sem("xn_transposed"), sem("xnT_ready")
        q_done = sem("q_done")
        qh_ready, ql_ready = sem("qh_ready"), sem("ql_ready")
        q_loaded = [sem(f"q_loaded{i}") for i in range(2)]
        m_loaded = [sem(f"m_loaded{i}") for i in range(2)]
        sa_done, sa_read, st_done = sem("sa_done"), sem("sa_read"), sem("st_done")
        mT_done, mT_ready = sem("mT_done"), sem("mT_ready")
        probs_ready, pv_done = sem("probs_ready"), sem("pv_done")
        oT_ready, o_done = sem("oT_ready"), sem("o_done")
        rden_ready, ctxn_ready = sem("rden_ready"), sem("ctxn_ready")
        ctxn_transposed, ctxnT_ready = sem("ctxn_transposed"), sem("ctxnT_ready")
        wo_done, att_ready, x1_ready = sem("wo_done"), sem("att_ready"), sem("x1_ready")
        ln2_step, rstd2_ready, xn2_ready = sem("ln2_step"), sem("rstd2_ready"), sem("xn2_ready")
        xn2_stored, xn2T_stored = sem("xn2_stored"), sem("xn2T_stored")
        xn2_transposed, xn2T_ready = sem("xn2_transposed"), sem("xn2T_ready")
        lg_done = sem("lg_done")
        logits_read, route, bias_loaded = sem("logits_read"), sem("route"), sem("bias_loaded")
        kf_padded, k_stacked = sem("kf_padded"), sem("k_stacked")
        mask_step = sem("mask_step")

        N_QDMA = 16 * 3 * HALF_PAIRS
        N_VDMA = 16 * 5
        N_WEIGHTS = 16 * (3 * KC + 2 + 2 + 2)

        CONSTS = 13
        ROUTE = 11

        def run_steps(eng, step):
            step(eng, -2, -1, 0, True, False, False, False)
            step(eng, -1, -1, 1, True, True, False, False)
            step(eng, 0, 0, 0, True, True, True, False)
            step(eng, 1, 0, 1, True, True, True, True)
            with eng.Fori(0, B - 2) as b:
                step(eng, b * 2 + 2, b + 1, 0, True, True, True, True)
                step(eng, b * 2 + 3, b + 1, 1, True, True, True, True)
            step(eng, NCH - 2, B - 1, 0, False, True, True, True)
            step(eng, NCH - 1, B - 1, 1, False, False, True, True)
            step(eng, NCH, B, 0, False, False, False, True)

        def raw(ap):
            return ap.bitcast(F32)

        with nc.Block() as block:
            @block.sync
            def _(sp):
                sp.dma_start(x_sb[:, 0:2 * CHUNK_TILES, :], x_t[:, 0:2 * CHUNK_TILES, :]).then_inc(x_loaded, 16)

                def load_ctx(b):
                    if b:
                        sp.wait_ge(ctxT_done, b)
                        sp.wait_ge(ctx_loaded, 32 * b)
                    sp.dma_start(ctx_sb[:, 0, :], ctx_in[b, 0:P, :]).then_inc(ctx_loaded, 16)
                    sp.dma_start(ctx_sb[0:REM, 1, :], ctx_in[b, P:SK, :]).then_inc(ctx_loaded, 16)

                load_ctx(0)
                for w_sb, w in ((wk_sb, wk), (wv_sb, wv), (wq_sb, wq)):
                    for kc in range(KC):
                        sp.dma_start(w_sb[:, kc], w[:, kc * P:(kc + 1) * P, :].rearrange("h p d -> p h d")
                                     ).then_inc(weights_loaded, 16)
                for b_sb, b_in in ((bq_sb, bq), (bk_sb, bk)):
                    sp.dma_start(b_sb[:], b_in.rearrange("(c h) d -> (h d) c", c=2), allow_slow_non_contiguous=True).then_inc(weights_loaded, 16)
                sp.dma_start(bv_sb[:], bv.rearrange("h d -> (h d)").partition_broadcast(P)).then_inc(weights_loaded, 16)
                sp.dma_start(bo_sb[:], bo.partition_broadcast(P)).then_inc(weights_loaded, 16)
                sp.dma_start(wo_sb[:], wo.rearrange("(c p) n -> p c n", p=P)).then_inc(weights_loaded, 16)
                sp.dma_start(rw_sb[:], router_w.rearrange("(c p) n -> p c n", p=P)).then_inc(weights_loaded, 16)
                sp.dma_start(bias_sb[:], expert_bias.partition_broadcast(P)).then_inc(bias_loaded, 16)
                sp.dma_start(gates[:, 0:1], g_xattn.partition_broadcast(P)).then_inc(gates_loaded, 16)
                sp.dma_start(gates[:, 1:2], g_ffn.partition_broadcast(P)).then_inc(gates_loaded, 16)
                for b in range(1, B):
                    load_ctx(b)
                for b in range(1, B):
                    sp.dma_start(x_sb[:, 2 * b * CHUNK_TILES:2 * (b + 1) * CHUNK_TILES, :],
                                 x_t[:, 2 * b * CHUNK_TILES:2 * (b + 1) * CHUNK_TILES, :]).then_inc(x_rest_loaded, 16)
                sp.wait_ge(consts_done, CONSTS)
                sp.dma_start(raw(k_st[ROWS:ROWS + 2, :, :]), ones_rows[:].rearrange("r (o n) -> r o n", o=1)
                             .to_broadcast([2, PAIRS, 3 * HALF + 2 * P])).then_inc(ones_loaded, 16)
                sp.wait_ge(kh_ready, 1)
                sp.wait_ge(kl_ready, 1)
                for part, src in enumerate((kh, kl, kh)):
                    for j in range(HALF_PAIRS):
                        sp.dma_start(
                            stacks[j::HALF_PAIRS, QUAD * part:QUAD * (part + 1)].rearrange("c r b n -> r c (b n)"),
                            raw(src[QUAD * j:QUAD * (j + 1)]).rearrange("r c b n -> r c (b n)")).then_inc(k_stacked, 16)
                sp.wait_ge(k_stacked, 16 * 3 * HALF_PAIRS)

                sp.dma_start(s12[:, :, 0, :], sw1[0].rearrange("(c p) n -> p c n", p=P)).then_inc(shared_w_loaded, 16)
                sp.dma_start(s12[:, :, 1, :], sw2[0].rearrange("(c p) n -> p c n", p=P)).then_inc(shared_w_loaded, 16)
                sp.dma_start(s3, sw3[0].rearrange("(c p) n -> p c n", p=P)).then_inc(shared_w_loaded, 16)
                sp.dma_start(slot_home.rearrange("(p t) o -> p (t o)", p=P), no_home[:]
                             ).then_inc(slots_cleared, 16)
                sp.dma_start(slots_x.rearrange("(t p) d -> p t d", p=P), zeros[:].rearrange(
                    "p (o d) -> p o d", o=1).to_broadcast([P, TILES, D])).then_inc(slots_cleared, 16)

                def step(sp, q, b, k, early, front, back, prev):
                    n, r = q + 1, q - 1
                    if prev:
                        sp.wait_ge(xn2_ready, q)
                        sp.dma_start(xn2_rows[:, chunk_tiles(r), :], xn2c[:]).then_inc(xn2_stored, 16)
                        sp.wait_ge(xn2T_ready, 2 * q)
                        sp.dma_start(xn2T_cols[:, :, bass.ds(r * CH, CH)], xn2T[:]).then_inc(xn2T_stored, 16)
                    if front and k:
                        if back:
                            sp.wait_ge(st_done, 20 * n)
                        for cols, keys in ((slice(HALF, 2 * HALF), slice(2 * P, 2 * KP)),
                                           (slice(3 * HALF, 3 * HALF + 2 * P), slice(0, 2 * P))):
                            sp.dma_start(raw(k_st[0:ROWS, :, cols]),
                                         stacks[:, :, bass.ds(b + 1, 1), keys].rearrange("p r o n -> r p (o n)")
                                         ).then_inc(kst_loaded, 16)
                    if front:
                        sp.wait_ge(mT_ready, n + 1)
                        for i in range(2):
                            sp.dma_start(raw(q_st[1 - k][ROWS + i:ROWS + i + 1, :, :]),
                                         raw(mT[PAIRS * i:PAIRS * (i + 1), :])).then_inc(m_loaded[1 - k], 16)
                    if early:
                        if back:
                            sp.wait_ge(st_done, 20 * n)
                        sp.wait_ge(ql_ready, 2 * n + 4)
                        for part, src in enumerate((qh, qh, ql)):
                            for j in range(HALF_PAIRS):
                                sp.dma_start(raw(q_st[k][QUAD * part:QUAD * (part + 1), j::HALF_PAIRS, :]),
                                             raw(src[QUAD * j:QUAD * (j + 1), :, :])).then_inc(q_loaded[k], 16)
                    if front and k:
                        if back:
                            sp.wait_ge(pv_done, 4 * n)
                        else:
                            sp.wait_ge(v_kept, 2 * B)
                        sp.dma_start(v_main[:, :, 0:HD + 1],
                                     v_all[:, 0, bass.ds(b + 1, 1)].rearrange("p o h d -> p (o h) d")
                                     ).then_inc(v_loaded, 16)
                        for j in range(4):
                            at = HALF * (j // 2) + j % 2
                            sp.dma_start(v_rem[at:at + 2 * REM - 1:2, :, QUAD * j:QUAD * j + HD + 1],
                                         v_all[0:REM, 1, bass.ds(b + 1, 1), j::4].rearrange("p o g d -> p (o g) d")
                                         ).then_inc(v_loaded, 16)
                    if early and not k:
                        if front:
                            sp.wait_ge(sa_done, 32 * (n + 1))
                        sp.dma_start(raw(k_max[:]), stacks[:, :, bass.ds(b + 1, 1), :].rearrange("p r o n -> r p (o n)")
                                     ).then_inc(kmax_loaded, 16)

                run_steps(sp, step)
                sp.wait_ge(shared_w_loaded, 48)
                sp.wait_ge(xn2_stored, 16 * NCH)
                sp.wait_ge(xn2T_stored, 16 * NCH)
                sp.wait_ge(slots_cleared, 32)

            @block.gpsimd
            def _(pool):
                g = nc.gpsimd
                count = [0]

                def const(ins):
                    ins.then_inc(consts_done, 1)
                    count[0] += 1
                    pool.wait_ge(consts_done, count[0])

                def select(ap, pattern, base, mult):
                    const(g.affine_select(out=ap, in_=ap, compare_op=ALU.not_equal, fill=1.0, base=base,
                                          pattern=pattern, channel_multiplier=mult))

                const(g.memset(zeros[:], 0.0))
                const(g.memset(ident[:], 0.0))
                const(g.memset(ones_rows[:], 0.0))
                const(g.memset(minus_half[:], -0.5))
                const(g.iota(no_home[:], pattern=[[1, TILES]], base=TOPK * T, channel_multiplier=TILES))
                const(g.iota(iota_e[:], pattern=[[1, E]], base=0, channel_multiplier=0,
                             allow_small_or_imprecise_dtypes=True))
                const(g.memset(v_main[:], 0.0))
                const(g.memset(v_rem[:], 0.0))
                const(g.memset(k_st[:].bitcast(F32), 0.0))
                select(ident[:], [[-1, P]], 0, 1)
                for c0, c1 in ((HALF, 2 * HALF), (3 * HALF, 3 * HALF + 2 * P)):
                    select(ones_rows[:, c0:c1].rearrange("r (n i) -> r n i", i=2), [[0, (c1 - c0) // 2], [-1, 2]], 0, 1)
                const(g.memset(v_all[:, :, :, :, HD:HD + 1], 1.0))
                assert count[0] == CONSTS
                pool.wait_ge(kf_ready, 2 * B)
                g.tensor_copy(kf[:, :, :, SK:KP], kf[:, :, :, SK - 1:SK].to_broadcast([P, 2, B, KP - SK])
                              ).then_inc(kf_padded, 1)

                def step(pool, q, b, k, early, front, back, prev):
                    e = q + 2
                    if early:
                        pool.wait_ge(ln_step, 3 * e + 3)
                        after(pool, xn_ready, e)
                        g.tensor_tensor(rstd[:], ve[:], minus_half[:], ALU.pow).then_inc(rstd_ready, 1)
                    if prev:
                        pool.wait_ge(ln2_step, 3 * q)
                        g.tensor_tensor(rstd2[:], ve2[:], minus_half[:], ALU.pow).then_inc(rstd2_ready, 1)

                run_steps(pool, step)

            @block.scalar
            def _(act):
                s = nc.scalar
                act.wait_ge(gates_loaded, 32)
                s.activation(tg[:], gates[:], ACT.Tanh).then_inc(tg_ready, 1)
                act.wait_ge(weights_loaded, N_WEIGHTS)
                for b in range(B):
                    act.wait_ge(ctxT_done, b + 1)
                    s.copy(ctxT[:, :, b, :], T0[:, 0:2 * SK].rearrange("p (c k) -> p c k", c=2)
                           ).then_inc(ctxT_ready, 1)
                for b in range(B):
                    for c in range(2):
                        act.wait_ge(kT_done, 2 * b + c + 1)
                        s.activation(kf[:, c, b, 0:SK], S[c][:, 0:SK], ACT.Identity, bias=bk_sb[:, c:c + 1]
                                     ).then_inc(kf_ready, 1)

                def step(act, q, b, k, early, front, back, prev):
                    e, r = q + 2, q - 1
                    events, banks = step_events(early, front, back, prev)
                    for kind, u in events:
                        if kind in ("C0", "C1"):
                            c = int(kind[1])
                            act.wait_ge(ctxn_transposed, 2 * r + c + 1)
                            after(act, wo_done, 2 * r)
                            s.copy(ctxnT[:, c, :], (T0, T1)[c][:]).then_inc(ctxnT_ready, 1)
                        if kind in ("X0", "XX"):
                            c = int(kind == "XX")
                            act.wait_ge(xn2_transposed, 2 * r + c + 1)
                            after(act, lg_done, r)
                            after(act, xn2T_stored, 16 * r)
                            s.copy(xn2T[:, c, :], T0[:]).then_inc(xn2T_ready, 1)
                        if kind == "RT":
                            act.wait_ge(lg_done, q)
                            after(act, route, ROUTE * r)
                            s.activation(exp_neg[:], M[:, 0:4 * E].rearrange("p (t e) -> p t e", t=4), ACT.Exp,
                                         scale=-1.0).then_inc(logits_read, 1)
                        if kind in ("N0", "N1"):
                            c = int(kind[1])
                            act.wait_ge(xn_transposed, 2 * e + c + 1)
                            after(act, q_done, 2 * e)
                            s.copy(xnT[:, c, :], T0[:]).then_inc(xnT_ready, 1)
                        if kind in ("Q0", "Q1"):
                            c = int(kind[1])
                            act.wait_ge(q_done, 2 * e + c + 1)
                            if front and c == 0:
                                act.wait_ge(q_loaded[1 - k], N_QDMA * (b + 1 + k))
                            s.activation(qh[:, c, :], M[:], ACT.Identity, bias=bq_sb[:, c:c + 1]).then_inc(qh_ready, 1)
                        if kind == "ST":
                            g, i = u // 5, u % 5
                            act.wait_ge(st_done, 20 * q + u + 1)
                            after(act, pv_done, 4 * q + g - 1)
                            s.activation(probs[:, g % 2, i, :], S[banks[kind, u]][:], ACT.Exp,
                                         scale=SCALE).then_inc(probs_ready, 1)
                        if kind == "PV" and u > 0:
                            copy_out(act, q, u - 1)
                            if u == 3:
                                copy_out(act, q, 3)

                def copy_out(act, q, g):
                    act.wait_ge(pv_done, 4 * q + g + 1)
                    after(act, o_done, 4 * q + g)
                    s.copy(oT[:], PV[:]).then_inc(oT_ready, 1)

                run_steps(act, step)

            @block.vector
            def _(dve):
                v = nc.vector
                for b in range(B):
                    for r, rows in ((0, P), (1, REM)):
                        dve.wait_ge(v_done, 2 * b + r + 1)
                        if b == 0 and r == 0:
                            dve.wait_ge(weights_loaded, N_WEIGHTS)
                        v.tensor_tensor(v_all[0:rows, r, b, :, 0:HD],
                                        S[2 + r][0:rows, 0:D].rearrange("p (h d) -> p h d", d=HD),
                                        bv_sb[0:rows, :].rearrange("p (h d) -> p h d", d=HD), ALU.add
                                        ).then_inc(v_kept, 1)

                dve.wait_ge(tg_ready, 1)
                dve.wait_ge(bias_loaded, 16)
                dve.wait_ge(consts_done, CONSTS)
                v.reduce_sum(mask_sum[:], ident[:].rearrange("p (n d) -> p n d", d=HD), AX).then_inc(mask_step, 1)
                dve.wait_ge(mask_step, 1)
                v.reduce_sum(head_mask[:], mask_sum[:].rearrange("p (j i) -> p i j", i=2), AX).then_inc(mask_step, 1)
                dve.wait_ge(mask_step, 2)
                dve.wait_ge(kf_padded, 1)
                by_head = [t[:].rearrange("p c b (k i) -> p (c b) k i", i=2) for t in (kh, kl)]
                kf_rows = kf.rearrange("p c b k -> p (c b) k")
                for i in range(2):
                    last = v.tensor_scalar(by_head[0][:, :, :, i], kf_rows, head_mask[:, i:i + 1], None, ALU.mult)
                last.then_inc(kh_ready, 1)
                dve.wait_ge(kh_ready, 1)
                for i in range(2):
                    last = v.scalar_tensor_tensor(by_head[1][:, :, :, i], kf_rows, head_mask[:, i:i + 1],
                                                  by_head[0][:, :, :, i].bitcast(F32), ALU.mult, ALU.subtract)
                last.then_inc(kl_ready, 1)

                def statistics(q, st_, mv_, ve_, step_sem, ve_read):
                    for t in range(CHUNK_TILES):
                        last = v.bn_stats(st_[:, t, :], x_sb[:, bass.ds(q * CHUNK_TILES + t, 1), :].rearrange(
                            "p o d -> p (o d)"))
                    last.then_inc(step_sem, 1)
                    dve.wait_ge(step_sem, 3 * q + 1)
                    dve.sem_inc(dve_holds, 1)
                    for t in range(CHUNK_TILES):
                        last = v.bn_aggr(mv_[:, t, :], st_[:, t, :])
                    last.then_inc(step_sem, 1)
                    dve.wait_ge(step_sem, 3 * q + 2)
                    after(dve, ve_read, q)
                    v.tensor_scalar(ve_[:], mv_[:, :, 1], EPS, None, ALU.add).then_inc(step_sem, 1)

                def normalise(q, mv_, rstd_, out_, done):
                    for t in range(CHUNK_TILES):
                        last = v.tensor_scalar(out_[:, t, :], x_sb[:, bass.ds(q * CHUNK_TILES + t, 1), :].rearrange(
                            "p o d -> p (o d)"), mv_[:, t, 0:1], rstd_[:, t:t + 1], ALU.subtract, ALU.mult)
                    last.then_inc(done, 1)

                def route_chunk(r, q):
                    done = [0]

                    def then(ins):
                        done[0] += 1
                        ins.then_inc(route, 1)
                        dve.wait_ge(route, r * ROUTE + done[0])
                        dve.sem_inc(dve_holds, 1)

                    dve.wait_ge(logits_read, q)
                    then(v.tensor_scalar(score[:], exp_neg[:], 1.0, None, ALU.add))
                    then(v.reciprocal(score[:], score[:]))
                    then(v.tensor_tensor(sel[:], score[:], bias_sb[:].rearrange("p (o e) -> p o e", o=1).to_broadcast(
                        [P, 4, E]), ALU.add))
                    for t in range(CHUNK_TILES):
                        last = v.max(best[:, t, :], sel[:, t, :])
                    then(last)
                    for t in range(CHUNK_TILES):
                        last = v.max_index(best_at[:, t, :], best[:, t, :], sel[:, t, :])
                    then(last)
                    then(v.tensor_copy(best_f[:], best_at[:, :, 0:TOPK]))
                    then(v.tensor_tensor(
                        hot[:, chunk_tiles(r)], iota_e[:].rearrange("p (o u e) -> p o u e", o=1, u=1).to_broadcast(
                            [P, 4, TOPK, E]),
                        best_f[:].rearrange("p t (k o) -> p t k o", o=1).to_broadcast([P, 4, TOPK, E]), ALU.is_equal))
                    then(v.tensor_tensor(hots[:, chunk_tiles(r), :], hot[:, chunk_tiles(r), 0, :],
                                         hot[:, chunk_tiles(r), 1, :], ALU.add))
                    then(v.tensor_tensor(gated[:], hot[:, chunk_tiles(r)], score[:].rearrange(
                        "p t (o e) -> p t o e", o=1).to_broadcast([P, 4, TOPK, E]), ALU.mult))
                    then(v.reduce_sum(gate[:, chunk_tiles(r), :], gated[:], AX))
                    then(v.tensor_scalar(gate[:, chunk_tiles(r), :], gate[:, chunk_tiles(r), :], tg[:, 1:2], None,
                                         ALU.mult))
                    assert done[0] == ROUTE

                def step(dve, q, b, k, early, front, back, prev):
                    n, e, r = q + 1, q + 2, q - 1
                    events, banks = step_events(early, front, back, prev)
                    for kind, u in events:
                        if kind == "L1":
                            if isinstance(e, int) and e < 2:
                                dve.wait_ge(x_loaded, 16)
                            else:
                                dve.wait_ge(x_rest_loaded, 16 * (B - 1))
                            statistics(e, stats, mv, ve, ln_step, rstd_ready)
                            dve.wait_ge(rstd_ready, e + 1)
                            after(dve, xn_transposed, 2 * e)
                            normalise(e, mv, rstd, xn, xn_ready)
                        if kind in ("W0", "W1"):
                            c = int(kind[1])
                            if c == 0:
                                after(dve, xn2_transposed, 2 * r)
                                after(dve, xn2_stored, 16 * r)
                            dve.wait_ge(wo_done, 2 * r + c + 1)
                            v.tensor_tensor(att[:, 2 * c:2 * c + 2, :],
                                            (M, PV)[c][:].rearrange("p (t d) -> p t d", t=2),
                                            bo_sb[:].rearrange("p (o d) -> p o d", o=1).to_broadcast([P, 2, D]),
                                            ALU.add).then_inc(att_ready, 1)
                        if kind == "X1":
                            dve.wait_ge(att_ready, 2 * r + 2)
                            v.scalar_tensor_tensor(x_sb[:, chunk_tiles(r), :], att[:], tg[:, 0:1],
                                                   x_sb[:, chunk_tiles(r), :], ALU.mult, ALU.add
                                                   ).then_inc(x1_ready, 1)
                        if kind == "L2":
                            dve.wait_ge(x1_ready, q)
                            dve.sem_inc(dve_holds, 1)
                            statistics(r, stats2, mv2, ve2, ln2_step, rstd2_ready)
                            dve.wait_ge(rstd2_ready, q)
                            normalise(r, mv2, rstd2, xn2c, xn2_ready)
                        if kind in ("Q0", "Q1"):
                            c = int(kind[1])
                            dve.wait_ge(qh_ready, 2 * e + c + 1)
                            v.scalar_tensor_tensor(ql[:, c, :], M[:], bq_sb[:, c:c + 1], qh[:, c, :].bitcast(F32),
                                                   ALU.add, ALU.subtract).then_inc(ql_ready, 1)
                        if kind == "SA":
                            t, p = u // PAIRS, u % PAIRS
                            dve.wait_ge(sa_done, 32 * n + u + 1)
                            if u == 0:
                                after(dve, mT_done, n)
                            v.reduce_max(mx[:, t, :, p], S[banks[kind, u]][:, 0:2 * KP].rearrange(
                                "p (k i) -> p i k", i=2), AX).then_inc(sa_read, 1)
                        if kind == "MT":
                            dve.wait_ge(mT_done, n + 1)
                            if back:
                                dve.wait_ge(m_loaded[k], 32 * (b + 1))
                            v.tensor_scalar(mT[:], T0[0:H, :], -1.0, None, ALU.mult).then_inc(mT_ready, 1)
                        if kind == "RT":
                            route_chunk(r, q)
                        if kind == "OT":
                            turned = T1[:].rearrange("p (t j r) -> p t j r", t=4, j=4)
                            dve.wait_ge(o_done, 4 * q + u + 1)
                            v.reciprocal(rden[:], turned[:, :, :, HD]).then_inc(rden_ready, 1)
                            dve.wait_ge(rden_ready, 4 * q + u + 1)
                            if u == 0:
                                after(dve, ctxn_transposed, 2 * q)
                            v.tensor_tensor(
                                ctxn[:, :, 4 * HD * u:4 * HD * (u + 1)].rearrange("p t (j d) -> p t j d", j=4),
                                turned[:, :, :, 0:HD],
                                rden[:].rearrange("p t (j o) -> p t j o", o=1).to_broadcast([P, 4, 4, HD]),
                                ALU.mult).then_inc(ctxn_ready, 1)

                run_steps(dve, step)

            @block.tensor
            def _(pe):
                mm, turn = nc.tensor.matmul, nc.tensor.transpose
                pe.wait_ge(consts_done, CONSTS)
                for b in range(B):
                    pe.wait_ge(ctx_loaded, 32 * (b + 1))
                    after(pe, ctxT_ready, b)
                    for c in range(KC):
                        turn(T0[:, c * SK:c * SK + P], ctx_sb[:, 0, c * P:(c + 1) * P], ident[:])
                        last = turn(T0[:, c * SK + P:(c + 1) * SK], ctx_sb[0:REM, 1, c * P:(c + 1) * P],
                                    ident[0:REM, 0:REM])
                    last.then_inc(ctxT_done, 1)
                pe.wait_ge(weights_loaded, N_WEIGHTS)
                for b in range(B):
                    pe.wait_ge(ctxT_ready, b + 1)
                    for c in range(2):
                        after(pe, kf_ready, 2 * b + c - 1)
                        for kc in range(KC):
                            last = mm(S[c][:, 0:SK], wk_sb[:, kc, 8 * c:8 * c + 8, :].rearrange("p h d -> p (h d)"),
                                      ctxT[:, kc, b, :], start=kc == 0, stop=kc == KC - 1)
                        last.then_inc(kT_done, 1)
                    for r, keys in ((0, slice(0, P)), (1, slice(P, SK))):
                        after(pe, v_kept, 2 * b + r - 1)
                        for kc in range(KC):
                            last = mm(S[2 + r][0:keys.stop - keys.start, 0:D], ctxT[:, kc, b, keys],
                                      wv_sb[:, kc].rearrange("p h d -> p (h d)"), start=kc == 0, stop=kc == KC - 1)
                        last.then_inc(v_done, 1)

                def step(pe, q, b, k, early, front, back, prev):
                    n, e, r = q + 1, q + 2, q - 1
                    events, banks = step_events(early, front, back, prev)
                    held = bank_holders(q, early, front, back, prev) if front or back else {}

                    def turn_chunk(bank, src, c, done):
                        for t in range(CHUNK_TILES):
                            last = turn(bank[:, t * P:(t + 1) * P], src[:, t, c * P:(c + 1) * P], ident[:])
                        last.then_inc(done, 1)

                    for kind, u in events:
                        if kind == "C0":
                            pe.wait_ge(ctxn_ready, 4 * r + 4)
                            if back:
                                pe.wait_ge(mT_ready, q + 1)
                            else:
                                pe.wait_ge(xn2T_ready, 2 * r)
                            turn_chunk(T0, ctxn, 0, ctxn_transposed)
                        if kind == "C1":
                            turn_chunk(T1, ctxn, 1, ctxn_transposed)
                        if kind in ("W0", "W1"):
                            c = int(kind[1])
                            bank = (M, PV)[c]
                            pe.wait_ge(ctxnT_ready, 2 * r + 2)
                            if c == 1:
                                pe.wait_ge(oT_ready, 4 * r + 4)
                            elif early or isinstance(q, int) and q == NCH - 2:
                                pe.wait_ge(ql_ready, 2 * n + 2)
                            else:
                                pe.wait_ge(logits_read, r)
                            for t in (2 * c, 2 * c + 1):
                                for kc in range(KC):
                                    last = mm(bank[:, (t % 2) * D:(t % 2 + 1) * D], ctxnT[:, kc, t * P:(t + 1) * P],
                                              wo_sb[:, kc, :], start=kc == 0, stop=kc == KC - 1)
                            last.then_inc(wo_done, 1)
                        if kind == "X0":
                            pe.wait_ge(xn2_ready, q)
                            pe.wait_ge(ctxnT_ready, 2 * r + 1)
                            turn_chunk(T0, xn2c, 0, xn2_transposed)
                        if kind == "XX":
                            pe.wait_ge(xn2T_ready, 2 * r + 1)
                            turn_chunk(T0, xn2c, 1, xn2_transposed)
                        if kind == "RT":
                            pe.wait_ge(xn2T_ready, 2 * r + 2)
                            pe.wait_ge(att_ready, 2 * r + 1)
                            for t in range(CHUNK_TILES):
                                for kc in range(KC):
                                    last = mm(M[:, t * E:(t + 1) * E], xn2T[:, kc, t * P:(t + 1) * P], rw_sb[:, kc, :],
                                              start=kc == 0, stop=kc == KC - 1)
                            last.then_inc(lg_done, 1)
                        if kind == "N0":
                            pe.wait_ge(xn_ready, e + 1)
                            if prev:
                                pe.wait_ge(xn2T_ready, 2 * r + 2)
                            elif back:
                                pe.wait_ge(mT_ready, 1)
                            elif front:
                                pe.wait_ge(xnT_ready, 2)
                            else:
                                pe.wait_ge(ctxT_ready, B)
                            turn_chunk(T0, xn, 0, xn_transposed)
                        if kind == "N1":
                            pe.wait_ge(xnT_ready, 2 * e + 1)
                            turn_chunk(T0, xn, 1, xn_transposed)
                        if kind in ("Q0", "Q1"):
                            c = int(kind[1])
                            pe.wait_ge(xnT_ready, 2 * e + 2)
                            if c == 0 and prev:
                                pe.wait_ge(logits_read, q)
                            else:
                                after(pe, ql_ready, 2 * e + c)
                            for kc in range(KC):
                                last = mm(M[:], wq_sb[:, kc, 8 * c:8 * c + 8, :].rearrange("p h d -> p (h d)"),
                                          xnT[:, kc, :], start=kc == 0, stop=kc == KC - 1)
                            last.then_inc(q_done, 1)
                        if kind == "MT":
                            pe.wait_ge(sa_read, 32 * (n + 1))
                            if early:
                                pe.wait_ge(xnT_ready, 2 * e + 2)
                            else:
                                pe.wait_ge(xn2T_ready, 2 * r + 2)
                            for t in range(CHUNK_TILES):
                                last = turn(T0[0:H, t * P:(t + 1) * P], mx[:, t].rearrange("p i c -> p (i c)"), ident[:])
                            last.then_inc(mT_done, 1)
                        if kind in ("ST", "SA"):
                            was, value = held[kind, u]
                            pe.wait_ge({"ST": probs_ready, "SA": sa_read, "K": kf_ready, "V": v_kept}[was], value)
                            bank = S[banks[kind, u]]
                        if kind == "SA":
                            t, p = u // PAIRS, u % PAIRS
                            if u == 0:
                                pe.wait_ge(q_loaded[1 - k], N_QDMA * (b + k + 1))
                                pe.wait_ge(kmax_loaded, 16 * (b + k + 1))
                            mm(bank[:, 0:2 * KP], q_st[1 - k][0:ROWS, p, t * P:(t + 1) * P],
                               k_max[:, p, :], start=True, stop=True
                               ).then_inc(sa_done, 1)
                        if kind == "ST":
                            g, i = u // 5, u % 5
                            if u == 0:
                                pe.wait_ge(m_loaded[k], 32 * (b + 1))
                                pe.wait_ge(kst_loaded, 32 * (b + 1))
                                pe.wait_ge(ones_loaded, 16)
                            if i < 4:
                                p = 2 * g + i // 2
                                last = mm(bank[:], k_st[:, p, 3 * HALF + i % 2:3 * HALF + i % 2 + 2 * P - 1:2], q_st[k][:, p, :],
                                          start=True, stop=True)
                            else:
                                for p in (2 * g, 2 * g + 1):
                                    at = HALF * (1 - p % 2)
                                    last = mm(bank[:], k_st[:, p, at:at + P], q_st[k][:, p, :],
                                              start=p == 2 * g, stop=p == 2 * g + 1)
                            last.then_inc(st_done, 1)
                        if kind == "PV":
                            pe.wait_ge(probs_ready, 20 * q + 5 * u + 5)
                            if u == 0:
                                pe.wait_ge(v_loaded, N_VDMA * (b + 1))
                                after(pe, att_ready, 2 * q)
                            else:
                                pe.wait_ge(oT_ready, 4 * q + u)
                            for j in range(4):
                                mm(PV[QUAD * j:QUAD * (j + 1), :], v_main[:, 4 * u + j, :], probs[:, u % 2, j, :],
                                   start=True, stop=False)
                            mm(PV[:], v_rem[:, u, :], probs[:, u % 2, 4, :], start=False, stop=True
                               ).then_inc(pv_done, 1)
                        if kind == "OT":
                            pe.wait_ge(oT_ready, 4 * q + u + 1)
                            if u > 0:
                                pe.wait_ge(ctxn_ready, 4 * q + u)
                            else:
                                after(pe, ctxnT_ready, 2 * q)
                            for t in range(CHUNK_TILES):
                                last = turn(T1[:, t * P:(t + 1) * P], oT[:, t * P:(t + 1) * P], ident[:])
                            last.then_inc(o_done, 1)

                run_steps(pe, step)

    with ExitStack() as st:
        def sb(name, shape, dt=F32):
            return sbuf(name, shape, dt, st)

        def ps(name):
            return st.enter_context(nc.psum_tensor(name, [P, CH], F32))

        TILE_TURNS = 6
        MAX_TILES = T // P
        NR = RH // P

        x_rows = slots_x
        y_rows = nc.dram_tensor("y_rows", [TOPK * T + TILES * P, D], F32, kind="Internal").ap()

        w12 = sb("w12", [P, E, KC, 2 * RH])
        w3 = sb("w3", [P, E, NR, D])
        s12_hi, s3_hi = sb("s12_hi", [P, KC, 2, SH], F32R), sb("s3_hi", [P, HT, D], F32R)
        s12_lo = over("shared_w", 0, "s12_lo", [P, KC, 2, SH], F32R)
        s3_lo = over("shared_w", KC * 2 * SH, "s3_lo", [P, HT, D], F32R)
        LATE = E - 4 * KC * CH // (NR * D)
        assert 2 * LATE >= E
        xT, xT_hi, xT_lo = ([over("w3", LATE * NR * D + (2 * part + i) * KC * CH, f"{name}{i}", [P, KC, CH], dt)
                             for i in range(2)] for name, part, dt in (("xT", 0, F32), ("xT_hi", 1, F32R), ("xT_lo", 0, F32R)))
        act_all = sb("act_all", [P, 8, CH])
        act_s, act_hi, act_lo = ([over("act_all", (4 * part + i) * CH, f"{name}{i}", [P, CH], dt) for i in range(4)]
                                 for name, part, dt in (("act_s", 0, F32), ("act_hi", 1, F32R), ("act_lo", 0, F32R)))

        iota_p = sb("iota_p", [P, MAX_TILES])
        iota_t = sb("iota_t", [1, TILES])
        before = sb("before", [P, P])
        ones = sb("ones", [P, P])
        home = sb("home", [P, NT, TOPK], I32)
        N = NT * E
        scratch = w3[:, 0:LATE].rearrange("p e r d -> p (e r d)")
        assert TILES * E + 5 * N <= LATE * NR * D
        tile_cmp = scratch[0:1, 0:TILES * E].rearrange("p (t e) -> p t e", e=E)
        at = TILES * E
        total, upto = (scratch[:, at + i * N:at + (i + 1) * N].rearrange("p (e t) -> p e t", e=E) for i in range(2))
        zero_row = scratch[:, at + 2 * N:at + 3 * N]
        tmp, rank = (scratch[:, at + i * N:at + (i + 1) * N].rearrange("p (t e) -> p t e", e=E) for i in (3, 4))
        xs = [sb(f"xs{i}", [P, D]) for i in range(2)]
        tiles = act_all[:].rearrange("p a n -> p (a n)").rearrange("p (a n) -> p a n", n=D)
        sil, hid, ys = ([tiles[:, 2 * n + i, :] for i in range(2)] for n in range(3))
        xsT, hidT = ([tiles[:, 2 * n + i, :].rearrange("p (c k) -> p c k", c=2) for i in range(2)] for n in (3, 4))
        count_e, pad_e, end_e = sb("count_e", [P, E]), sb("pad_e", [P, E]), sb("end_e", [P, E])
        shift_e = sb("shift_e", [P, E])
        slot_f = sb("slot_f", [P, NT, TOPK])
        slot = sb("slot", [P, NT, TOPK], I32)
        tile_f, tile_e = sb("tile_f", [1, TILES]), sb("tile_e", [1, TILES], I32)

        idx = [sb(f"idx{i}", [P, CHUNK_TILES, TOPK], I32) for i in range(2)]
        home_now = [sb(f"home_now{i}", [P, CHUNK_TILES, TOPK], I32) for i in range(2)]
        homes = sb("homes", [P, TILES], I32)
        tile_home = [sb(f"tile_home{i}", [P, 1], I32) for i in range(2)]
        EARLY = 2 * CHUNK_TILES * D // (KC * 2 * RH)
        rows = [w12[:, 0:EARLY].rearrange("p e c n -> p (e c n)").rearrange("p (i t d) -> p i t d", i=2, d=D)[:, i]
                for i in range(2)]

        bank = [ps(f"bank{i}") for i in range(8)]

        we_loaded = sem("we_loaded")
        iotas_done = sem("iotas_done")
        xT_loaded = [sem(f"xT_loaded{i}") for i in range(2)]
        steps = sem("steps")
        ranks_done, ranks_kept = sem("ranks_done"), sem("ranks_kept")
        slots_ready = sem("slots_ready")
        tiles_ready = sem("tiles_ready")
        s12_hi_ready, s12_ready = sem("s12_hi_ready"), sem("s12_ready")
        s3_hi_ready, s3_ready = sem("s3_hi_ready"), sem("s3_ready")
        xT_hi_ready, xT_ready = sem("xT_hi_ready"), sem("xT_ready")
        h_done, silu_ready, prod_ready = sem("h_done"), sem("silu_ready"), sem("prod_ready")
        act_hi_ready, act_ready = sem("act_hi_ready"), sem("act_ready")
        act_used, y_added = sem("act_used"), sem("y_added")
        rows_loaded = [sem(f"rows_loaded{i}") for i in range(2)]
        idx_ready = sem("idx_ready")
        homes_loaded, home_ready = sem("homes_loaded"), sem("home_ready")
        rows_placed = [sem(f"rows_placed{i}") for i in range(2)]
        xs_loaded = [sem(f"xs_loaded{i}") for i in range(2)]
        xs_turned, xsT_ready = sem("xs_turned"), sem("xsT_ready")
        up_done, sil_ready, hid_ready = sem("up_done"), sem("sil_ready"), sem("hid_ready")
        hid_turned, hidT_ready = sem("hid_turned"), sem("hidT_ready")
        down_done, ys_ready = sem("down_done"), sem("ys_ready")
        ys_stored = [sem(f"ys_stored{i}") for i in range(2)]
        got = [sem(f"got{i}") for i in range(2)]
        got_used = sem("got_used")
        out_stored = sem("out_stored")

        IOTAS = 6
        N_SCATTER = 2 * 16 * CHUNK_TILES * TOPK
        outs_in = [w12[:, i * TOPK * CHUNK_TILES // (2 * KC):(i + 1) * TOPK * CHUNK_TILES // (2 * KC)].rearrange(
            "p e c n -> p (e c n)").rearrange("p (k t d) -> p k t d", k=TOPK, t=CHUNK_TILES) for i in range(2)]

        def run_tiles(eng, first, last, step):
            turns = (last - first) // TILE_TURNS
            with eng.Fori(0, turns) as j:
                for i in range(TILE_TURNS):
                    step(j * TILE_TURNS + first + i, i % 2)
            for t in range(first + turns * TILE_TURNS, last):
                step(t, t % 2)

        def run_chunks(eng, step):
            step(0, 0)
            with eng.Fori(0, NCH // 2 - 1) as j:
                for i in range(2):
                    step(j * 2 + 1 + i, 1 - i)
            step(NCH - 1, 1)

        with nc.Block() as block:
            @block.sync
            def _(sp):
                for i in range(2):
                    sp.dma_start(xT[i][:], xn2T_cols[:, :, i * CH:(i + 1) * CH]).then_inc(xT_loaded[i], 16)
                for i in range(2):
                    sp.dma_start(rows[i], xn2_rows[:, i * CHUNK_TILES:(i + 1) * CHUNK_TILES, :]
                                 ).then_inc(rows_loaded[i], 16)

                def load_w12(experts):
                    for kc in range(KC):
                        for u, w in enumerate((rw1, rw2)):
                            sp.dma_start(w12[:, experts, kc, u * RH:(u + 1) * RH],
                                         w[experts, kc * P:(kc + 1) * P, :].rearrange("e p n -> p e n")
                                         ).then_inc(we_loaded, 16)

                def load_w3(experts):
                    for r in range(NR):
                        sp.dma_start(w3[:, experts, r, :],
                                     rw3[experts, r * P:(r + 1) * P, :].rearrange("e p n -> p e n")
                                     ).then_inc(we_loaded, 16)

                load_w12(slice(EARLY, E))
                sp.wait_ge(slots_ready, 1)
                sp.wait_ge(tiles_ready, 1)
                load_w3(slice(0, LATE))
                with sp.Fori(1, NCH // 2) as j:
                    for i in range(2):
                        sp.wait_ge(h_done, HT * (j * 2 + i - 1))
                        sp.dma_start(xT[i][:], xn2T_cols[:, :, bass.ds((j * 2 + i) * CH, CH)]
                                     ).then_inc(xT_loaded[i], 16)
                    for i in range(2):
                        sp.wait_ge(rows_placed[i], j * N_SCATTER)
                        sp.dma_start(rows[i], xn2_rows[:, bass.ds((j * 2 + i) * CHUNK_TILES, CHUNK_TILES), :]
                                     ).then_inc(rows_loaded[i], 16)
                for i in range(2):
                    sp.wait_ge(rows_placed[i], NCH // 2 * N_SCATTER)
                load_w12(slice(0, EARLY))

                def load_tile(t, i):
                    after(sp, xs_turned, t - 1)
                    sp.dma_start(xs[i][:], x_rows[bass.ds(t * P, P), :]).then_inc(xs_loaded[i], 16)

                load_tile(0, 0)
                load_tile(1, 1)
                sp.wait_ge(h_done, NCH * HT)
                load_w3(slice(LATE, E))
                sp.dma_start(homes[:], slot_home.rearrange("(t p) o -> p (t o)", p=P), allow_slow_non_contiguous=True
                             ).then_inc(homes_loaded, 16)
                run_tiles(sp, 2, TILES, load_tile)

                for i in range(2):
                    sp.wait_ge(ys_stored[i], 16 * (TILES // 2))

                def load_outputs(c, i):
                    for k in range(TOPK):
                        sp.dma_start(outs_in[i][:, k], y_rows[bass.ds(c * CH + k * T, CH), :].rearrange(
                            "(t p) d -> p t d", p=P)).then_inc(got[i], 16)

                def store_out(c):
                    sp.wait_ge(got_used, c + 1)
                    sp.dma_start(out_t[:, chunk_tiles(c), :], x_sb[:, chunk_tiles(c), :]).then_inc(out_stored, 16)

                load_outputs(0, 0)
                load_outputs(1, 1)
                with sp.Fori(0, NCH // 2 - 1) as j:
                    for i in range(2):
                        store_out(j * 2 + i)
                        load_outputs(j * 2 + 2 + i, i)
                store_out(NCH - 2)
                store_out(NCH - 1)
                sp.wait_ge(out_stored, 16 * NCH)

            @block.gpsimd
            def _(pool):
                g = nc.gpsimd
                count = [0]

                def const(ins):
                    ins.then_inc(iotas_done, 1)
                    count[0] += 1
                    pool.wait_ge(iotas_done, count[0])

                fl = dict(allow_small_or_imprecise_dtypes=True)
                const(g.iota(home[:], pattern=[[P, NT], [T, TOPK]], base=0, channel_multiplier=1))
                const(g.iota(iota_p[:], pattern=[[P, MAX_TILES]], base=0, channel_multiplier=0, **fl))
                const(g.iota(iota_t[:], pattern=[[1, TILES]], base=0, channel_multiplier=0, **fl))
                const(g.memset(ones[:], 1.0))
                const(g.memset(zero_row[:], 0.0))
                const(g.affine_select(out=before[:], in_=ones[:], compare_op=ALU.is_gt, fill=0.0, base=0,
                                      pattern=[[1, P]], channel_multiplier=-1))
                assert count[0] == IOTAS
                pool.wait_ge(slots_ready, 1)

                def place(c, i, j):
                    after(pool, rows_placed[i], j * N_SCATTER)
                    pool.sem_inc(pool_holds, 1)
                    g.tensor_copy(idx[i][:], slot[:, chunk_tiles(c), :]).then_inc(idx_ready, 1)
                    g.tensor_copy(home_now[i][:], home[:, chunk_tiles(c), :]).then_inc(idx_ready, 1)
                    pool.wait_ge(idx_ready, 2 * c + 2)
                    pool.wait_ge(rows_loaded[i], j * 16 + 16)
                    pool.sem_inc(pool_holds, 1)
                    for t in range(CHUNK_TILES):
                        for k in range(TOPK):
                            at_slot = bass.IndirectOffsetOnAxis(ap=idx[i][:, t, k:k + 1], axis=0)
                            pool.indirect_dma_start(out=x_rows, out_offset=at_slot, in_=rows[i][:, t, :],
                                                    in_offset=None).then_inc(rows_placed[i], 16)
                            pool.indirect_dma_start(out=slot_home, out_offset=at_slot, in_=home_now[i][:, t, k:k + 1],
                                                    in_offset=None).then_inc(rows_placed[i], 16)

                place(0, 0, 0)
                place(1, 1, 0)
                with pool.Fori(1, NCH // 2) as j:
                    for i in range(2):
                        place(j * 2 + i, i, j)

                def store_tile(t, i):
                    if not isinstance(t, int) or t >= 2:
                        pool.wait_ge(ys_stored[i], (t - i) * 8)
                        pool.sem_inc(pool_holds, 1)
                    g.tensor_copy(tile_home[i][:], homes[:, bass.ds(t, 1)]).then_inc(home_ready, 1)
                    pool.wait_ge(home_ready, t + 1)
                    pool.wait_ge(ys_ready, t + 1)
                    pool.sem_inc(pool_holds, 1)
                    pool.indirect_dma_start(
                        out=y_rows, out_offset=bass.IndirectOffsetOnAxis(ap=tile_home[i][:], axis=0),
                        in_=ys[i][:], in_offset=None).then_inc(ys_stored[i], 16)

                pool.wait_ge(homes_loaded, 16)
                store_tile(0, 0)
                store_tile(1, 1)
                run_tiles(pool, 2, TILES, store_tile)

            @block.scalar
            def _(act):
                s = nc.scalar
                act.wait_ge(ranks_done, 1)
                s.copy(rank[:], bank[4][:].rearrange("p (t e) -> p t e", e=E)).then_inc(ranks_kept, 1)
                s.copy(total[:], bank[5][:].rearrange("p (t e) -> p e t", e=E)).then_inc(ranks_kept, 1)

                def high_xT(c, i):
                    act.wait_ge(xT_loaded[i], (c - i) * 8 + 16)
                    s.copy(xT_hi[i][:], xT[i][:]).then_inc(xT_hi_ready, 1)

                def high_s12(m):
                    cols = slice(m * P, (m + 1) * P)
                    s.copy(s12_hi[:, :, :, cols], s12[:, :, :, cols]).then_inc(s12_hi_ready, 1)

                def shared(c, i):
                    for m in range(HT):
                        n = c * HT + m
                        if isinstance(c, int) and c == 0:
                            if m == 0:
                                high_s12(0)
                                high_xT(0, 0)
                                high_s12(1)
                            elif m < HT - 1:
                                high_s12(m + 1)
                            s.copy(s3_hi[:, m, :], s3[:, m, :]).then_inc(s3_hi_ready, 1)
                        act.wait_ge(h_done, n + 1)
                        after(act, act_used, n - 3)
                        s.activation(act_s[m % 4][:], bank[m % 2][:], ACT.Silu).then_inc(silu_ready, 1)
                        act.wait_ge(prod_ready, n + 1)
                        s.copy(act_hi[m % 4][:], act_s[m % 4][:]).then_inc(act_hi_ready, 1)
                        if m == 3 and not (isinstance(c, int) and c == NCH - 1):
                            high_xT(c + 1, 1 - i)

                run_chunks(act, shared)

                def turn_in(t, i):
                    act.wait_ge(xs_turned, t + 1)
                    after(act, up_done, t - 1)
                    s.copy(xsT[i][:], bank[i][:, 0:D].rearrange("p (c k) -> p c k", c=KC)).then_inc(xsT_ready, 1)

                def silu(t, i):
                    act.wait_ge(up_done, t + 1)
                    after(act, hid_ready, t - 1)
                    s.activation(sil[i][:], bank[2 + i][:, 0:RH], ACT.Silu).then_inc(sil_ready, 1)

                turn_in(0, 0)
                turn_in(1, 1)
                silu(0, 0)
                turn_in(2, 0)
                silu(1, 1)
                turn_in(3, 1)
                silu(2, 0)

                def tile_step(t, i):
                    turn_in(t, i)
                    silu(t - 1, 1 - i)

                run_tiles(act, 4, TILES, tile_step)
                silu(TILES - 1, 1)

            @block.vector
            def _(dve):
                v = nc.vector
                done = [0]

                def then(ins):
                    done[0] += 1
                    ins.then_inc(steps, 1)
                    dve.wait_ge(steps, done[0])

                def over_e(ap):
                    return ap.rearrange("p (o e) -> p o e", o=1).to_broadcast([P, NT, E])

                def count_tokens():
                    then(v.tensor_tensor_scan(upto[:].rearrange("p e t -> p (e t)"), total[:].rearrange("p e t -> p (e t)"),
                                              zero_row, 0.0, ALU.add, ALU.add))
                    then(v.tensor_copy(end_e[:], upto[:, :, NT - 1]))
                    then(v.tensor_copy(count_e[:, 0:1], end_e[:, 0:1]))
                    then(v.tensor_tensor(count_e[:, 1:E], end_e[:, 1:E], end_e[:, 0:E - 1], ALU.subtract))

                def count_tiles():
                    cmp = tmp[:].rearrange("p t e -> p (t e)").rearrange("p (e n) -> p e n", e=E)
                    then(v.tensor_tensor(cmp, count_e[:].rearrange("p (e o) -> p e o", o=1).to_broadcast([P, E, MAX_TILES]),
                                         iota_p[:].rearrange("p (o n) -> p o n", o=1).to_broadcast([P, E, MAX_TILES]),
                                         ALU.is_gt))
                    then(v.reduce_sum(pad_e[:], cmp, AX))
                    then(v.tensor_tensor(shift_e[:], count_e[:], end_e[:], ALU.subtract))
                    then(v.tensor_tensor_scan(end_e[:], pad_e[:], zero_row[:, 0:E], 0.0, ALU.add, ALU.add))
                    then(v.tensor_tensor(pad_e[:], end_e[:], pad_e[:], ALU.subtract))
                    then(v.scalar_tensor_tensor(shift_e[:], pad_e[:], float(P), shift_e[:], ALU.mult, ALU.add))

                def place_tokens():
                    then(v.tensor_tensor(upto[:], upto[:], total[:], ALU.subtract))
                    then(v.tensor_tensor(tmp[:], rank[:], upto[:].rearrange("p e t -> p t e"), ALU.add))
                    then(v.tensor_tensor(tmp[:], tmp[:], over_e(shift_e[:]), ALU.add))

                def pick_slots():
                    for k in range(TOPK):
                        then(v.tensor_tensor(total[:].rearrange("p e t -> p (e t)").rearrange("p (t e) -> p t e", e=E),
                                             hot[:, :, k, :], tmp[:], ALU.mult))
                        then(v.reduce_sum(slot_f[:, :, k], total[:].rearrange("p e t -> p (e t)").rearrange(
                            "p (t e) -> p t e", e=E), AX))
                    v.tensor_copy(slot[:], slot_f[:]).then_inc(slots_ready, 1)

                def tiles_experts():
                    then(v.tensor_tensor(tile_cmp[:], end_e[0:1, :].rearrange("p (o e) -> p o e", o=1).to_broadcast(
                        [1, TILES, E]), iota_t[:].rearrange("p (t o) -> p t o", o=1).to_broadcast([1, TILES, E]), ALU.is_le))
                    then(v.reduce_sum(tile_f[:], tile_cmp[:], AX))
                    v.tensor_scalar(tile_e[:], tile_f[:], float(E - 1), None, ALU.min).then_inc(tiles_ready, 1)

                dve.wait_ge(iotas_done, IOTAS)

                def low_xT(c, i):
                    dve.wait_ge(xT_hi_ready, c + 1)
                    v.tensor_tensor(xT_lo[i][:], xT[i][:], xT_hi[i][:].bitcast(F32), ALU.subtract).then_inc(xT_ready, 1)

                def shared(c, i):
                    first = isinstance(c, int) and c == 0
                    for m in range(HT):
                        n = c * HT + m
                        if first:
                            if m == 0:
                                low_s12(0)
                                low_xT(0, 0)
                                low_s12(1)
                            elif m < HT - 1:
                                low_s12(m + 1)
                            low_s3(m)
                        dve.wait_ge(silu_ready, n + 1)
                        v.tensor_tensor(act_s[m % 4][:], act_s[m % 4][:], bank[2 + m % 2][:], ALU.mult
                                        ).then_inc(prod_ready, 1)
                        dve.wait_ge(act_hi_ready, n + 1)
                        v.tensor_tensor(act_lo[m % 4][:], act_s[m % 4][:], act_hi[m % 4][:].bitcast(F32), ALU.subtract
                                        ).then_inc(act_ready, 1)
                        if m == 3 and not (isinstance(c, int) and c == NCH - 1):
                            low_xT(c + 1, 1 - i)
                        if m == 1 and not first:
                            add_outputs(c - 1)
                        if first:
                            if m == 0:
                                dve.wait_ge(ranks_kept, 2)
                                count_tokens()
                            elif m == 1:
                                count_tiles()
                            elif m == 2:
                                place_tokens()
                            elif m == 4:
                                pick_slots()
                            elif m == 5:
                                tiles_experts()

                def low_s12(m):
                    dve.wait_ge(s12_hi_ready, m + 1)
                    w = (slice(None), slice(None), slice(None), slice(m * P, (m + 1) * P))
                    v.tensor_tensor(s12_lo[w], s12[w], s12_hi[w].bitcast(F32), ALU.subtract).then_inc(s12_ready, 1)

                def low_s3(m):
                    dve.wait_ge(s3_hi_ready, m + 1)
                    v.tensor_tensor(s3_lo[:, m, :], s3[:, m, :], s3_hi[:, m, :].bitcast(F32), ALU.subtract
                                    ).then_inc(s3_ready, 1)

                def add_outputs(c):
                    dve.wait_ge(act_used, c * HT + HT)
                    for t in range(CHUNK_TILES):
                        row = x_sb[:, bass.ds(c * CHUNK_TILES + t, 1), :].rearrange("p o d -> p (o d)")
                        last = v.scalar_tensor_tensor(row, bank[4 + t][:, 0:D], tg[:, 1:2], row, ALU.mult, ALU.add)
                    last.then_inc(y_added, 1)

                run_chunks(dve, shared)
                add_outputs(NCH - 1)

                def hidden(t, i):
                    dve.wait_ge(sil_ready, t + 1)
                    after(dve, hid_turned, t - 1)
                    v.tensor_tensor(hid[i][:], sil[i][:], bank[2 + i][:, RH:2 * RH], ALU.mult).then_inc(hid_ready, 1)

                def turn_hidden(t, i):
                    dve.wait_ge(hid_turned, t + 1)
                    after(dve, down_done, t - 1)
                    v.tensor_copy(hidT[i][:], bank[4 + i][:, 0:RH].rearrange("p (c k) -> p c k", c=NR)
                                  ).then_inc(hidT_ready, 1)

                def outputs(t, i):
                    dve.wait_ge(down_done, t + 1)
                    if isinstance(t, int) and t < 2:
                        pass
                    else:
                        dve.wait_ge(ys_stored[i], (t - i) * 8)
                    v.tensor_copy(ys[i][:], bank[6 + i][:, 0:D]).then_inc(ys_ready, 1)

                hidden(0, 0)
                hidden(1, 1)
                turn_hidden(0, 0)
                hidden(2, 0)
                turn_hidden(1, 1)
                outputs(0, 0)
                hidden(3, 1)
                turn_hidden(2, 0)
                outputs(1, 1)

                def tile_step(t, i):
                    hidden(t + 2, i)
                    turn_hidden(t + 1, 1 - i)
                    outputs(t, i)

                run_tiles(dve, 2, TILES - 2, tile_step)
                turn_hidden(TILES - 1, 1)
                outputs(TILES - 2, 0)
                outputs(TILES - 1, 1)

                with dve.Fori(0, NCH // 2) as j:
                    for i in range(2):
                        c = j * 2 + i
                        dve.wait_ge(got[i], j * 16 * TOPK + 16 * TOPK)
                        for k in range(TOPK):
                            for t in range(CHUNK_TILES):
                                row = x_sb[:, bass.ds(c * CHUNK_TILES + t, 1), :].rearrange("p o d -> p (o d)")
                                last = v.scalar_tensor_tensor(
                                    row, outs_in[i][:, k, t, :],
                                    gate[:, bass.ds(c * CHUNK_TILES + t, 1), k], row, ALU.mult, ALU.add)
                            if k == 0:
                                last.then_inc(y_added, 1)
                                dve.wait_ge(y_added, NCH + c + 1)
                        last.then_inc(got_used, 1)

            @block.tensor
            def _(pe):
                mm, turn = nc.tensor.matmul, nc.tensor.transpose
                pe.wait_ge(iotas_done, IOTAS)
                mm(bank[4][:], before[:], hots[:].rearrange("p t e -> p (t e)"), start=True, stop=True)
                mm(bank[5][:], ones[:], hots[:].rearrange("p t e -> p (t e)"), start=True, stop=True
                   ).then_inc(ranks_done, 1)

                def three_passes(out_, lhs_hi, lhs_lo, rhs_hi, rhs_lo, start, stop):
                    mm(out_, lhs_hi, rhs_hi, start=start, stop=False)
                    mm(out_, lhs_hi, rhs_lo, start=False, stop=False)
                    return mm(out_, lhs_lo, rhs_hi, start=False, stop=stop)

                def shared(c, i):
                    first = isinstance(c, int) and c == 0
                    pe.wait_ge(xT_ready, c + 1)
                    for m in range(HT):
                        n = c * HT + m
                        if first:
                            pe.wait_ge(s12_ready, m + 1)
                        after(pe, prod_ready, n - 1)
                        cols = slice(m * P, (m + 1) * P)
                        for u in range(2):
                            for kc in range(KC):
                                last = three_passes(bank[2 * u + m % 2][:], s12_hi[:, kc, u, cols],
                                                    s12_lo[:, kc, u, cols], xT_hi[i][:, kc, :], xT_lo[i][:, kc, :],
                                                    kc == 0, kc == KC - 1)
                        last.then_inc(h_done, 1)
                        if m >= 2:
                            down_shared(c, m - 2)
                        elif not first:
                            down_shared(c - 1, HT - 2 + m)

                def down_shared(c, m):
                    pe.wait_ge(act_ready, c * HT + m + 1)
                    if isinstance(c, int) and c == 0:
                        pe.wait_ge(s3_ready, m + 1)
                        if m == 0:
                            pe.wait_ge(ranks_kept, 2)
                    elif m == 0:
                        pe.wait_ge(y_added, c)
                    for t in range(CHUNK_TILES):
                        rows_ = slice(t * P, (t + 1) * P)
                        last = three_passes(bank[4 + t][:, 0:D], act_hi[m % 4][:, rows_], act_lo[m % 4][:, rows_],
                                            s3_hi[:, m, :], s3_lo[:, m, :], m == 0, m == HT - 1)
                    last.then_inc(act_used, 1)

                run_chunks(pe, shared)
                down_shared(NCH - 1, HT - 2)
                down_shared(NCH - 1, HT - 1)

                pe.wait_ge(we_loaded, 16 * 2 * (2 * KC + NR))
                pe.wait_ge(tiles_ready, 1)

                def expert(t):
                    return pe.value_load(tile_e[0:1, bass.ds(t, 1)], min_val=0, max_val=E - 1)

                def turn_in(t, i):
                    pe.wait_ge(xs_loaded[i], (t - i) * 8 + 16)
                    after(pe, xsT_ready, t - 1)
                    for kc in range(KC):
                        last = turn(bank[i][:, kc * P:(kc + 1) * P], xs[i][:, kc * P:(kc + 1) * P], ident[:])
                    last.then_inc(xs_turned, 1)

                def up(t, i, e):
                    pe.wait_ge(xsT_ready, t + 1)
                    after(pe, hid_ready, t - 1)
                    for kc in range(KC):
                        last = mm(bank[2 + i][:], xsT[i][:, kc, :],
                                  w12[:, bass.ds(e, 1), kc, :].rearrange("p o n -> p (o n)"),
                                  start=kc == 0, stop=kc == KC - 1)
                    last.then_inc(up_done, 1)

                def turn_hidden(t, i):
                    pe.wait_ge(hid_ready, t + 1)
                    after(pe, hidT_ready, t - 1)
                    for r in range(NR):
                        last = turn(bank[4 + i][:, r * P:(r + 1) * P], hid[i][:, r * P:(r + 1) * P], ident[:])
                    last.then_inc(hid_turned, 1)

                def down(t, i, e):
                    pe.wait_ge(hidT_ready, t + 1)
                    after(pe, ys_ready, t - 1)
                    for r in range(NR):
                        last = mm(bank[6 + i][:, 0:D], hidT[i][:, r, :],
                                  w3[:, bass.ds(e, 1), r, :].rearrange("p o n -> p (o n)"),
                                  start=r == 0, stop=r == NR - 1)
                    last.then_inc(down_done, 1)

                pe.wait_ge(y_added, NCH)
                turn_in(0, 0)
                turn_in(1, 1)
                up(0, 0, expert(0))
                turn_in(2, 0)
                up(1, 1, expert(1))
                turn_hidden(0, 0)

                def tile_step(t, i):
                    turn_in(t + 3, 1 - i)
                    up(t + 2, i, expert(t + 2))
                    turn_hidden(t + 1, 1 - i)
                    down(t, i, expert(t))

                tile_step(0, 0)
                tile_step(1, 1)
                run_tiles(pe, 2, TILES - 4, tile_step)
                turn_in(TILES - 1, 1)
                up(TILES - 2, 0, expert(TILES - 2))
                turn_hidden(TILES - 3, 1)
                down(TILES - 4, 0, expert(TILES - 4))
                up(TILES - 1, 1, expert(TILES - 1))
                turn_hidden(TILES - 2, 0)
                down(TILES - 3, 1, expert(TILES - 3))
                turn_hidden(TILES - 1, 1)
                down(TILES - 2, 0, expert(TILES - 2))
                down(TILES - 1, 1, expert(TILES - 1))

    keep.close()


_INS = ["x", "ctx_1024", "g_xattn", "g_ffn", "L0_xattn_wq", "L0_xattn_bq", "L0_xattn_wk", "L0_xattn_bk",
        "L0_xattn_wv", "L0_xattn_bv", "L0_xattn_wo", "L0_xattn_bo", "L0_ffn_router_w", "L0_ffn_expert_bias",
        "L0_ffn_shared_w1", "L0_ffn_shared_w2", "L0_ffn_shared_w3", "L0_ffn_routed_w1", "L0_ffn_routed_w2",
        "L0_ffn_routed_w3"]


def kernel(**inputs):
    import numpy as _np
    import concourse.bacc as _bacc
    from concourse import mybir as _mybir
    from concourse.bass_utils import run_bass_kernel_spmd as _run

    nc = _bacc.Bacc("TRN2", target_bir_lowering=False, num_devices=1)
    arrays, args = {}, []
    for name in _INS:
        a = _np.ascontiguousarray(inputs[name])
        arrays[f"in_{name}_dram"] = a
        args.append(nc.dram_tensor(f"in_{name}_dram", a.shape, _mybir.dt.from_np(a.dtype), kind="ExternalInput").ap())
    shape = inputs["x"].shape
    args.append(nc.dram_tensor("out_dram", shape, _mybir.dt.float32, kind="ExternalOutput").ap())
    flamingo_block(nc, *args)
    return _run(nc, [arrays], core_ids=[0]).results[0]["out_dram"]
```

```python
from contextlib import ExitStack

import concourse.bass as bass
from concourse import mybir

F32 = mybir.dt.float32
F32R = mybir.dt.float32r
I32 = mybir.dt.int32
U32 = mybir.dt.uint32
ALU = mybir.AluOpType
ACT = mybir.ActivationFunctionType
AX = mybir.AxisListType.X

P = 128
QUAD = 32
CHUNK_TILES = 4
CH = CHUNK_TILES * P
EPS = 1e-5


PLACES = {
    "S1": (-1, -1, -1, -1), "A1": (-1,), "L1": (-1, -1, -1, -1), "N0": (2,), "N1": (4,), "Q0": (6,), "Q1": (9,),
    "C0": (-1,), "C1": (-1,), "W0": (1,), "W1": (2,),
    "S2": (4, 5, 6, 6), "A2": (6,), "L2": (9, 9, 9, 10), "X0": (10,), "XX": (12,), "RT": (16,),
    "RD": (16, 16, 17, 18, 18, 18, 18, 18, 18, 19, 19),
    "SA": (1, 1, 2, 2, 3, 3, 4, 4, 4, 5, 5, 5, 5, 6, 7, 7, 8, 9, 10, 10, 11, 11, 12, 12, 12, 13, 13, 14, 15,
            16, 17, 17),
    "PV": (7, 10, 18, 20), "PC": (7, 11, 18, 20), "OT": (11, 15, 20, 20), "MT": (20,),
}
EARLY, FRONT, BACK = ("S1", "A1", "L1", "N0", "N1", "Q0", "Q1"), ("SA", "MT"), ("OT", "PV", "PC")
PREV = ("C0", "C1", "W0", "W1", "S2", "A2", "L2", "X0", "XX", "RT", "RD")
RANKS = ("S1", "A1", "L1", "C0", "C1", "W0", "W1", "S2", "A2", "L2", "SA", "MT", "OT", "PV", "PC", "N0", "N1",
         "X0", "XX", "Q0", "Q1", "RT", "RD")


def step_events(early, front, back, prev):
    kinds = (EARLY if early else ()) + (FRONT if front else ()) + (BACK if back else ()) + (PREV if prev else ())
    order = []
    for n in range(-1, 21):
        if back and 0 <= n < 20:
            order.append(("ST", n))
        here = [(u, RANKS.index(kind), kind) for kind in kinds for u, place in enumerate(PLACES[kind]) if place == n]
        order += [(kind, u) for u, rank, kind in sorted(here, key=lambda e: (
            RANKS.index("PV") + 0.1 * e[0] + {"PV": 0, "PC": 0.04, "OT": 0.05}[e[2]]
            if e[2] in BACK else e[1], e[0]))]
    units = [e for e in order if e[0] in ("ST", "SA")]
    return order, {e: n % 4 for n, e in enumerate(units)}


def bank_holders(q, early, front, back, prev):
    def count(step, e):
        return (20 * step if e[0] == "ST" else 32 * (step + 1)) + e[1] + 1

    units = [e for e in step_events(early, front, back, prev)[0] if e[0] in ("ST", "SA")]
    if not back:
        before = [("K", 7), ("K", 8), ("V", 7), ("V", 8)]
    else:
        first = isinstance(q, int) and q == 0
        last4 = [e for e in step_events(True, True, not first, False)[0] if e[0] in ("ST", "SA")][-4:]
        before = [(e[0], count(q - 1, e)) for e in last4]
    held = before + [(e[0], count(q, e)) for e in units]
    return {e: held[n] for n, e in enumerate(units)}


def flamingo_block(nc, x, ctx_in, g_xattn, g_ffn, wq, bq, wk, bk, wv, bv, wo, bo,
                   router_w, expert_bias, sw1, sw2, sw3, rw1, rw2, rw3, out):
    B, SQ, D = x.shape
    SK = ctx_in.shape[1]
    H, _, HD = wq.shape
    KC = D // P
    PAIRS = H // 2
    HALF_PAIRS = PAIRS // 2
    KP = 160
    REM = SK - P
    T = B * SQ
    NT, NCH = T // P, T // CH
    GROUPS = H // 4
    ROWS = 3 * QUAD
    HALF = P // 2
    SCALE = float(HD) ** -0.5
    E, _, RH = rw1.shape
    SH = sw1.shape[2]
    HT = SH // P
    assert SQ == 2 * CH and D == 2 * P and P < SK <= P + QUAD and HD == 16 and H == 16

    x_t = x.rearrange("b (n p) d -> p (b n) d", p=P)
    out_t = out.rearrange("b (n p) d -> p (b n) d", p=P)

    keep = ExitStack()

    place = {}

    def sbuf(name, shape, dt=F32, stack=keep):
        tensor = stack.enter_context(nc.sbuf_tensor(name, shape, dt))
        size = 4
        for n in shape[1:]:
            size *= n
        place[name] = nc.sbuf_base - (size + 31) // 32 * 32
        return tensor

    def over(host, at, name, shape, dt=F32):
        return nc.alloc_sbuf_tensor_at(name, shape, dt, offset=place[host] + 4 * at)

    def sem(name):
        return keep.enter_context(nc.semaphore(name))

    TOPK = 2
    TILES = (TOPK * T - E) // P + E
    TILES += TILES % 2
    assert TILES % NCH == 0
    slots_x = nc.dram_tensor("slots_x", [TILES * P, D], F32, kind="Internal").ap()
    slot_home = nc.dram_tensor("slot_home", [TILES * P, 1], I32, kind="Internal").ap()

    def after(eng, semaphore, value):
        if not isinstance(value, int) or value > 0:
            eng.wait_ge(semaphore, value)

    def chunk_tiles(q):
        return bass.ds(q * CHUNK_TILES, CHUNK_TILES)

    dve_holds, pool_holds, sp_holds = sem("dve_holds"), sem("pool_holds"), sem("sp_holds")

    x_sb = sbuf("x_sb", [P, NT, D])
    xn2_rows = nc.dram_tensor("xn2_rows", [P, NT, D], F32, kind="Internal").ap()
    stacks = nc.dram_tensor("stacks", [PAIRS, ROWS, B, 2 * KP], F32, kind="Internal").ap()
    xn2T_cols = nc.dram_tensor("xn2T_cols", [P, KC, T], F32, kind="Internal").ap()
    hot = sbuf("hot", [P, NT, TOPK, E])
    hots = sbuf("hots", [P, NT, E])
    gate = sbuf("gate", [P, NT, TOPK])
    shared_w_loaded = sem("shared_w_loaded")
    ident = sbuf("ident", [P, P])
    gates = sbuf("gates", [P, 2])
    tg = sbuf("tg", [P, 2])
    shared_w = sbuf("shared_w", [P, KC * 2 * SH + HT * D])
    s12 = shared_w[:, 0:KC * 2 * SH].rearrange("p (c u n) -> p c u n", c=KC, u=2)
    s3 = shared_w[:, KC * 2 * SH:].rearrange("p (m d) -> p m d", m=HT)

    with ExitStack() as st:
        def sb(name, shape, dt=F32):
            return sbuf(name, shape, dt, st)

        def ps(name):
            return st.enter_context(nc.psum_tensor(name, [P, CH], F32))

        q_st = [sb(f"q_st{i}", [ROWS + 2, PAIRS, CH], F32R) for i in range(2)]
        s12_hi = over("q_st0", 0, "s12_hi", [P, KC, 2, SH], F32R)
        s3_hi = over("q_st1", 0, "s3_hi", [P, HT, D], F32R)
        s12_lo = over("shared_w", 0, "s12_lo", [P, KC, 2, SH], F32R)
        s3_lo = over("shared_w", KC * 2 * SH, "s3_lo", [P, HT, D], F32R)
        assert place["q_st1"] == place["q_st0"] + 4 * KC * 2 * SH
        wq_sb, wk_sb, wv_sb = (sb(n, [P, KC, H, HD]) for n in ("wq_sb", "wk_sb", "wv_sb"))
        wo_sb = sb("wo_sb", [P, KC, D])
        rw_sb = sb("rw_sb", [P, KC, E])
        bq_sb, bk_sb = sb("bq_sb", [P, 2]), sb("bk_sb", [P, 2])
        bv_sb, bo_sb = sb("bv_sb", [P, D]), sb("bo_sb", [P, D])
        oT = sb("oT", [P, CH])
        ctxT = sb("ctxT", [P, KC, B, SK])
        probs = sb("probs", [P, 2, 5, CH])
        kf = probs[:].rearrange("p g i n -> p (g i n)")[:, 0:2 * B * KP].rearrange("p (c b k) -> p c b k", c=2, b=B)
        ctx_sb = probs[:].rearrange("p g i n -> p (g i n)")[:, 2 * B * KP:2 * B * KP + 2 * B * D].rearrange(
            "p (r b d) -> p r b d", r=2, b=B)
        kh, kl = (over("shared_w", n * 4 * B * KP, f"k{n}", [P, 2, B, KP * 2], F32R) for n in range(2))
        v_all = sb("v_all", [P, 2, B, H, HD + 1])
        k_max = sb("k_max", [ROWS, PAIRS, 2 * KP], F32R)
        k_st = sb("k_st", [ROWS + 2, PAIRS, 3 * HALF + 2 * P], F32R)
        head_mask, mask_sum = sb("head_mask", [P, 2]), sb("mask_sum", [P, 8])
        ones_rows = sb("ones_rows", [2, 3 * HALF + 2 * P])
        v_main = sb("v_main", [P, H, QUAD])
        v_rem = sb("v_rem", [P, GROUPS, P])
        stats, mv = sb("stats", [P, 4, 6]), sb("mv", [P, 4, 2])
        ve, rstd = sb("ve", [P, 4]), sb("rstd", [P, 4])
        minus_half = sb("minus_half", [P, 4])
        stats2, mv2 = sb("stats2", [P, 4, 6]), sb("mv2", [P, 4, 2])
        ve2, rstd2 = sb("ve2", [P, 4]), sb("rstd2", [P, 4])
        xn = sb("xn", [P, 4, D])
        xnT = sb("xnT", [P, KC, CH])
        qh, ql = sb("qh", [P, 2, CH], F32R), sb("ql", [P, 2, CH], F32R)
        mx = sb("mx", [P, 4, 2, PAIRS])
        mT = sb("mT", [H, CH], F32R)
        rden = sb("rden", [P, 4, 4])
        ctxn = sb("ctxn", [P, 4, D])
        ctxnT = sb("ctxnT", [P, KC, CH])
        xn2c = sb("xn2c", [P, 4, D])
        xn2T = sb("xn2T", [P, KC, CH])

        zeros = sb("zeros", [P, D])
        no_home = sb("no_home", [P, TILES], I32)
        bias_sb, iota_e = sb("bias_sb", [P, E]), sb("iota_e", [P, E])
        exp_neg, score, sel = (sb(n, [P, 4, E]) for n in ("exp_neg", "score", "sel"))
        best, best_at = sb("best", [P, 4, 8]), sb("best_at", [P, 4, 8], U32)
        best_f = sb("best_f", [P, 4, TOPK])
        gated = sb("gated", [P, 4, TOPK, E])

        T0, T1, M, PV = ps("T0"), ps("T1"), ps("M"), ps("PV")
        S = [ps(f"S{i}") for i in range(4)]

        consts_done = sem("consts_done")
        wk_loaded, weights_loaded = sem("wk_loaded"), sem("weights_loaded")
        ones_loaded = sem("ones_loaded")
        slots_cleared = sem("slots_cleared")
        gates_loaded, tg_ready = sem("gates_loaded"), sem("tg_ready")
        ctx_loaded = sem("ctx_loaded")
        ctxT_done, ctxT_ready = sem("ctxT_done"), sem("ctxT_ready")
        kT_done, kf_ready = sem("kT_done"), sem("kf_ready")
        kh_ready, kl_ready = sem("kh_ready"), sem("kl_ready")
        kmax_loaded, kst_loaded = sem("kmax_loaded"), sem("kst_loaded")
        v_done, v_kept, v_loaded = sem("v_done"), sem("v_kept"), sem("v_loaded")
        x_loaded, x_rest_loaded = sem("x_loaded"), sem("x_rest_loaded")
        ln_step, rstd_ready, xn_ready = sem("ln_step"), sem("rstd_ready"), sem("xn_ready")
        xn_transposed, xnT_ready = sem("xn_transposed"), sem("xnT_ready")
        q_done = sem("q_done")
        qh_ready, ql_ready = sem("qh_ready"), sem("ql_ready")
        q_loaded = [[sem(f"q_loaded{i}_{c}") for c in range(2)] for i in range(2)]
        m_loaded = [sem(f"m_loaded{i}") for i in range(2)]
        sa_done, sa_read, st_done = sem("sa_done"), sem("sa_read"), sem("st_done")
        mT_done, mT_ready = sem("mT_done"), sem("mT_ready")
        probs_ready, pv_done = sem("probs_ready"), sem("pv_done")
        oT_ready, o_done = sem("oT_ready"), sem("o_done")
        rden_ready, ctxn_ready = sem("rden_ready"), sem("ctxn_ready")
        ctxn_transposed, ctxnT_ready = sem("ctxn_transposed"), sem("ctxnT_ready")
        wo_done, att_ready = sem("wo_done"), sem("att_ready")
        bo_ready, x_biased = sem("bo_ready"), sem("x_biased")
        ln2_step, rstd2_ready, xn2_ready = sem("ln2_step"), sem("rstd2_ready"), sem("xn2_ready")
        xn2_stored, xn2T_stored = sem("xn2_stored"), sem("xn2T_stored")
        xn2_transposed, xn2T_ready = sem("xn2_transposed"), sem("xn2T_ready")
        lg_done = sem("lg_done")
        logits_read, route, bias_loaded = sem("logits_read"), sem("route"), sem("bias_loaded")
        kf_padded, k_stacked = sem("kf_padded"), sem("k_stacked")
        mask_step = sem("mask_step")
        s12_hi_ready, s3_hi_ready = sem("s12_hi_ready"), sem("s3_hi_ready")

        N_QDMA = 16 * 3 * HALF_PAIRS
        N_VDMA = 16 * 5
        N_WEIGHTS = 16 * (2 * KC + 1 + 2 + 2)

        IDENT, CONSTS = 2, 13
        ROUTE = 11

        def run_steps(eng, step):
            step(eng, -2, -1, 0, True, False, False, False)
            step(eng, -1, -1, 1, True, True, False, False)
            step(eng, 0, 0, 0, True, True, True, False)
            step(eng, 1, 0, 1, True, True, True, True)
            with eng.Fori(0, B - 2) as b:
                step(eng, b * 2 + 2, b + 1, 0, True, True, True, True)
                step(eng, b * 2 + 3, b + 1, 1, True, True, True, True)
            step(eng, NCH - 2, B - 1, 0, False, True, True, True)
            step(eng, NCH - 1, B - 1, 1, False, False, True, True)
            step(eng, NCH, B, 0, False, False, False, True)

        def max_unit(u):
            return u % 16 // HALF_PAIRS, u // 16 * HALF_PAIRS + u % HALF_PAIRS

        def raw(ap):
            return ap.bitcast(F32)

        with nc.Block() as block:
            @block.sync
            def _(sp):

                sp.dma_start(ctx_sb[:, 0], ctx_in[:, 0:P, :].rearrange("b p d -> p b d")).then_inc(ctx_loaded, 16)
                sp.dma_start(ctx_sb[0:REM, 1], ctx_in[:, P:SK, :].rearrange("b p d -> p b d")).then_inc(ctx_loaded, 16)
                def load_projection(w_sb, w, done):
                    for kc in range(KC):
                        sp.dma_start(w_sb[:, kc], w[:, kc * P:(kc + 1) * P, :].rearrange("h p d -> p h d")
                                     ).then_inc(done, 16)

                load_projection(wk_sb, wk, wk_loaded)
                sp.dma_start(bk_sb[:], bk.rearrange("(c h) d -> (h d) c", c=2), allow_slow_non_contiguous=True
                             ).then_inc(wk_loaded, 16)
                sp.dma_start(x_sb[:, 0:2 * CHUNK_TILES, :], x_t[:, 0:2 * CHUNK_TILES, :]).then_inc(x_loaded, 16)
                load_projection(wq_sb, wq, weights_loaded)
                load_projection(wv_sb, wv, weights_loaded)
                sp.dma_start(bq_sb[:], bq.rearrange("(c h) d -> (h d) c", c=2), allow_slow_non_contiguous=True
                             ).then_inc(weights_loaded, 16)
                sp.dma_start(bv_sb[:], bv.rearrange("h d -> (h d)").partition_broadcast(P)).then_inc(weights_loaded, 16)
                sp.dma_start(bo_sb[:], bo.partition_broadcast(P)).then_inc(weights_loaded, 16)
                sp.dma_start(wo_sb[:], wo.rearrange("(c p) n -> p c n", p=P)).then_inc(weights_loaded, 16)
                sp.dma_start(rw_sb[:], router_w.rearrange("(c p) n -> p c n", p=P)).then_inc(weights_loaded, 16)
                sp.dma_start(bias_sb[:], expert_bias.partition_broadcast(P)).then_inc(bias_loaded, 16)
                sp.dma_start(gates[:, 0:1], g_xattn.partition_broadcast(P)).then_inc(gates_loaded, 16)
                sp.dma_start(gates[:, 1:2], g_ffn.partition_broadcast(P)).then_inc(gates_loaded, 16)
                sp.wait_ge(consts_done, CONSTS)
                sp.dma_start(raw(k_st[ROWS:ROWS + 2, :, :]), ones_rows[:].rearrange("r (o n) -> r o n", o=1)
                             .to_broadcast([2, PAIRS, 3 * HALF + 2 * P])).then_inc(ones_loaded, 16)
                sp.wait_ge(kh_ready, 1)
                sp.wait_ge(kl_ready, 1)
                for part, src in enumerate((kh, kl, kh)):
                    for j in range(HALF_PAIRS):
                        sp.dma_start(
                            stacks[j::HALF_PAIRS, QUAD * part:QUAD * (part + 1)].rearrange("c r b n -> r c (b n)"),
                            raw(src[QUAD * j:QUAD * (j + 1)]).rearrange("r c b n -> r c (b n)")).then_inc(k_stacked, 16)
                sp.wait_ge(k_stacked, 16 * 3 * HALF_PAIRS)


                def place_queries(n, k, c, back):
                    if back:
                        sp.wait_ge(st_done, 20 * n - 10 * (1 - c))
                        sp.sem_inc(sp_holds, 1)
                    sp.wait_ge(ql_ready, 2 * n + 3 + c)
                    for part, src in enumerate((qh, qh, ql)):
                        for j in range(HALF_PAIRS):
                            sp.dma_start(raw(q_st[k][QUAD * part:QUAD * (part + 1), c * HALF_PAIRS + j, :]),
                                         raw(src[QUAD * j:QUAD * (j + 1), c, :])).then_inc(q_loaded[k][c], 16)

                def step(sp, q, b, k, early, front, back, prev):
                    n, r = q + 1, q - 1
                    if prev:
                        sp.wait_ge(xn2_ready, q)
                        sp.dma_start(xn2_rows[:, chunk_tiles(r), :], xn2c[:]).then_inc(xn2_stored, 16)
                    if early:
                        place_queries(n, k, 0, back)
                    if prev:
                        sp.wait_ge(xn2T_ready, 2 * q)
                        sp.dma_start(xn2T_cols[:, :, bass.ds(r * CH, CH)], xn2T[:]).then_inc(xn2T_stored, 16)
                    if front and k:
                        if back:
                            sp.wait_ge(st_done, 20 * n)
                        for cols, keys in ((slice(HALF, 2 * HALF), slice(2 * P, 2 * KP)),
                                           (slice(3 * HALF, 3 * HALF + 2 * P), slice(0, 2 * P))):
                            sp.dma_start(raw(k_st[0:ROWS, :, cols]),
                                         stacks[:, :, bass.ds(b + 1, 1), keys].rearrange("p r o n -> r p (o n)")
                                         ).then_inc(kst_loaded, 16)
                    if front:
                        sp.wait_ge(mT_ready, n + 1)
                        for i in range(2):
                            sp.dma_start(raw(q_st[1 - k][ROWS + i:ROWS + i + 1, :, :]),
                                         raw(mT[PAIRS * i:PAIRS * (i + 1), :])).then_inc(m_loaded[1 - k], 16)
                    if early and not k:
                        if front:
                            sp.wait_ge(sa_done, 32 * (n + 1))
                        sp.dma_start(raw(k_max[:]), stacks[:, :, bass.ds(b + 1, 1), :].rearrange("p r o n -> r p (o n)")
                                     ).then_inc(kmax_loaded, 16)
                    if early:
                        place_queries(n, k, 1, back)
                    if front and k:
                        if back:
                            sp.wait_ge(pv_done, 4 * n)
                        else:
                            sp.wait_ge(v_kept, 2 * B)
                        sp.dma_start(v_main[:, :, 0:HD + 1],
                                     v_all[:, 0, bass.ds(b + 1, 1)].rearrange("p o h d -> p (o h) d")
                                     ).then_inc(v_loaded, 16)
                        for j in range(4):
                            at = HALF * (j // 2) + j % 2
                            sp.dma_start(v_rem[at:at + 2 * REM - 1:2, :, QUAD * j:QUAD * j + HD + 1],
                                         v_all[0:REM, 1, bass.ds(b + 1, 1), j::4].rearrange("p o g d -> p (o g) d")
                                         ).then_inc(v_loaded, 16)
                    if isinstance(q, int) and q == -2:
                        for pair in range(1, B):
                            sp.dma_start(x_sb[:, 2 * pair * CHUNK_TILES:2 * (pair + 1) * CHUNK_TILES, :],
                                         x_t[:, 2 * pair * CHUNK_TILES:2 * (pair + 1) * CHUNK_TILES, :]
                                         ).then_inc(x_rest_loaded, 16)
                    if isinstance(q, int) and q == 0:
                        for u, w in enumerate((sw1, sw2)):
                            sp.dma_start(s12[:, :, u, :], w[0].rearrange("(c p) n -> p c n", p=P)
                                         ).then_inc(shared_w_loaded, 16)
                        sp.dma_start(s3, sw3[0].rearrange("(c p) n -> p c n", p=P)).then_inc(shared_w_loaded, 16)
                        sp.dma_start(slot_home.rearrange("(p t) o -> p (t o)", p=P), no_home[:]
                                     ).then_inc(slots_cleared, 16)
                    if back:
                        part = bass.ds(q * (TILES // NCH), TILES // NCH)
                        sp.dma_start(slots_x.rearrange("(t p) d -> p t d", p=P)[:, part, :],
                                     zeros[:].rearrange("p (o d) -> p o d", o=1).to_broadcast([P, TILES // NCH, D])
                                     ).then_inc(slots_cleared, 16)

                run_steps(sp, step)
                sp.wait_ge(shared_w_loaded, 48)
                sp.wait_ge(xn2_stored, 16 * NCH)
                sp.wait_ge(xn2T_stored, 16 * NCH)
                sp.wait_ge(slots_cleared, 16 * (NCH + 1))

            @block.gpsimd
            def _(pool):
                g = nc.gpsimd
                count = [0]

                def const(ins):
                    ins.then_inc(consts_done, 1)
                    count[0] += 1
                    pool.wait_ge(consts_done, count[0])

                def select(ap, pattern, base, mult):
                    const(g.affine_select(out=ap, in_=ap, compare_op=ALU.not_equal, fill=1.0, base=base,
                                          pattern=pattern, channel_multiplier=mult))

                const(g.memset(ident[:], 0.0))
                select(ident[:], [[-1, P]], 0, 1)
                assert count[0] == IDENT
                const(g.memset(zeros[:], 0.0))
                const(g.memset(ones_rows[:], 0.0))
                const(g.memset(minus_half[:], -0.5))
                const(g.iota(no_home[:], pattern=[[1, TILES]], base=TOPK * T, channel_multiplier=TILES))
                const(g.iota(iota_e[:], pattern=[[1, E]], base=0, channel_multiplier=0,
                             allow_small_or_imprecise_dtypes=True))
                const(g.memset(v_main[:], 0.0))
                const(g.memset(v_rem[:], 0.0))
                const(g.memset(k_st[:].bitcast(F32), 0.0))
                for c0, c1 in ((HALF, 2 * HALF), (3 * HALF, 3 * HALF + 2 * P)):
                    select(ones_rows[:, c0:c1].rearrange("r (n i) -> r n i", i=2), [[0, (c1 - c0) // 2], [-1, 2]], 0, 1)
                const(g.memset(v_all[:, :, :, :, HD:HD + 1], 1.0))
                assert count[0] == CONSTS

                def step(pool, q, b, k, early, front, back, prev):
                    e = q + 2
                    if early:
                        pool.wait_ge(ln_step, 3 * e + 3)
                        after(pool, xn_ready, e)
                        g.tensor_tensor(rstd[:], ve[:], minus_half[:], ALU.pow).then_inc(rstd_ready, 1)
                    if isinstance(q, int) and q == -2:
                        pool.wait_ge(kf_ready, 2 * B)
                        g.tensor_copy(kf[:, :, :, SK:KP], kf[:, :, :, SK - 1:SK].to_broadcast([P, 2, B, KP - SK])
                                      ).then_inc(kf_padded, 1)
                    if prev:
                        pool.wait_ge(ln2_step, 3 * q)
                        g.tensor_tensor(rstd2[:], ve2[:], minus_half[:], ALU.pow).then_inc(rstd2_ready, 1)

                    if back:
                        if isinstance(q, int) and q == 0:
                            pool.wait_ge(bo_ready, 1)
                        pool.wait_ge(xn_ready, q + 1)
                        pool.sem_inc(pool_holds, 1)
                        g.tensor_tensor(x_sb[:, chunk_tiles(q), :], x_sb[:, chunk_tiles(q), :],
                                        bo_sb[:].rearrange("p (o d) -> p o d", o=1).to_broadcast([P, 4, D]), ALU.add
                                        ).then_inc(x_biased, 1)

                run_steps(pool, step)

            @block.scalar
            def _(act):
                s = nc.scalar
                for b in range(B):
                    act.wait_ge(ctxT_done, b + 1)
                    s.copy(ctxT[:, :, b, :], (T0, T1)[b % 2][:, 0:2 * SK].rearrange("p (c k) -> p c k", c=2)
                           ).then_inc(ctxT_ready, 1)
                act.wait_ge(wk_loaded, 16 * (KC + 1))
                for b in range(B):
                    for c in range(2):
                        act.wait_ge(kT_done, 2 * b + c + 1)
                        s.activation(kf[:, c, b, 0:SK], S[c][:, 0:SK], ACT.Identity, bias=bk_sb[:, c:c + 1]
                                     ).then_inc(kf_ready, 1)

                act.wait_ge(gates_loaded, 32)
                s.activation(tg[:], gates[:], ACT.Tanh).then_inc(tg_ready, 1)
                act.wait_ge(weights_loaded, N_WEIGHTS)

                def high_weights():
                    act.wait_ge(shared_w_loaded, 48)
                    act.wait_ge(st_done, 20 * NCH)
                    for m in range(0, HT, 2):
                        cols = slice(m * P, (m + 2) * P)
                        s.copy(s12_hi[:, :, :, cols], s12[:, :, :, cols]).then_inc(s12_hi_ready, 1)
                    for m in range(0, HT, 4):
                        s.copy(s3_hi[:, m:m + 4, :], s3[:, m:m + 4, :]).then_inc(s3_hi_ready, 1)

                def step(act, q, b, k, early, front, back, prev):
                    n, e, r = q + 1, q + 2, q - 1
                    events, banks = step_events(early, front, back, prev)
                    for kind, u in events:
                        if kind == "X0" and isinstance(q, int) and q == NCH:
                            high_weights()
                        if kind in ("C0", "C1"):
                            c = int(kind[1])
                            act.wait_ge(ctxn_transposed, 2 * r + c + 1)
                            after(act, wo_done, 2 * r)
                            s.copy(ctxnT[:, c, :], (T0, T1)[c][:]).then_inc(ctxnT_ready, 1)
                        if kind in ("X0", "XX"):
                            c = int(kind == "XX")
                            act.wait_ge(xn2_transposed, 2 * r + c + 1)
                            after(act, lg_done, r)
                            after(act, xn2T_stored, 16 * r)
                            s.copy(xn2T[:, c, :], T0[:]).then_inc(xn2T_ready, 1)
                        if kind == "RT":
                            act.wait_ge(lg_done, q)
                            after(act, route, ROUTE * r)
                            s.activation(exp_neg[:], M[:, 0:4 * E].rearrange("p (t e) -> p t e", t=4), ACT.Exp,
                                         scale=-1.0).then_inc(logits_read, 1)
                        if kind in ("N0", "N1"):
                            c = int(kind[1])
                            act.wait_ge(xn_transposed, 2 * e + c + 1)
                            after(act, q_done, 2 * e)
                            s.copy(xnT[:, c, :], T0[:]).then_inc(xnT_ready, 1)
                        if kind in ("Q0", "Q1"):
                            c = int(kind[1])
                            act.wait_ge(q_done, 2 * e + c + 1)
                            if front:
                                act.wait_ge(q_loaded[1 - k][c], N_QDMA * (b + 1 + k))
                            s.activation(qh[:, c, :], M[:], ACT.Identity, bias=bq_sb[:, c:c + 1]).then_inc(qh_ready, 1)
                        if kind == "ST":
                            g, i = u // 5, u % 5
                            act.wait_ge(st_done, 20 * q + u + 1)
                            after(act, pv_done, 4 * q + g - 1)
                            s.activation(probs[:, g % 2, i, :], S[banks[kind, u]][:], ACT.Exp,
                                         scale=SCALE).then_inc(probs_ready, 1)
                        if kind == "MT":
                            act.wait_ge(mT_done, n + 1)
                            if back:
                                act.wait_ge(m_loaded[k], 32 * (b + 1))
                            s.activation(mT[:], T0[0:H, :], ACT.Copy, scale=-1.0).then_inc(mT_ready, 1)
                        if kind == "PC":
                            act.wait_ge(pv_done, 4 * q + u + 1)
                            after(act, o_done, 4 * q + u)
                            s.copy(oT[:], PV[:]).then_inc(oT_ready, 1)

                run_steps(act, step)

            @block.vector
            def _(dve):
                v = nc.vector
                dve.wait_ge(consts_done, IDENT)
                v.reduce_sum(mask_sum[:], ident[:].rearrange("p (n d) -> p n d", d=HD), AX).then_inc(mask_step, 1)
                dve.wait_ge(mask_step, 1)
                v.reduce_sum(head_mask[:], mask_sum[:].rearrange("p (j i) -> p i j", i=2), AX).then_inc(mask_step, 1)
                dve.wait_ge(mask_step, 2)
                def split_keys():
                    dve.wait_ge(kf_padded, 1)
                    by_head = [t[:].rearrange("p c b (k i) -> p (c b) k i", i=2) for t in (kh, kl)]
                    kf_rows = kf.rearrange("p c b k -> p (c b) k")
                    for i in range(2):
                        last = v.tensor_scalar(by_head[0][:, :, :, i], kf_rows, head_mask[:, i:i + 1], None, ALU.mult)
                    last.then_inc(kh_ready, 1)
                    dve.wait_ge(kh_ready, 1)
                    for i in range(2):
                        last = v.scalar_tensor_tensor(by_head[1][:, :, :, i], kf_rows, head_mask[:, i:i + 1],
                                                      by_head[0][:, :, :, i].bitcast(F32), ALU.mult, ALU.subtract)
                    last.then_inc(kl_ready, 1)

                def keep_values():
                    for b in range(B):
                        for r, rows in ((0, P), (1, REM)):
                            dve.wait_ge(v_done, 2 * b + r + 1)
                            if b == 0 and r == 0:
                                dve.wait_ge(weights_loaded, N_WEIGHTS)
                            v.tensor_tensor(v_all[0:rows, r, b, :, 0:HD],
                                            S[2 + r][0:rows, 0:D].rearrange("p (h d) -> p h d", d=HD),
                                            bv_sb[0:rows, :].rearrange("p (h d) -> p h d", d=HD), ALU.add
                                            ).then_inc(v_kept, 1)

                def row(q, t):
                    return x_sb[:, bass.ds(q * CHUNK_TILES + t, 1), :].rearrange("p o d -> p (o d)")

                def moments(q, st_, mv_, ve_, step_sem, ve_read):
                    dve.wait_ge(step_sem, 3 * q + 1)
                    dve.sem_inc(dve_holds, 1)
                    for t in range(CHUNK_TILES):
                        last = v.bn_aggr(mv_[:, t, :], st_[:, t, :])
                    last.then_inc(step_sem, 1)
                    dve.wait_ge(step_sem, 3 * q + 2)
                    after(dve, ve_read, q)
                    v.tensor_scalar(ve_[:], mv_[:, :, 1], EPS, None, ALU.add).then_inc(step_sem, 1)

                def route_step(r, u):
                    t = chunk_tiles(r)
                    if u == 0:
                        dve.wait_ge(logits_read, r + 1)
                        last = v.tensor_scalar(score[:], exp_neg[:], 1.0, None, ALU.add)
                    else:
                        dve.wait_ge(route, r * ROUTE + u)
                        dve.sem_inc(dve_holds, 1)
                    if u == 1:
                        last = v.reciprocal(score[:], score[:])
                    if u == 2:
                        last = v.tensor_tensor(sel[:], score[:], bias_sb[:].rearrange(
                            "p (o e) -> p o e", o=1).to_broadcast([P, 4, E]), ALU.add)
                    if u == 3:
                        for i in range(CHUNK_TILES):
                            last = v.max(best[:, i, :], sel[:, i, :])
                    if u == 4:
                        for i in range(CHUNK_TILES):
                            last = v.max_index(best_at[:, i, :], best[:, i, :], sel[:, i, :])
                    if u == 5:
                        last = v.tensor_copy(best_f[:], best_at[:, :, 0:TOPK])
                    if u == 6:
                        last = v.tensor_tensor(
                            hot[:, t], iota_e[:].rearrange("p (o u e) -> p o u e", o=1, u=1).to_broadcast(
                                [P, 4, TOPK, E]),
                            best_f[:].rearrange("p t (k o) -> p t k o", o=1).to_broadcast([P, 4, TOPK, E]), ALU.is_equal)
                    if u == 7:
                        last = v.tensor_tensor(hots[:, t, :], hot[:, t, 0, :], hot[:, t, 1, :], ALU.add)
                    if u == 8:
                        last = v.tensor_tensor(gated[:], hot[:, t], score[:].rearrange(
                            "p t (o e) -> p t o e", o=1).to_broadcast([P, 4, TOPK, E]), ALU.mult)
                    if u == 9:
                        last = v.reduce_sum(gate[:, t, :], gated[:], AX)
                    if u == 10:
                        last = v.tensor_scalar(gate[:, t, :], gate[:, t, :], tg[:, 1:2], None, ALU.mult)
                    last.then_inc(route, 1)

                def low_weights(m):
                    dve.wait_ge(s12_hi_ready, m // 2 + 1)
                    w = (slice(None), slice(None), slice(None), slice(m * P, (m + 2) * P))
                    v.tensor_tensor(s12_lo[w], s12[w], s12_hi[w].bitcast(F32), ALU.subtract)
                    if m % 4 == 2:
                        dve.wait_ge(s3_hi_ready, m // 4 + 1)
                        v.tensor_tensor(s3_lo[:, m - 2:m + 2, :], s3[:, m - 2:m + 2, :],
                                        s3_hi[:, m - 2:m + 2, :].bitcast(F32), ALU.subtract)

                def step(dve, q, b, k, early, front, back, prev):
                    n, e, r = q + 1, q + 2, q - 1
                    events, banks = step_events(early, front, back, prev)
                    if isinstance(q, int) and q == -1:
                        keep_values()
                        dve.wait_ge(tg_ready, 1)
                        dve.wait_ge(bias_loaded, 16)
                        v.tensor_scalar(bo_sb[:], bo_sb[:], tg[:, 0:1], None, ALU.mult).then_inc(bo_ready, 1)
                    for kind, u in events:
                        if kind == "S1":
                            if u == 0 and isinstance(e, int) and e < 2:
                                dve.wait_ge(x_loaded, 16)
                            elif u == 0:
                                dve.wait_ge(x_rest_loaded, 16 * (B - 1))
                            last = v.bn_stats(stats[:, u, :], row(e, u))
                            if u == CHUNK_TILES - 1:
                                last.then_inc(ln_step, 1)
                        if kind == "A1":
                            moments(e, stats, mv, ve, ln_step, rstd_ready)
                        if kind == "L1":
                            if u == 0:
                                dve.wait_ge(rstd_ready, e + 1)
                                after(dve, xn_transposed, 2 * e)
                            last = v.tensor_scalar(xn[:, u, :], row(e, u), mv[:, u, 0:1], rstd[:, u:u + 1],
                                                   ALU.subtract, ALU.mult)
                            if u == CHUNK_TILES - 1:
                                last.then_inc(xn_ready, 1)
                                if isinstance(q, int) and q == -2:
                                    split_keys()
                        if kind in ("W0", "W1"):
                            c = int(kind[1])
                            if c == 0:
                                dve.wait_ge(x_biased, q)
                                dve.sem_inc(dve_holds, 1)
                            dve.wait_ge(wo_done, 2 * r + c + 1)
                            two = x_sb[:, bass.ds(r * CHUNK_TILES + 2 * c, 2), :]
                            v.scalar_tensor_tensor(two, (M, PV)[c][:].rearrange("p (t d) -> p t d", t=2), tg[:, 0:1],
                                                   two, ALU.mult, ALU.add).then_inc(att_ready, 1)
                        if kind == "S2":
                            if u == 0:
                                dve.wait_ge(att_ready, 2 * q)
                                dve.sem_inc(dve_holds, 1)
                            last = v.bn_stats(stats2[:, u, :], row(r, u))
                            if u == CHUNK_TILES - 1:
                                last.then_inc(ln2_step, 1)
                        if kind == "A2":
                            moments(r, stats2, mv2, ve2, ln2_step, rstd2_ready)
                        if kind == "L2":
                            if u == 0:
                                dve.wait_ge(rstd2_ready, q)
                                after(dve, xn2_transposed, 2 * r)
                                after(dve, xn2_stored, 16 * r)
                            last = v.tensor_scalar(xn2c[:, u, :], row(r, u), mv2[:, u, 0:1], rstd2[:, u:u + 1],
                                                   ALU.subtract, ALU.mult)
                            if u == CHUNK_TILES - 1:
                                last.then_inc(xn2_ready, 1)
                                if isinstance(q, int) and q == NCH:
                                    for m in range(0, HT, 2):
                                        low_weights(m)
                        if kind in ("Q0", "Q1"):
                            c = int(kind[1])
                            dve.wait_ge(qh_ready, 2 * e + c + 1)
                            v.scalar_tensor_tensor(ql[:, c, :], M[:], bq_sb[:, c:c + 1], qh[:, c, :].bitcast(F32),
                                                   ALU.add, ALU.subtract).then_inc(ql_ready, 1)
                        if kind == "SA":
                            t, p = max_unit(u)
                            dve.wait_ge(sa_done, 32 * n + u + 1)
                            if u == 0:
                                after(dve, mT_done, n)
                            v.reduce_max(mx[:, t, :, p], S[banks[kind, u]][:, 0:2 * KP].rearrange(
                                "p (k i) -> p i k", i=2), AX).then_inc(sa_read, 1)
                        if kind == "RD":
                            route_step(r, u)
                        if kind == "OT":
                            turned = T1[:].rearrange("p (t j r) -> p t j r", t=4, j=4)
                            dve.wait_ge(o_done, 4 * q + u + 1)
                            v.reciprocal(rden[:], turned[:, :, :, HD]).then_inc(rden_ready, 1)
                            dve.wait_ge(rden_ready, 4 * q + u + 1)
                            if u == 0:
                                after(dve, ctxn_transposed, 2 * q)
                            v.tensor_tensor(
                                ctxn[:, :, 4 * HD * u:4 * HD * (u + 1)].rearrange("p t (j d) -> p t j d", j=4),
                                turned[:, :, :, 0:HD],
                                rden[:].rearrange("p t (j o) -> p t j o", o=1).to_broadcast([P, 4, 4, HD]),
                                ALU.mult).then_inc(ctxn_ready, 1)

                run_steps(dve, step)

            @block.tensor
            def _(pe):
                mm, turn = nc.tensor.matmul, nc.tensor.transpose
                pe.wait_ge(consts_done, IDENT)
                pe.wait_ge(ctx_loaded, 32)
                for b in range(B):
                    after(pe, ctxT_ready, b - 1)
                    bank = (T0, T1)[b % 2]
                    for c in range(KC):
                        turn(bank[:, c * SK:c * SK + P], ctx_sb[:, 0, b, c * P:(c + 1) * P], ident[:])
                        last = turn(bank[:, c * SK + P:(c + 1) * SK], ctx_sb[0:REM, 1, b, c * P:(c + 1) * P],
                                    ident[0:REM, 0:REM])
                    last.then_inc(ctxT_done, 1)
                pe.wait_ge(wk_loaded, 16 * (KC + 1))
                for b in range(B):
                    pe.wait_ge(ctxT_ready, b + 1)
                    for c in range(2):
                        after(pe, kf_ready, 2 * b + c - 1)
                        for kc in range(KC):
                            last = mm(S[c][:, 0:SK], wk_sb[:, kc, 8 * c:8 * c + 8, :].rearrange("p h d -> p (h d)"),
                                      ctxT[:, kc, b, :], start=kc == 0, stop=kc == KC - 1)
                        last.then_inc(kT_done, 1)

                pe.wait_ge(weights_loaded, N_WEIGHTS)

                def project_values():
                    for b in range(B):
                        for r, keys in ((0, slice(0, P)), (1, slice(P, SK))):
                            after(pe, v_kept, 2 * b + r - 1)
                            for kc in range(KC):
                                last = mm(S[2 + r][0:keys.stop - keys.start, 0:D], ctxT[:, kc, b, keys],
                                          wv_sb[:, kc].rearrange("p h d -> p (h d)"), start=kc == 0, stop=kc == KC - 1)
                            last.then_inc(v_done, 1)

                def step(pe, q, b, k, early, front, back, prev):
                    n, e, r = q + 1, q + 2, q - 1
                    events, banks = step_events(early, front, back, prev)
                    held = bank_holders(q, early, front, back, prev) if front or back else {}

                    def turn_chunk(bank, src, c, done):
                        for t in range(CHUNK_TILES):
                            last = turn(bank[:, t * P:(t + 1) * P], src[:, t, c * P:(c + 1) * P], ident[:])
                        last.then_inc(done, 1)

                    if isinstance(q, int) and q == -1:
                        project_values()
                    for kind, u in events:
                        if kind == "C0":
                            pe.wait_ge(ctxn_ready, 4 * r + 4)
                            if back:
                                pe.wait_ge(mT_ready, q + 1)
                            else:
                                pe.wait_ge(xn2T_ready, 2 * r)
                            turn_chunk(T0, ctxn, 0, ctxn_transposed)
                        if kind == "C1":
                            turn_chunk(T1, ctxn, 1, ctxn_transposed)
                        if kind in ("W0", "W1"):
                            c = int(kind[1])
                            bank = (M, PV)[c]
                            pe.wait_ge(ctxnT_ready, 2 * r + 2)
                            if c == 1:
                                pe.wait_ge(oT_ready, 4 * r + 4)
                            elif isinstance(r, int) and r == 0:
                                pe.wait_ge(ql_ready, 2 * n + 2)
                            else:
                                pe.wait_ge(logits_read, r)
                            for t in (2 * c, 2 * c + 1):
                                for kc in range(KC):
                                    last = mm(bank[:, (t % 2) * D:(t % 2 + 1) * D], ctxnT[:, kc, t * P:(t + 1) * P],
                                              wo_sb[:, kc, :], start=kc == 0, stop=kc == KC - 1)
                            last.then_inc(wo_done, 1)
                        if kind == "X0":
                            pe.wait_ge(xn2_ready, q)
                            if early:
                                pe.wait_ge(xnT_ready, 2 * e + 2)
                            else:
                                pe.wait_ge(ctxnT_ready, 2 * r + 1)
                            turn_chunk(T0, xn2c, 0, xn2_transposed)
                        if kind == "XX":
                            pe.wait_ge(xn2T_ready, 2 * r + 1)
                            turn_chunk(T0, xn2c, 1, xn2_transposed)
                        if kind == "RT":
                            pe.wait_ge(xn2T_ready, 2 * r + 2)
                            if early:
                                pe.wait_ge(ql_ready, 2 * e + 2)
                            else:
                                pe.wait_ge(att_ready, 2 * r + 1)
                            for t in range(CHUNK_TILES):
                                for kc in range(KC):
                                    last = mm(M[:, t * E:(t + 1) * E], xn2T[:, kc, t * P:(t + 1) * P], rw_sb[:, kc, :],
                                              start=kc == 0, stop=kc == KC - 1)
                            last.then_inc(lg_done, 1)
                        if kind == "N0":
                            pe.wait_ge(xn_ready, e + 1)
                            if prev:
                                pe.wait_ge(ctxnT_ready, 2 * r + 1)
                            elif back:
                                pe.wait_ge(mT_ready, 1)
                            elif front:
                                pe.wait_ge(xnT_ready, 2)
                            else:
                                pe.wait_ge(ctxT_ready, B)
                            turn_chunk(T0, xn, 0, xn_transposed)
                        if kind == "N1":
                            pe.wait_ge(xnT_ready, 2 * e + 1)
                            turn_chunk(T0, xn, 1, xn_transposed)
                        if kind in ("Q0", "Q1"):
                            c = int(kind[1])
                            pe.wait_ge(xnT_ready, 2 * e + 2)
                            if c == 0 and prev:
                                pe.wait_ge(att_ready, 2 * r + 1)
                            else:
                                after(pe, ql_ready, 2 * e + c)
                            for kc in range(KC):
                                last = mm(M[:], wq_sb[:, kc, 8 * c:8 * c + 8, :].rearrange("p h d -> p (h d)"),
                                          xnT[:, kc, :], start=kc == 0, stop=kc == KC - 1)
                            last.then_inc(q_done, 1)
                        if kind == "MT":
                            pe.wait_ge(sa_read, 32 * (n + 1))
                            if prev:
                                pe.wait_ge(xn2T_ready, 2 * r + 2)
                            else:
                                pe.wait_ge(xnT_ready, 2 * e + 2)
                            for t in range(CHUNK_TILES):
                                last = turn(T0[0:H, t * P:(t + 1) * P], mx[:, t].rearrange("p i c -> p (i c)"), ident[:])
                            last.then_inc(mT_done, 1)
                        if kind in ("ST", "SA"):
                            was, value = held[kind, u]
                            pe.wait_ge({"ST": probs_ready, "SA": sa_read, "K": kf_ready, "V": v_kept}[was], value)
                            bank = S[banks[kind, u]]
                        if kind == "SA":
                            t, p = max_unit(u)
                            if u == 0:
                                pe.wait_ge(kmax_loaded, 16 * (b + k + 1))
                            if u % 16 == 0:
                                pe.wait_ge(q_loaded[1 - k][u // 16], N_QDMA * (b + k + 1))
                            mm(bank[:, 0:2 * KP], q_st[1 - k][0:ROWS, p, t * P:(t + 1) * P],
                               k_max[:, p, :], start=True, stop=True
                               ).then_inc(sa_done, 1)
                        if kind == "ST":
                            g, i = u // 5, u % 5
                            if u == 0:
                                pe.wait_ge(m_loaded[k], 32 * (b + 1))
                                pe.wait_ge(kst_loaded, 32 * (b + 1))
                                pe.wait_ge(ones_loaded, 16)
                            if i < 4:
                                p = 2 * g + i // 2
                                last = mm(bank[:], k_st[:, p, 3 * HALF + i % 2:3 * HALF + i % 2 + 2 * P - 1:2], q_st[k][:, p, :],
                                          start=True, stop=True)
                            else:
                                for p in (2 * g, 2 * g + 1):
                                    at = HALF * (1 - p % 2)
                                    last = mm(bank[:], k_st[:, p, at:at + P], q_st[k][:, p, :],
                                              start=p == 2 * g, stop=p == 2 * g + 1)
                            last.then_inc(st_done, 1)
                        if kind == "PV":
                            pe.wait_ge(probs_ready, 20 * q + 5 * u + 5)
                            if u == 0:
                                pe.wait_ge(v_loaded, N_VDMA * (b + 1))
                                after(pe, att_ready, 2 * q)
                            else:
                                pe.wait_ge(oT_ready, 4 * q + u)
                            for j in range(4):
                                mm(PV[QUAD * j:QUAD * (j + 1), :], v_main[:, 4 * u + j, :], probs[:, u % 2, j, :],
                                   start=True, stop=False)
                            mm(PV[:], v_rem[:, u, :], probs[:, u % 2, 4, :], start=False, stop=True
                               ).then_inc(pv_done, 1)
                        if kind == "OT":
                            pe.wait_ge(oT_ready, 4 * q + u + 1)
                            if u > 0:
                                pe.wait_ge(ctxn_ready, 4 * q + u)
                            else:
                                after(pe, ctxnT_ready, 2 * q)
                            for t in range(CHUNK_TILES):
                                last = turn(T1[:, t * P:(t + 1) * P], oT[:, t * P:(t + 1) * P], ident[:])
                            last.then_inc(o_done, 1)

                run_steps(pe, step)

    with ExitStack() as st:
        def sb(name, shape, dt=F32):
            return sbuf(name, shape, dt, st)

        def ps(name):
            return st.enter_context(nc.psum_tensor(name, [P, CH], F32))

        AHEAD = 4
        TILE_TURNS = 6
        MAX_TILES = T // P
        NR = RH // P

        x_rows = slots_x
        y_rows = nc.dram_tensor("y_rows", [TOPK * T + TILES * P, D], F32, kind="Internal").ap()

        shared_hi = sb("shared_hi", [P, KC * 2 * SH + HT * D])
        assert place["shared_hi"] == place["q_st0"]
        act_all = sb("act_all", [P, 8, CH])
        w12 = sb("w12", [P, E, KC, 2 * RH])
        w3 = sb("w3", [P, E, NR, D])
        w12_lo = over("w12", 0, "w12_lo", [P, E, KC, 2 * RH], F32R)
        w12_hi = over("shared_w", 0, "w12_hi", [P, E, KC, 2 * RH], F32R)
        assert place["act_all"] + 4 * 8 * CH == place["shared_w"] + 4 * E * KC * 2 * RH
        expert_words = KC * 2 * RH
        up_only = [e for e in range(E) if e * expert_words < KC * 2 * SH
                   or 0 <= e * expert_words - (KC * 2 * SH + HT * D) < KC * 2 * SH]
        split_order = up_only + [e for e in range(E) if e not in up_only]
        POOL_SPLITS = (1, 4, 7, 10, 13)
        LATE = E - 4 * KC * CH // (NR * D)
        assert 2 * LATE >= E
        xT, xT_hi, xT_lo = ([over("w3", LATE * NR * D + (2 * part + i) * KC * CH, f"{name}{i}", [P, KC, CH], dt)
                             for i in range(2)] for name, part, dt in (("xT", 0, F32), ("xT_hi", 1, F32R), ("xT_lo", 0, F32R)))
        act_s, act_hi, act_lo = ([over("act_all", (4 * part + i) * CH, f"{name}{i}", [P, CH], dt) for i in range(4)]
                                 for name, part, dt in (("act_s", 0, F32), ("act_hi", 1, F32R), ("act_lo", 0, F32R)))

        iota_p = sb("iota_p", [P, MAX_TILES])
        iota_t = sb("iota_t", [1, TILES])
        before = sb("before", [P, P])
        ones = sb("ones", [P, P])
        warm = sb("warm", [P, 2])
        home = sb("home", [P, NT, TOPK], I32)
        N = NT * E
        scratch = w3[:, 0:LATE].rearrange("p e r d -> p (e r d)")
        assert TILES * E + 5 * N <= LATE * NR * D
        tile_cmp = scratch[0:1, 0:TILES * E].rearrange("p (t e) -> p t e", e=E)
        at = TILES * E
        total, upto = (scratch[:, at + i * N:at + (i + 1) * N].rearrange("p (e t) -> p e t", e=E) for i in range(2))
        zero_row = scratch[:, at + 2 * N:at + 3 * N]
        tmp, rank = (scratch[:, at + i * N:at + (i + 1) * N].rearrange("p (t e) -> p t e", e=E) for i in (3, 4))
        xs = [sb(f"xs{i}", [P, D]) for i in range(2)]
        hid = [sb(f"hid{i}", [P, D]) for i in range(2)]
        ys = [over("before", 0, "ys0", [P, D]), sb("ys1", [P, D])]
        xsT_hi, xsT_lo = ([over("hot", (2 * part + i) * D, f"{name}{i}", [P, KC, P], F32R) for i in range(2)]
                          for part, name in enumerate(("xsT_hi", "xsT_lo")))
        hidT = [over("hots", i * D, f"hidT{i}", [P, NR, P]) for i in range(2)]
        assert TOPK * NT * E >= 4 * D and NT * E >= 2 * D and place["ones"] == place["before"] + 4 * P and D == 2 * P
        count_e, pad_e, end_e = sb("count_e", [P, E]), sb("pad_e", [P, E]), sb("end_e", [P, E])
        shift_e = sb("shift_e", [P, E])
        slot_f = sb("slot_f", [P, NT, TOPK])
        slot = sb("slot", [P, NT, TOPK], I32)
        tile_f, tile_e = sb("tile_f", [1, TILES]), sb("tile_e", [1, TILES], I32)

        idx = [sb(f"idx{i}", [P, CHUNK_TILES, TOPK], I32) for i in range(2)]
        home_now = [sb(f"home_now{i}", [P, CHUNK_TILES, TOPK], I32) for i in range(2)]
        homes = sb("homes", [P, TILES], I32)
        tile_home = [sb(f"tile_home{i}", [P, 1], I32) for i in range(2)]
        EARLY = 2 * CHUNK_TILES * D // (KC * 2 * RH)
        rows = [w12[:, 0:EARLY].rearrange("p e c n -> p (e c n)").rearrange("p (i t d) -> p i t d", i=2, d=D)[:, i]
                for i in range(2)]

        bank = [ps(f"bank{i}") for i in range(8)]

        w12_loaded, w12_hi_ready = sem("w12_loaded"), sem("w12_hi_ready")
        w12_ready, w12_ready_pool = sem("w12_ready"), sem("w12_ready_pool")
        we_loaded = sem("we_loaded")
        iotas_done = sem("iotas_done")
        xT_loaded = [sem(f"xT_loaded{i}") for i in range(2)]
        steps = sem("steps")
        ranks_done, ranks_kept = sem("ranks_done"), sem("ranks_kept")
        slots_ready = sem("slots_ready")
        tiles_ready = sem("tiles_ready")
        xT_hi_ready, xT_ready = sem("xT_hi_ready"), sem("xT_ready")
        h_done, silu_ready, prod_ready = sem("h_done"), sem("silu_ready"), sem("prod_ready")
        act_hi_ready, act_ready = sem("act_hi_ready"), sem("act_ready")
        act_used, y_added = sem("act_used"), sem("y_added")
        rows_loaded = [sem(f"rows_loaded{i}") for i in range(2)]
        idx_ready = sem("idx_ready")
        homes_loaded, home_ready = sem("homes_loaded"), sem("home_ready")
        rows_placed = [sem(f"rows_placed{i}") for i in range(2)]
        xs_loaded = [sem(f"xs_loaded{i}") for i in range(2)]
        xsT_hi_ready = sem("xsT_hi_ready")
        xs_turned, xsT_ready = sem("xs_turned"), sem("xsT_ready")
        up_done, sil_ready, hid_ready = sem("up_done"), sem("sil_ready"), sem("hid_ready")
        hid_turned, hidT_ready = sem("hid_turned"), sem("hidT_ready")
        down_done, ys_ready = sem("down_done"), sem("ys_ready")
        ys_stored = [sem(f"ys_stored{i}") for i in range(2)]
        got = [sem(f"got{i}") for i in range(AHEAD)]
        got_used = sem("got_used")
        out_stored = sem("out_stored")

        IOTAS = 6
        N_SCATTER = 2 * 16 * CHUNK_TILES * TOPK
        assert TOPK * NT * D <= E * KC * 2 * RH
        outs_in = w12[:].rearrange("p e c n -> p (e c n)")[:, 0:TOPK * NT * D].rearrange(
            "p (t k d) -> p t k d", k=TOPK, d=D)

        def run_tiles(eng, first, last, step):
            turns = (last - first) // TILE_TURNS
            with eng.Fori(0, turns) as j:
                for i in range(TILE_TURNS):
                    step(j * TILE_TURNS + first + i, i % 2)
            for t in range(first + turns * TILE_TURNS, last):
                step(t, t % 2)

        def run_chunks(eng, step):
            step(0, 0)
            with eng.Fori(0, NCH // 2 - 1) as j:
                for i in range(2):
                    step(j * 2 + 1 + i, 1 - i)
            step(NCH - 1, 1)

        with nc.Block() as block:
            @block.sync
            def _(sp):
                for i in range(2):
                    sp.dma_start(xT[i][:], xn2T_cols[:, :, i * CH:(i + 1) * CH]).then_inc(xT_loaded[i], 16)
                for i in range(2):
                    sp.dma_start(rows[i], xn2_rows[:, i * CHUNK_TILES:(i + 1) * CHUNK_TILES, :]
                                 ).then_inc(rows_loaded[i], 16)

                def load_w12(experts):
                    for kc in range(KC):
                        for u, w in enumerate((rw1, rw2)):
                            sp.dma_start(w12[:, experts, kc, u * RH:(u + 1) * RH],
                                         w[experts, kc * P:(kc + 1) * P, :].rearrange("e p n -> p e n")
                                         ).then_inc(w12_loaded, 16)

                def load_w3(experts):
                    for r in range(NR):
                        sp.dma_start(w3[:, experts, r, :],
                                     rw3[experts, r * P:(r + 1) * P, :].rearrange("e p n -> p e n")
                                     ).then_inc(we_loaded, 16)

                load_w12(slice(EARLY, E))
                sp.wait_ge(slots_ready, 1)
                sp.wait_ge(tiles_ready, 1)
                load_w3(slice(0, LATE))
                with sp.Fori(1, NCH // 2) as j:
                    for i in range(2):
                        sp.wait_ge(h_done, HT * (j * 2 + i - 1))
                        sp.dma_start(xT[i][:], xn2T_cols[:, :, bass.ds((j * 2 + i) * CH, CH)]
                                     ).then_inc(xT_loaded[i], 16)
                    for i in range(2):
                        sp.wait_ge(rows_placed[i], j * N_SCATTER)
                        sp.dma_start(rows[i], xn2_rows[:, bass.ds((j * 2 + i) * CHUNK_TILES, CHUNK_TILES), :]
                                     ).then_inc(rows_loaded[i], 16)
                for i in range(2):
                    sp.wait_ge(rows_placed[i], NCH // 2 * N_SCATTER)
                load_w12(slice(0, EARLY))

                def load_tile(t, i):
                    after(sp, xs_turned, t - 1)
                    sp.dma_start(xs[i][:], x_rows[bass.ds(t * P, P), :]).then_inc(xs_loaded[i], 16)

                load_tile(0, 0)
                load_tile(1, 1)
                sp.wait_ge(h_done, NCH * HT)
                load_w3(slice(LATE, E))
                sp.dma_start(homes[:], slot_home.rearrange("(t p) o -> p (t o)", p=P), allow_slow_non_contiguous=True
                             ).then_inc(homes_loaded, 16)
                run_tiles(sp, 2, TILES, load_tile)

                for i in range(2):
                    sp.wait_ge(ys_stored[i], 16 * (TILES // 2))

                def load_outputs(c, i):
                    for k in range(TOPK):
                        sp.dma_start(outs_in[:, chunk_tiles(c), k, :], y_rows[bass.ds(c * CH + k * T, CH), :].rearrange(
                            "(t p) d -> p t d", p=P)).then_inc(got[i], 16)

                def store_out(c):
                    sp.wait_ge(got_used, c + 1)
                    sp.dma_start(out_t[:, chunk_tiles(c), :], x_sb[:, chunk_tiles(c), :]).then_inc(out_stored, 16)

                for i in range(AHEAD):
                    load_outputs(i, i)
                with sp.Fori(0, NCH // AHEAD - 1) as j:
                    for i in range(AHEAD):
                        store_out(j * AHEAD + i)
                        load_outputs(j * AHEAD + AHEAD + i, i)
                for c in range(NCH - AHEAD, NCH):
                    store_out(c)
                sp.wait_ge(out_stored, 16 * NCH)

            @block.gpsimd
            def _(pool):
                g = nc.gpsimd
                count = [0]

                def const(ins):
                    ins.then_inc(iotas_done, 1)
                    count[0] += 1
                    pool.wait_ge(iotas_done, count[0])

                fl = dict(allow_small_or_imprecise_dtypes=True)
                const(g.iota(home[:], pattern=[[P, NT], [T, TOPK]], base=0, channel_multiplier=1))
                const(g.iota(iota_p[:], pattern=[[P, MAX_TILES]], base=0, channel_multiplier=0, **fl))
                const(g.iota(iota_t[:], pattern=[[1, TILES]], base=0, channel_multiplier=0, **fl))
                const(g.memset(ones[:], 1.0))
                const(g.memset(zero_row[:], 0.0))
                const(g.affine_select(out=before[:], in_=ones[:], compare_op=ALU.is_gt, fill=0.0, base=0,
                                      pattern=[[1, P]], channel_multiplier=-1))
                assert count[0] == IOTAS
                pool.wait_ge(slots_ready, 1)

                def place(c, i, j):
                    after(pool, rows_placed[i], j * N_SCATTER)
                    pool.sem_inc(pool_holds, 1)
                    g.tensor_copy(idx[i][:], slot[:, chunk_tiles(c), :]).then_inc(idx_ready, 1)
                    g.tensor_copy(home_now[i][:], home[:, chunk_tiles(c), :]).then_inc(idx_ready, 1)
                    pool.wait_ge(idx_ready, 2 * c + 2)
                    pool.wait_ge(rows_loaded[i], j * 16 + 16)
                    pool.sem_inc(pool_holds, 1)
                    for t in range(CHUNK_TILES):
                        for k in range(TOPK):
                            at_slot = bass.IndirectOffsetOnAxis(ap=idx[i][:, t, k:k + 1], axis=0)
                            pool.indirect_dma_start(out=x_rows, out_offset=at_slot, in_=rows[i][:, t, :],
                                                    in_offset=None).then_inc(rows_placed[i], 16)
                            pool.indirect_dma_start(out=slot_home, out_offset=at_slot, in_=home_now[i][:, t, k:k + 1],
                                                    in_offset=None).then_inc(rows_placed[i], 16)

                place(0, 0, 0)
                place(1, 1, 0)
                with pool.Fori(1, NCH // 2) as j:
                    for i in range(2):
                        place(j * 2 + i, i, j)

                def store_tile(t, i):
                    if not isinstance(t, int) or t >= 2:
                        pool.wait_ge(ys_stored[i], (t - i) * 8)
                        pool.sem_inc(pool_holds, 1)
                    g.tensor_copy(tile_home[i][:], homes[:, bass.ds(t, 1)]).then_inc(home_ready, 1)
                    pool.wait_ge(home_ready, t + 1)
                    pool.wait_ge(ys_ready, t + 1)
                    pool.sem_inc(pool_holds, 1)
                    pool.indirect_dma_start(
                        out=y_rows, out_offset=bass.IndirectOffsetOnAxis(ap=tile_home[i][:], axis=0),
                        in_=ys[i][:], in_offset=None).then_inc(ys_stored[i], 16)

                for n in POOL_SPLITS:
                    e = split_order[n]
                    pool.wait_ge(w12_hi_ready, n + 1)
                    g.tensor_tensor(w12_lo[:, e], w12[:, e], w12_hi[:, e].bitcast(F32), ALU.subtract
                                    ).then_inc(w12_ready_pool, 1)
                pool.wait_ge(homes_loaded, 16)
                store_tile(0, 0)
                store_tile(1, 1)
                run_tiles(pool, 2, TILES, store_tile)

            @block.scalar
            def _(act):
                s = nc.scalar
                s.activation(warm[:], tg[:], ACT.Silu)

                def high_xT(c, i):
                    act.wait_ge(xT_loaded[i], (c - i) * 8 + 16)
                    s.copy(xT_hi[i][:], xT[i][:]).then_inc(xT_hi_ready, 1)

                def keep_ranks():
                    act.wait_ge(ranks_done, 1)
                    s.copy(rank[:], bank[4][:].rearrange("p (t e) -> p t e", e=E)).then_inc(ranks_kept, 1)
                    s.copy(total[:], bank[5][:].rearrange("p (t e) -> p e t", e=E)).then_inc(ranks_kept, 1)

                def shared(c, i):
                    for m in range(HT):
                        n = c * HT + m
                        if m == 0 and isinstance(c, int) and c == 0:
                            high_xT(0, 0)
                            keep_ranks()
                        act.wait_ge(h_done, n + 1)
                        after(act, act_used, n - 3)
                        s.activation(act_s[m % 4][:], bank[m % 2][:], ACT.Silu).then_inc(silu_ready, 1)
                        act.wait_ge(prod_ready, n + 1)
                        s.copy(act_hi[m % 4][:], act_s[m % 4][:]).then_inc(act_hi_ready, 1)
                        if m == 3 and not (isinstance(c, int) and c == NCH - 1):
                            high_xT(c + 1, 1 - i)

                run_chunks(act, shared)

                act.wait_ge(w12_loaded, 16 * 4 * KC)
                act.wait_ge(h_done, NCH * HT)
                for n, e in enumerate(split_order):
                    if n == len(up_only):
                        act.wait_ge(act_used, NCH * HT)
                    s.copy(w12_hi[:, e], w12[:, e]).then_inc(w12_hi_ready, 1)

                def turn_in(t, i):
                    act.wait_ge(xs_turned, t + 1)
                    after(act, up_done, t - 1)
                    s.copy(xsT_hi[i][:], bank[i][:, 0:D].rearrange("p (c k) -> p c k", c=KC)).then_inc(xsT_hi_ready, 1)

                def silu(t, i):
                    act.wait_ge(up_done, t + 1)
                    after(act, hid_turned, t - 1)
                    s.activation(hid[i][:], bank[2 + i][:, 0:RH], ACT.Silu).then_inc(sil_ready, 1)

                turn_in(0, 0)
                turn_in(1, 1)
                silu(0, 0)
                turn_in(2, 0)
                silu(1, 1)
                turn_in(3, 1)
                silu(2, 0)

                def tile_step(t, i):
                    turn_in(t, i)
                    silu(t - 1, 1 - i)

                run_tiles(act, 4, TILES, tile_step)
                silu(TILES - 1, 1)

            @block.vector
            def _(dve):
                v = nc.vector
                done = [0]

                def then(ins):
                    done[0] += 1
                    ins.then_inc(steps, 1)
                    dve.wait_ge(steps, done[0])

                def over_e(ap):
                    return ap.rearrange("p (o e) -> p o e", o=1).to_broadcast([P, NT, E])

                def count_tokens():
                    then(v.tensor_tensor_scan(upto[:].rearrange("p e t -> p (e t)"), total[:].rearrange("p e t -> p (e t)"),
                                              zero_row, 0.0, ALU.add, ALU.add))
                    then(v.tensor_copy(end_e[:], upto[:, :, NT - 1]))
                    then(v.tensor_copy(count_e[:, 0:1], end_e[:, 0:1]))
                    then(v.tensor_tensor(count_e[:, 1:E], end_e[:, 1:E], end_e[:, 0:E - 1], ALU.subtract))

                def count_tiles():
                    cmp = tmp[:].rearrange("p t e -> p (t e)").rearrange("p (e n) -> p e n", e=E)
                    then(v.tensor_tensor(cmp, count_e[:].rearrange("p (e o) -> p e o", o=1).to_broadcast([P, E, MAX_TILES]),
                                         iota_p[:].rearrange("p (o n) -> p o n", o=1).to_broadcast([P, E, MAX_TILES]),
                                         ALU.is_gt))
                    then(v.reduce_sum(pad_e[:], cmp, AX))
                    then(v.tensor_tensor(shift_e[:], count_e[:], end_e[:], ALU.subtract))
                    then(v.tensor_tensor_scan(end_e[:], pad_e[:], zero_row[:, 0:E], 0.0, ALU.add, ALU.add))
                    then(v.tensor_tensor(pad_e[:], end_e[:], pad_e[:], ALU.subtract))
                    then(v.scalar_tensor_tensor(shift_e[:], pad_e[:], float(P), shift_e[:], ALU.mult, ALU.add))

                def place_tokens():
                    then(v.tensor_tensor(upto[:], upto[:], total[:], ALU.subtract))
                    then(v.tensor_tensor(tmp[:], rank[:], upto[:].rearrange("p e t -> p t e"), ALU.add))
                    then(v.tensor_tensor(tmp[:], tmp[:], over_e(shift_e[:]), ALU.add))

                def pick_slots():
                    for k in range(TOPK):
                        then(v.tensor_tensor(total[:].rearrange("p e t -> p (e t)").rearrange("p (t e) -> p t e", e=E),
                                             hot[:, :, k, :], tmp[:], ALU.mult))
                        then(v.reduce_sum(slot_f[:, :, k], total[:].rearrange("p e t -> p (e t)").rearrange(
                            "p (t e) -> p t e", e=E), AX))
                    v.tensor_copy(slot[:], slot_f[:]).then_inc(slots_ready, 1)

                def tiles_experts():
                    then(v.tensor_tensor(tile_cmp[:], end_e[0:1, :].rearrange("p (o e) -> p o e", o=1).to_broadcast(
                        [1, TILES, E]), iota_t[:].rearrange("p (t o) -> p t o", o=1).to_broadcast([1, TILES, E]), ALU.is_le))
                    then(v.reduce_sum(tile_f[:], tile_cmp[:], AX))
                    v.tensor_scalar(tile_e[:], tile_f[:], float(E - 1), None, ALU.min).then_inc(tiles_ready, 1)

                dve.wait_ge(iotas_done, IOTAS)

                def low_xT(c, i):
                    dve.wait_ge(xT_hi_ready, c + 1)
                    v.tensor_tensor(xT_lo[i][:], xT[i][:], xT_hi[i][:].bitcast(F32), ALU.subtract).then_inc(xT_ready, 1)

                def shared(c, i):
                    first = isinstance(c, int) and c == 0
                    for m in range(HT):
                        n = c * HT + m
                        if first:
                            if m == 0:
                                low_xT(0, 0)
                        dve.wait_ge(silu_ready, n + 1)
                        v.tensor_tensor(act_s[m % 4][:], act_s[m % 4][:], bank[2 + m % 2][:], ALU.mult
                                        ).then_inc(prod_ready, 1)
                        dve.wait_ge(act_hi_ready, n + 1)
                        v.tensor_tensor(act_lo[m % 4][:], act_s[m % 4][:], act_hi[m % 4][:].bitcast(F32), ALU.subtract
                                        ).then_inc(act_ready, 1)
                        if m == 3 and not (isinstance(c, int) and c == NCH - 1):
                            low_xT(c + 1, 1 - i)
                        if m == 1 and not first:
                            add_outputs(c - 1)
                        if first:
                            if m == 0:
                                dve.wait_ge(ranks_kept, 2)
                                count_tokens()
                            elif m == 1:
                                count_tiles()
                            elif m == 2:
                                place_tokens()
                            elif m == 4:
                                pick_slots()
                            elif m == 5:
                                tiles_experts()

                def add_outputs(c):
                    dve.wait_ge(act_used, c * HT + HT)
                    for t in range(CHUNK_TILES):
                        row = x_sb[:, bass.ds(c * CHUNK_TILES + t, 1), :].rearrange("p o d -> p (o d)")
                        last = v.scalar_tensor_tensor(row, bank[4 + t][:, 0:D], tg[:, 1:2], row, ALU.mult, ALU.add)
                    last.then_inc(y_added, 1)

                run_chunks(dve, shared)

                for n, e in enumerate(split_order):
                    if n == 2:
                        add_outputs(NCH - 1)
                    if n not in POOL_SPLITS:
                        dve.wait_ge(w12_hi_ready, n + 1)
                        v.tensor_tensor(w12_lo[:, e], w12[:, e], w12_hi[:, e].bitcast(F32), ALU.subtract
                                        ).then_inc(w12_ready, 1)

                def low_xs(t, i):
                    dve.wait_ge(xsT_hi_ready, t + 1)
                    v.tensor_tensor(xsT_lo[i][:], bank[i][:, 0:D].rearrange("p (c k) -> p c k", c=KC),
                                    xsT_hi[i][:].bitcast(F32), ALU.subtract).then_inc(xsT_ready, 1)

                def hidden(t, i):
                    dve.wait_ge(sil_ready, t + 1)
                    v.tensor_tensor(hid[i][:], hid[i][:], bank[2 + i][:, RH:2 * RH], ALU.mult).then_inc(hid_ready, 1)

                def turn_hidden(t, i):
                    dve.wait_ge(hid_turned, t + 1)
                    after(dve, down_done, t - 1)
                    v.tensor_copy(hidT[i][:], bank[4 + i][:, 0:RH].rearrange("p (c k) -> p c k", c=NR)
                                  ).then_inc(hidT_ready, 1)

                def outputs(t, i):
                    dve.wait_ge(down_done, t + 1)
                    if isinstance(t, int) and t < 2:
                        pass
                    else:
                        dve.wait_ge(ys_stored[i], (t - i) * 8)
                    v.tensor_copy(ys[i][:], bank[6 + i][:, 0:D]).then_inc(ys_ready, 1)

                low_xs(0, 0)
                low_xs(1, 1)
                hidden(0, 0)
                low_xs(2, 0)
                hidden(1, 1)
                turn_hidden(0, 0)
                low_xs(3, 1)
                hidden(2, 0)
                turn_hidden(1, 1)
                outputs(0, 0)
                low_xs(4, 0)
                hidden(3, 1)
                turn_hidden(2, 0)
                outputs(1, 1)

                def tile_step(t, i):
                    if not isinstance(t, int) or t + 3 < TILES:
                        low_xs(t + 3, 1 - i)
                    hidden(t + 2, i)
                    turn_hidden(t + 1, 1 - i)
                    outputs(t, i)

                run_tiles(dve, 2, TILES - 2, tile_step)
                turn_hidden(TILES - 1, 1)
                outputs(TILES - 2, 0)
                outputs(TILES - 1, 1)

                with dve.Fori(0, NCH // AHEAD) as j:
                    for i in range(AHEAD):
                        c = j * AHEAD + i
                        dve.wait_ge(got[i], j * (16 * TOPK) + 16 * TOPK)
                        for k in range(TOPK):
                            for t in range(CHUNK_TILES):
                                tile = bass.ds(c * CHUNK_TILES + t, 1)
                                row = x_sb[:, tile, :].rearrange("p o d -> p (o d)")
                                last = v.scalar_tensor_tensor(row, outs_in[:, tile, k, :].rearrange("p o d -> p (o d)"),
                                                              gate[:, tile, k], row, ALU.mult, ALU.add)
                            if k == 0:
                                last.then_inc(y_added, 1)
                                dve.wait_ge(y_added, NCH + c + 1)
                        last.then_inc(got_used, 1)

            @block.tensor
            def _(pe):
                mm, turn = nc.tensor.matmul, nc.tensor.transpose
                pe.wait_ge(iotas_done, IOTAS)
                mm(bank[4][:], before[:], hots[:].rearrange("p t e -> p (t e)"), start=True, stop=True)
                mm(bank[5][:], ones[:], hots[:].rearrange("p t e -> p (t e)"), start=True, stop=True
                   ).then_inc(ranks_done, 1)

                def three_passes(out_, lhs_hi, lhs_lo, rhs_hi, rhs_lo, start, stop):
                    mm(out_, lhs_hi, rhs_hi, start=start, stop=False)
                    mm(out_, lhs_hi, rhs_lo, start=False, stop=False)
                    return mm(out_, lhs_lo, rhs_hi, start=False, stop=stop)

                def shared(c, i):
                    first = isinstance(c, int) and c == 0
                    pe.wait_ge(xT_ready, c + 1)
                    for m in range(HT):
                        n = c * HT + m
                        after(pe, prod_ready, n - 1)
                        cols = slice(m * P, (m + 1) * P)
                        for u in range(2):
                            for kc in range(KC):
                                last = three_passes(bank[2 * u + m % 2][:], s12_hi[:, kc, u, cols],
                                                    s12_lo[:, kc, u, cols], xT_hi[i][:, kc, :], xT_lo[i][:, kc, :],
                                                    kc == 0, kc == KC - 1)
                        last.then_inc(h_done, 1)
                        if m >= 2:
                            down_shared(c, m - 2)
                        elif not first:
                            down_shared(c - 1, HT - 2 + m)

                def down_shared(c, m):
                    pe.wait_ge(act_ready, c * HT + m + 1)
                    if isinstance(c, int) and c == 0:
                        if m == 0:
                            pe.wait_ge(ranks_kept, 2)
                    elif m == 0:
                        pe.wait_ge(y_added, c)
                    for t in range(CHUNK_TILES):
                        rows_ = slice(t * P, (t + 1) * P)
                        last = three_passes(bank[4 + t][:, 0:D], act_hi[m % 4][:, rows_], act_lo[m % 4][:, rows_],
                                            s3_hi[:, m, :], s3_lo[:, m, :], m == 0, m == HT - 1)
                    last.then_inc(act_used, 1)

                run_chunks(pe, shared)
                down_shared(NCH - 1, HT - 2)
                down_shared(NCH - 1, HT - 1)

                pe.wait_ge(tiles_ready, 1)

                def expert(t):
                    return pe.value_load(tile_e[0:1, bass.ds(t, 1)], min_val=0, max_val=E - 1)

                def turn_in(t, i):
                    pe.wait_ge(xs_loaded[i], (t - i) * 8 + 16)
                    after(pe, xsT_ready, t - 1)
                    for kc in range(KC):
                        last = turn(bank[i][:, kc * P:(kc + 1) * P], xs[i][:, kc * P:(kc + 1) * P], ident[:])
                    last.then_inc(xs_turned, 1)

                def up(t, i, e):
                    pe.wait_ge(xsT_ready, t + 1)
                    after(pe, hid_ready, t - 1)
                    for kc in range(KC):
                        hi, lo = (w[:, bass.ds(e, 1), kc, :].rearrange("p o n -> p (o n)") for w in (w12_hi, w12_lo))
                        last = three_passes(bank[2 + i][:], xsT_hi[i][:, kc, :], xsT_lo[i][:, kc, :], hi, lo,
                                            kc == 0, kc == KC - 1)
                    last.then_inc(up_done, 1)

                def turn_hidden(t, i):
                    pe.wait_ge(hid_ready, t + 1)
                    after(pe, hidT_ready, t - 1)
                    for r in range(NR):
                        last = turn(bank[4 + i][:, r * P:(r + 1) * P], hid[i][:, r * P:(r + 1) * P], ident[:])
                    last.then_inc(hid_turned, 1)

                def down(t, i, e):
                    pe.wait_ge(hidT_ready, t + 1)
                    after(pe, ys_ready, t - 1)
                    for r in range(NR):
                        last = mm(bank[6 + i][:, 0:D], hidT[i][:, r, :],
                                  w3[:, bass.ds(e, 1), r, :].rearrange("p o n -> p (o n)"),
                                  start=r == 0, stop=r == NR - 1)
                    last.then_inc(down_done, 1)

                pe.wait_ge(y_added, NCH)
                turn_in(0, 0)
                turn_in(1, 1)
                pe.wait_ge(w12_ready, E - len(POOL_SPLITS))
                pe.wait_ge(w12_ready_pool, len(POOL_SPLITS))
                up(0, 0, expert(0))
                turn_in(2, 0)
                up(1, 1, expert(1))
                turn_hidden(0, 0)

                def tile_step(t, i, u=0):
                    if u == 0:
                        kept.clear()
                    kept[u + 2] = expert(t + 2)
                    turn_in(t + 3, 1 - i)
                    up(t + 2, i, kept[u + 2])
                    turn_hidden(t + 1, 1 - i)
                    down(t, i, kept[u] if u in kept else expert(t))

                kept = {}
                pe.wait_ge(we_loaded, 16 * 2 * NR)
                tile_step(0, 0)
                tile_step(1, 1)
                turns = (TILES - 6) // TILE_TURNS
                with pe.Fori(0, turns) as j:
                    for u in range(TILE_TURNS):
                        tile_step(j * TILE_TURNS + 2 + u, u % 2, u)
                for t in range(2 + turns * TILE_TURNS, TILES - 4):
                    tile_step(t, t % 2)
                turn_in(TILES - 1, 1)
                up(TILES - 2, 0, expert(TILES - 2))
                turn_hidden(TILES - 3, 1)
                down(TILES - 4, 0, expert(TILES - 4))
                up(TILES - 1, 1, expert(TILES - 1))
                turn_hidden(TILES - 2, 0)
                down(TILES - 3, 1, expert(TILES - 3))
                turn_hidden(TILES - 1, 1)
                down(TILES - 2, 0, expert(TILES - 2))
                down(TILES - 1, 1, expert(TILES - 1))

    keep.close()


_INS = ["x", "ctx_1024", "g_xattn", "g_ffn", "L0_xattn_wq", "L0_xattn_bq", "L0_xattn_wk", "L0_xattn_bk",
        "L0_xattn_wv", "L0_xattn_bv", "L0_xattn_wo", "L0_xattn_bo", "L0_ffn_router_w", "L0_ffn_expert_bias",
        "L0_ffn_shared_w1", "L0_ffn_shared_w2", "L0_ffn_shared_w3", "L0_ffn_routed_w1", "L0_ffn_routed_w2",
        "L0_ffn_routed_w3"]


def kernel(**inputs):
    import numpy as _np
    import concourse.bacc as _bacc
    from concourse import mybir as _mybir
    from concourse.bass_utils import run_bass_kernel_spmd as _run

    nc = _bacc.Bacc("TRN2", target_bir_lowering=False, num_devices=1)
    arrays, args = {}, []
    for name in _INS:
        a = _np.ascontiguousarray(inputs[name])
        arrays[f"in_{name}_dram"] = a
        args.append(nc.dram_tensor(f"in_{name}_dram", a.shape, _mybir.dt.from_np(a.dtype), kind="ExternalInput").ap())
    shape = inputs["x"].shape
    args.append(nc.dram_tensor("out_dram", shape, _mybir.dt.float32, kind="ExternalOutput").ap())
    flamingo_block(nc, *args)
    return _run(nc, [arrays], core_ids=[0]).results[0]["out_dram"]
```
